# Optimizing a Trainium2 kernel written in Bass

```python
import numpy as np
import jax
import jax.numpy as jnp

def _softmax(x, axis=-1):
    return jax.nn.softmax(x, axis=axis)

def _gelu(x):
    return jax.nn.gelu(x, approximate=True)

def _silu(x):
    return jax.nn.silu(x)

def _sigmoid(x):
    return jax.nn.sigmoid(x)

def _layernorm(x, axis=-1, eps=1e-05):
    m = jnp.mean(x, axis=axis, keepdims=True)
    v = jnp.var(x, axis=axis, keepdims=True)
    return (x - m) / jnp.sqrt(v + eps)

def _scatter_add(tgt, idx, src, axis=0):
    return tgt.at[idx].add(src)

def _segment_sum(src, seg, n):
    return jax.ops.segment_sum(src, seg, n)
kernel_name = 'mk_xattn_seq_d2_seqx_r8_91249a'

def setup_inputs(seed: int=0):
    np.random.seed(seed)
    _w = jnp.asarray

    def _rec_inputs():
        import jax
        import jax.numpy as jnp
        _rk = jax.random.key(seed)
        x = -0.0005207 + 1.001 * jax.random.normal(jax.random.fold_in(_rk, 1), (8, 56, 128), jnp.float32)
        _lenS = 56 - jax.random.randint(jax.random.fold_in(_rk, 7), (8,), 0, max(1, 56 // 4) + 1, jnp.int32)
        _lenS2 = 1500 - jax.random.randint(jax.random.fold_in(_rk, 8), (8,), 0, max(1, 1500 // 4) + 1, jnp.int32)
        _ctx_1024P = jax.random.normal(jax.random.fold_in(_rk, 11), (8, 16, 128), jnp.float32)
        _ctx_1024c = jax.random.dirichlet(jax.random.fold_in(_rk, 511), 0.3 * jnp.ones((16,), jnp.float32), (8, 1500))
        _ctx_1024t = jnp.einsum('bsk,bkd->bsd', _ctx_1024c, _ctx_1024P)
        _ctx_1024t = _ctx_1024t * jax.lax.rsqrt(jnp.mean(jnp.square(_ctx_1024t)) + 1e-12) * 0.953939
        ctx_1024 = 4.13588e-05 + 0.999923 * (_ctx_1024t + 0.3 * jax.random.normal(jax.random.fold_in(_rk, 611), (8, 1500, 128), jnp.float32))
        return (x, ctx_1024)
    x, ctx_1024 = _rec_inputs()

    def _L0_xattn_setup():
        import jax, jax.numpy as jnp
        import numpy as np
        D, H, E, K, DFF = (128, 16, 8, 2, 512)
        B, L, T = (4, 64, 256)
        EPS = 1e-05

        def _xavier(key, shape):
            fan_in, fan_out = (shape[-1], shape[-2])
            a = jnp.sqrt(6.0 / (fan_in + fan_out))
            return jax.random.uniform(key, shape, jnp.float32, -a, a)

        def _ln(x, g, b):
            m = x.mean(-1, keepdims=True)
            v = ((x - m) ** 2).mean(-1, keepdims=True)
            return (x - m) / jnp.sqrt(v + EPS) * g + b

        def _mha(q_in, kv_in, in_w, in_b, out_w, out_b):
            wq, wk, wv = jnp.split(in_w, 3, axis=0)
            bq, bk, bv = jnp.split(in_b, 3, axis=0)
            dh = D // H

            def heads(x, w, b):
                y = x @ w.T + b
                return y.reshape(x.shape[0], x.shape[1], H, dh).transpose(0, 2, 1, 3)
            q = heads(q_in, wq, bq)
            k = heads(kv_in, wk, bk)
            v = heads(kv_in, wv, bv)
            scores = jnp.einsum('bhqd,bhkd->bhqk', q, k) / jnp.sqrt(jnp.float32(dh))
            attn = jax.nn.softmax(scores, axis=-1)
            out = jnp.einsum('bhqk,bhkd->bhqd', attn, v)
            out = out.transpose(0, 2, 1, 3).reshape(q_in.shape[0], q_in.shape[1], D)
            return out @ out_w.T + out_b

        def _fuse_moe(x, ln_g, ln_b, rw, rb, fc1_w, fc1_b, fc2_w, fc2_b):
            h = _ln(x, ln_g, ln_b)
            logits = h @ rw.T + rb
            vals, idx = jax.lax.top_k(logits, K)
            gates = jax.nn.softmax(vals, axis=-1)
            N = x.shape[0] * x.shape[1]
            hf = h.reshape(N, D)
            h1 = jax.nn.gelu(jnp.einsum('nd,efd->enf', hf, fc1_w) + fc1_b[:, None, :], approximate=False)
            eo = jnp.einsum('enf,edf->end', h1, fc2_w) + fc2_b[:, None, :]
            idx_f = idx.reshape(N, K)
            gates_f = gates.reshape(N, K)
            gathered = eo[idx_f, jnp.arange(N)[:, None], :]
            mixed = (gathered * gates_f[..., None]).sum(axis=1).reshape(x.shape)
            return x + mixed
        key = jax.random.key(seed)
        ks = jax.random.split(key, 16)
        inp = {'latents': jax.random.normal(ks[0], (B, L, D), jnp.float32), 'tokens': jax.random.normal(ks[1], (B, T, D), jnp.float32), 'sa_ln_g': jnp.ones((D,)), 'sa_ln_b': jnp.zeros((D,)), 'sa_in_w': _xavier(ks[2], (3 * D, D)), 'sa_in_b': jnp.zeros((3 * D,)), 'sa_out_w': _xavier(ks[3], (D, D)), 'sa_out_b': jnp.zeros((D,)), 'ca_q_ln_g': jnp.ones((D,)), 'ca_q_ln_b': jnp.zeros((D,)), 'ca_kv_ln_g': jnp.ones((D,)), 'ca_kv_ln_b': jnp.zeros((D,)), 'ca_in_w': _xavier(ks[4], (3 * D, D)), 'ca_in_b': jnp.zeros((3 * D,)), 'ca_out_w': _xavier(ks[5], (D, D)), 'ca_out_b': jnp.zeros((D,)), 'moe_ln_g': jnp.ones((D,)), 'moe_ln_b': jnp.zeros((D,)), 'router_w': _xavier(ks[6], (E, D)), 'router_b': jnp.zeros((E,)), 'e_fc1_w': jax.vmap(lambda k: _xavier(k, (DFF, D)))(jax.random.split(ks[7], E)), 'e_fc1_b': jnp.zeros((E, DFF)), 'e_fc2_w': jax.vmap(lambda k: _xavier(k, (D, DFF)))(jax.random.split(ks[8], E)), 'e_fc2_b': jnp.zeros((E, D))}
        return inp
    _L0_xattn_all = _L0_xattn_setup()
    _L0_xattn_in = {k: v for k, v in _L0_xattn_all.items() if k in ('sa_ln_g', 'sa_ln_b', 'sa_in_w', 'sa_in_b', 'sa_out_w', 'sa_out_b', 'ca_q_ln_g', 'ca_q_ln_b', 'ca_kv_ln_g', 'ca_kv_ln_b', 'ca_in_w', 'ca_in_b', 'ca_out_w', 'ca_out_b', 'moe_ln_g', 'moe_ln_b', 'router_w', 'router_b', 'e_fc1_w', 'e_fc1_b', 'e_fc2_w', 'e_fc2_b')}
    del _L0_xattn_all

    def _L1_xattn_setup():
        import jax, jax.numpy as jnp
        import numpy as np
        D_MODEL = 128
        NUM_HEADS = 16
        HEAD_DIM = D_MODEL // NUM_HEADS
        SCALE = HEAD_DIM ** (-0.5)
        LN_EPS = 1e-05
        Q_EPS = 1e-05

        def bit_quant(W):
            gamma = jnp.mean(jnp.abs(W))
            Wq = jnp.clip(jnp.round(W / (gamma + Q_EPS)), -1.0, 1.0) * gamma
            return W + jax.lax.stop_gradient(Wq - W)

        def layer_norm(x, gamma, beta):
            mu = jnp.mean(x, axis=-1, keepdims=True)
            var = jnp.mean(jnp.square(x - mu), axis=-1, keepdims=True)
            return (x - mu) * jax.lax.rsqrt(var + LN_EPS) * gamma + beta
        key = jax.random.key(seed)
        ks = jax.random.split(key, 8)
        B, T, T_ctx, C = (4, 128, 256, D_MODEL)
        w_std = C ** (-0.5)
        return {'x': jax.random.normal(ks[0], (B, T, C), jnp.float32), 'context': jax.random.normal(ks[1], (B, T_ctx, C), jnp.float32), 'Wq': jax.random.normal(ks[2], (C, C), jnp.float32) * w_std, 'bq': jnp.zeros((C,), jnp.float32), 'Wk': jax.random.normal(ks[3], (C, C), jnp.float32) * w_std, 'bk': jnp.zeros((C,), jnp.float32), 'Wv': jax.random.normal(ks[4], (C, C), jnp.float32) * w_std, 'bv': jnp.zeros((C,), jnp.float32), 'Wo': jax.random.normal(ks[5], (C, C), jnp.float32) * w_std, 'bo': jnp.zeros((C,), jnp.float32), 'ln_gamma': jnp.ones((C,), jnp.float32), 'ln_beta': jnp.zeros((C,), jnp.float32)}
    _L1_xattn_all = _L1_xattn_setup()
    _L1_xattn_in = {k: v for k, v in _L1_xattn_all.items() if k in ('Wq', 'bq', 'Wk', 'bk', 'Wv', 'bv', 'Wo', 'bo', 'ln_gamma', 'ln_beta')}
    del _L1_xattn_all
    return {'x': x, 'ctx_1024': ctx_1024, 'L0_xattn_sa_ln_g': _L0_xattn_in['sa_ln_g'], 'L0_xattn_sa_ln_b': _L0_xattn_in['sa_ln_b'], 'L0_xattn_sa_in_w': _L0_xattn_in['sa_in_w'], 'L0_xattn_sa_in_b': _L0_xattn_in['sa_in_b'], 'L0_xattn_sa_out_w': _L0_xattn_in['sa_out_w'], 'L0_xattn_sa_out_b': _L0_xattn_in['sa_out_b'], 'L0_xattn_ca_q_ln_g': _L0_xattn_in['ca_q_ln_g'], 'L0_xattn_ca_q_ln_b': _L0_xattn_in['ca_q_ln_b'], 'L0_xattn_ca_kv_ln_g': _L0_xattn_in['ca_kv_ln_g'], 'L0_xattn_ca_kv_ln_b': _L0_xattn_in['ca_kv_ln_b'], 'L0_xattn_ca_in_w': _L0_xattn_in['ca_in_w'], 'L0_xattn_ca_in_b': _L0_xattn_in['ca_in_b'], 'L0_xattn_ca_out_w': _L0_xattn_in['ca_out_w'], 'L0_xattn_ca_out_b': _L0_xattn_in['ca_out_b'], 'L0_xattn_moe_ln_g': _L0_xattn_in['moe_ln_g'], 'L0_xattn_moe_ln_b': _L0_xattn_in['moe_ln_b'], 'L0_xattn_router_w': _L0_xattn_in['router_w'], 'L0_xattn_router_b': _L0_xattn_in['router_b'], 'L0_xattn_e_fc1_w': _L0_xattn_in['e_fc1_w'], 'L0_xattn_e_fc1_b': _L0_xattn_in['e_fc1_b'], 'L0_xattn_e_fc2_w': _L0_xattn_in['e_fc2_w'], 'L0_xattn_e_fc2_b': _L0_xattn_in['e_fc2_b'], 'L1_xattn_Wq': _L1_xattn_in['Wq'], 'L1_xattn_bq': _L1_xattn_in['bq'], 'L1_xattn_Wk': _L1_xattn_in['Wk'], 'L1_xattn_bk': _L1_xattn_in['bk'], 'L1_xattn_Wv': _L1_xattn_in['Wv'], 'L1_xattn_bv': _L1_xattn_in['bv'], 'L1_xattn_Wo': _L1_xattn_in['Wo'], 'L1_xattn_bo': _L1_xattn_in['bo'], 'L1_xattn_ln_gamma': _L1_xattn_in['ln_gamma'], 'L1_xattn_ln_beta': _L1_xattn_in['ln_beta']}

def reference(x, ctx_1024, L0_xattn_sa_ln_g, L0_xattn_sa_ln_b, L0_xattn_sa_in_w, L0_xattn_sa_in_b, L0_xattn_sa_out_w, L0_xattn_sa_out_b, L0_xattn_ca_q_ln_g, L0_xattn_ca_q_ln_b, L0_xattn_ca_kv_ln_g, L0_xattn_ca_kv_ln_b, L0_xattn_ca_in_w, L0_xattn_ca_in_b, L0_xattn_ca_out_w, L0_xattn_ca_out_b, L0_xattn_moe_ln_g, L0_xattn_moe_ln_b, L0_xattn_router_w, L0_xattn_router_b, L0_xattn_e_fc1_w, L0_xattn_e_fc1_b, L0_xattn_e_fc2_w, L0_xattn_e_fc2_b, L1_xattn_Wq, L1_xattn_bq, L1_xattn_Wk, L1_xattn_bk, L1_xattn_Wv, L1_xattn_bv, L1_xattn_Wo, L1_xattn_bo, L1_xattn_ln_gamma, L1_xattn_ln_beta):
    import jax
    import jax.numpy as jnp

    def _L0_xattn_ref(latents, tokens, sa_ln_g, sa_ln_b, sa_in_w, sa_in_b, sa_out_w, sa_out_b, ca_q_ln_g, ca_q_ln_b, ca_kv_ln_g, ca_kv_ln_b, ca_in_w, ca_in_b, ca_out_w, ca_out_b, moe_ln_g, moe_ln_b, router_w, router_b, e_fc1_w, e_fc1_b, e_fc2_w, e_fc2_b):
        import jax, jax.numpy as jnp
        import numpy as np
        D, H, E, K, DFF = (128, 16, 8, 2, 512)
        B, L, T = (4, 64, 256)
        EPS = 1e-05

        def _xavier(key, shape):
            fan_in, fan_out = (shape[-1], shape[-2])
            a = jnp.sqrt(6.0 / (fan_in + fan_out))
            return jax.random.uniform(key, shape, jnp.float32, -a, a)

        def _ln(x, g, b):
            m = x.mean(-1, keepdims=True)
            v = ((x - m) ** 2).mean(-1, keepdims=True)
            return (x - m) / jnp.sqrt(v + EPS) * g + b

        def _mha(q_in, kv_in, in_w, in_b, out_w, out_b):
            wq, wk, wv = jnp.split(in_w, 3, axis=0)
            bq, bk, bv = jnp.split(in_b, 3, axis=0)
            dh = D // H

            def heads(x, w, b):
                y = x @ w.T + b
                return y.reshape(x.shape[0], x.shape[1], H, dh).transpose(0, 2, 1, 3)
            q = heads(q_in, wq, bq)
            k = heads(kv_in, wk, bk)
            v = heads(kv_in, wv, bv)
            scores = jnp.einsum('bhqd,bhkd->bhqk', q, k) / jnp.sqrt(jnp.float32(dh))
            attn = jax.nn.softmax(scores, axis=-1)
            out = jnp.einsum('bhqk,bhkd->bhqd', attn, v)
            out = out.transpose(0, 2, 1, 3).reshape(q_in.shape[0], q_in.shape[1], D)
            return out @ out_w.T + out_b

        def _fuse_moe(x, ln_g, ln_b, rw, rb, fc1_w, fc1_b, fc2_w, fc2_b):
            h = _ln(x, ln_g, ln_b)
            logits = h @ rw.T + rb
            vals, idx = jax.lax.top_k(logits, K)
            gates = jax.nn.softmax(vals, axis=-1)
            N = x.shape[0] * x.shape[1]
            hf = h.reshape(N, D)
            h1 = jax.nn.gelu(jnp.einsum('nd,efd->enf', hf, fc1_w) + fc1_b[:, None, :], approximate=False)
            eo = jnp.einsum('enf,edf->end', h1, fc2_w) + fc2_b[:, None, :]
            idx_f = idx.reshape(N, K)
            gates_f = gates.reshape(N, K)
            gathered = eo[idx_f, jnp.arange(N)[:, None], :]
            mixed = (gathered * gates_f[..., None]).sum(axis=1).reshape(x.shape)
            return x + mixed
        q = _ln(latents, sa_ln_g, sa_ln_b)
        x = latents + _mha(q, q, sa_in_w, sa_in_b, sa_out_w, sa_out_b)
        qc = _ln(x, ca_q_ln_g, ca_q_ln_b)
        kv = _ln(tokens, ca_kv_ln_g, ca_kv_ln_b)
        x = x + _mha(qc, kv, ca_in_w, ca_in_b, ca_out_w, ca_out_b)
        return _fuse_moe(x, moe_ln_g, moe_ln_b, router_w, router_b, e_fc1_w, e_fc1_b, e_fc2_w, e_fc2_b)

    def _L1_xattn_ref(x, context, Wq, bq, Wk, bk, Wv, bv, Wo, bo, ln_gamma, ln_beta):
        import jax, jax.numpy as jnp
        import numpy as np
        D_MODEL = 128
        NUM_HEADS = 16
        HEAD_DIM = D_MODEL // NUM_HEADS
        SCALE = HEAD_DIM ** (-0.5)
        LN_EPS = 1e-05
        Q_EPS = 1e-05

        def bit_quant(W):
            gamma = jnp.mean(jnp.abs(W))
            Wq = jnp.clip(jnp.round(W / (gamma + Q_EPS)), -1.0, 1.0) * gamma
            return W + jax.lax.stop_gradient(Wq - W)

        def layer_norm(x, gamma, beta):
            mu = jnp.mean(x, axis=-1, keepdims=True)
            var = jnp.mean(jnp.square(x - mu), axis=-1, keepdims=True)
            return (x - mu) * jax.lax.rsqrt(var + LN_EPS) * gamma + beta
        B, T, C = x.shape
        T_ctx = context.shape[1]
        residual = x
        xn = layer_norm(x, ln_gamma, ln_beta)
        q = xn @ bit_quant(Wq).T + bq
        k = context @ bit_quant(Wk).T + bk
        v = context @ bit_quant(Wv).T + bv
        q = q.reshape(B, T, NUM_HEADS, HEAD_DIM)
        k = k.reshape(B, T_ctx, NUM_HEADS, HEAD_DIM)
        v = v.reshape(B, T_ctx, NUM_HEADS, HEAD_DIM)
        scores = jnp.einsum('bqhd,bkhd->bhqk', q, k) * SCALE
        probs = jax.nn.softmax(scores, axis=-1)
        out = jnp.einsum('bhqk,bkhd->bqhd', probs, v).reshape(B, T, C)
        return residual + (out @ bit_quant(Wo).T + bo)
    x = _L0_xattn_ref(x, ctx_1024, L0_xattn_sa_ln_g, L0_xattn_sa_ln_b, L0_xattn_sa_in_w, L0_xattn_sa_in_b, L0_xattn_sa_out_w, L0_xattn_sa_out_b, L0_xattn_ca_q_ln_g, L0_xattn_ca_q_ln_b, L0_xattn_ca_kv_ln_g, L0_xattn_ca_kv_ln_b, L0_xattn_ca_in_w, L0_xattn_ca_in_b, L0_xattn_ca_out_w, L0_xattn_ca_out_b, L0_xattn_moe_ln_g, L0_xattn_moe_ln_b, L0_xattn_router_w, L0_xattn_router_b, L0_xattn_e_fc1_w, L0_xattn_e_fc1_b, L0_xattn_e_fc2_w, L0_xattn_e_fc2_b)
    x = _L1_xattn_ref(x, ctx_1024, L1_xattn_Wq, L1_xattn_bq, L1_xattn_Wk, L1_xattn_bk, L1_xattn_Wv, L1_xattn_bv, L1_xattn_Wo, L1_xattn_bo, L1_xattn_ln_gamma, L1_xattn_ln_beta)
    return x

_drawn_inputs = setup_inputs


def setup_inputs(seed=0):
    import zlib

    import numpy as np

    out = dict(_drawn_inputs(seed))
    spreads = {'L0_xattn_sa_ln_g': (1.0, 0.2),
     'L0_xattn_sa_ln_b': (0.0, 0.1),
     'L0_xattn_sa_in_b': (0.0, 0.1),
     'L0_xattn_sa_out_b': (0.0, 0.1),
     'L0_xattn_ca_q_ln_g': (1.0, 0.2),
     'L0_xattn_ca_q_ln_b': (0.0, 0.381),
     'L0_xattn_ca_kv_ln_g': (1.0, 0.2),
     'L0_xattn_ca_kv_ln_b': (0.0, 0.1),
     'L0_xattn_ca_in_b': (0.0, 0.1),
     'L0_xattn_ca_out_b': (0.0, 0.1),
     'L0_xattn_moe_ln_g': (1.0, 0.2),
     'L0_xattn_moe_ln_b': (0.0, 0.1),
     'L0_xattn_router_b': (0.0, 0.1),
     'L0_xattn_e_fc1_b': (0.0, 0.1),
     'L0_xattn_e_fc2_b': (0.0, 0.1),
     'L1_xattn_bq': (0.0, 0.8),
     'L1_xattn_bk': (0.0, 0.8),
     'L1_xattn_bv': (0.0, 0.1),
     'L1_xattn_bo': (0.0, 0.1),
     'L1_xattn_ln_gamma': (1.0, 0.6),
     'L1_xattn_ln_beta': (0.0, 0.8)}
    factors = {}
    for name, (base, spread) in spreads.items():
        noise = np.random.default_rng([zlib.crc32(name.encode()), seed]).standard_normal(out[name].shape)
        drawn = base * np.exp(spread * noise) if base else spread * noise
        out[name] = jnp.asarray(drawn.astype(out[name].dtype))
    for name, factor in factors.items():
        out[name] = (out[name] * factor).astype(out[name].dtype)
    return out
```

```python
from contextlib import ExitStack

import numpy as np

import concourse.bass as bass
from concourse import mybir

ALU = mybir.AluOpType
ACT = mybir.ActivationFunctionType
AX = mybir.AxisListType
F32 = mybir.dt.float32
BF16 = mybir.dt.bfloat16

B, L, D, T = 8, 56, 128, 1500
H, DH = 16, 8
E, DFF = 8, 512
EPS = 1e-5
N = B * L
TT, TP = 4, 112
PAIRS = H // 2
PR = 2 * DH
K_PART = (0, 0, 0, 1, 1, 2)
Q_PART = (0, 1, 2, 0, 1, 0)
TERMS = len(K_PART)
SROWS = TERMS * PR
MROWS = 2
KROWS = SROWS + MROWS
PC = 2 * L
KC = 125
NCH = T // KC
STEPS = NCH
HSTEP = STEPS // 2
TPAD = KC * (NCH - 1) + 128
THIRD = T // 3
CPT = NCH // 3
VW = 9
VCOLS = 160
SCALE = float(DH) ** -0.5
TILES = PAIRS * 3
CPE = DFF // D
WB = 3
N_LN = 5
RB0, TRI0 = 3 * D, 3 * D + E


K_STEP, BACK_STEP, V_STEP, MX_STEP, FORTH_STEP, CTX_STEP = 0, 3, 4, 6, 7, STEPS - 3


def tiles_of_step():
    per = (2, 3, 3, 2, 2, 2, 2, 2, 1, 1, 2, 2)
    at = [sum(per[:k]) for k in range(STEPS + 1)]
    assert at[-1] == TILES and at[MX_STEP] >= TILES // 2
    return [range(at[k], at[k + 1]) for k in range(STEPS)]


STEP_TILES = tiles_of_step()


class Unit:

    def __init__(self, s, it, c):
        self.s, self.it, self.c = s, it, c
        self.par = c % 2
        self.u = c if it is None else it * 2 + c

    def __add__(self, d):
        return Unit(self.s, self.it, self.c + d)

    def exists(self):
        return self.it is not None or 0 <= self.c < B

    def count(self, per, off):
        base = (B * self.s + self.c) * per + off
        return base if self.it is None else self.it * (2 * per) + base

    def pass_par_count(self, per, off):
        base = self.c // 2 * per + off
        return base if self.it is None else self.it * per + base

    def par_count(self, per, off):
        base = (B // 2 * self.s + self.c // 2) * per + off
        return base if self.it is None else self.it * per + base


def wait(eng, sem, value):
    if not isinstance(value, int) or value > 0:
        eng.wait_ge(sem, value)


def run_windows(eng, s, window):
    window(Unit(s, None, 0))
    with eng.Fori(0, 2) as it:
        window(Unit(s, it, 1))
        window(Unit(s, it, 2))
    for u in range(5, B):
        window(Unit(s, None, u))


def build_kernel(nc, x_in, ctx_in, ctxT_in, watt_in, vec_in, rows_in, rwT_in, w1T_in, w2T_in, b2_in,
                 ident_in, out):
    with ExitStack() as ctx:
        def sb(name, shape, dt=F32):
            return ctx.enter_context(nc.sbuf_tensor(name, shape, dt))

        def sem(name):
            return ctx.enter_context(nc.semaphore(name))

        ST = ctx.enter_context(nc.psum_tensor("ST", [128, 2, 2, 512], F32))
        SM = ctx.enter_context(nc.psum_tensor("SM", [128, 2, 512], F32))
        PO = ctx.enter_context(nc.psum_tensor("PO", [128, 512], F32))
        MI = ctx.enter_context(nc.psum_tensor("MI", [128, 512], F32))
        MX = [ST[0:MROWS * 4, k % 2, 0, 4 * PC:4 * PC + L].bitcast(BF16) for k in (MX_STEP, 1)]
        OT = ST[:, FORTH_STEP % 2, 1, 4 * PC:4 * PC + L]

        ident = sb("ident", [128, 128])
        identb = sb("identb", [128, 128], BF16)
        vec = sb("vec", [128, 3 * WB + 2 * N_LN + E * CPE])
        rows = sb("rows", [TP, 3 * D + E + E * E])
        watt = sb("watt", [128, 3, 4, 128])
        rwT = sb("rwT", [128, E])
        b2 = sb("b2", [E, 128])
        xt = sb("xt", [TP, TT, D])
        xn = sb("xn", [TP, TT, D])
        hT = sb("hT", [128, N])
        xstat = sb("xstat", [TP, TT, 6])
        xmv = sb("xmv", [TP, TT, 2])
        xvar = sb("xvar", [TP, TT])
        xrstd = sb("xrstd", [TP, TT])
        half_neg = sb("half_neg", [128, 16])
        ones_rows = sb("ones_rows", [MROWS, TPAD], BF16)
        qf = sb("qf", [128, N])
        qr = sb("qr", [128, N])
        qsplit = sb("qsplit", [128, 3, N], BF16)
        qall = sb("qall", [SROWS, PAIRS, 2, N], BF16)
        qst = [sb(f"qst{i}", [KROWS, PAIRS, PC], BF16) for i in range(2)]
        kf = sb("kf", [128, T])
        kr = sb("kr", [128, T])
        ksplit = [sb(f"ksplit{i}", [128, 3, T], BF16) for i in range(2)]
        kst = [sb(f"kst{i}", [KROWS, PAIRS, TPAD], BF16) for i in range(2)]
        cx = [sb(f"cx{i}", [KC, NCH, D]) for i in range(2)]
        cstat = sb("cstat", [KC, NCH, 6])
        cmv = sb("cmv", [KC, NCH, 2])
        cvar = sb("cvar", [KC, NCH])
        crstd = sb("crstd", [KC, NCH])
        xT = [sb(f"xT{i}", [128, T]) for i in range(2)]
        vaug = [sb(f"vaug{i}", [KC, NCH, VCOLS]) for i in range(2)]
        PT = sb("PT", [128, 2, 2, 4 * PC])
        po = sb("po", [128, 2 * PC])
        on = sb("on", [L, 2, H, DH])
        rden = sb("rden", [L, H])
        attnT = sb("attnT", [128, N])
        mxp = sb("mxp", [PC, PAIRS, 3])
        nmx = sb("nmx", [PC, 4])
        mparts = sb("mparts", [PC, MROWS, 4], BF16)
        mrow = sb("mrow", [MROWS * 4, 2, PC], BF16)
        ks_sa = sb("ks_sa", [128, 3, N], BF16)
        kst_sa = sb("kst_sa", [SROWS, PAIRS, N], BF16)
        vaug_sa = sb("vaug_sa", [L, B, VCOLS])
        nmx_sa = sb("nmx_sa", [PC, PAIRS, B])
        mparts_sa = sb("mparts_sa", [PC, MROWS, B * PAIRS], BF16)
        mrow_sa = sb("mrow_sa", [128, PC], BF16)
        wabs = sb("wabs", [128, 4])
        mean_w = sb("mean_w", [128, 128])
        gam = sb("gam", [128, 4])
        wt = sb("wt", [128, 2, 4, 128])
        thr = sb("thr", [128, 2, 4])
        lg = sb("lg", [TP, TT, E])
        cmp = ks_sa[0:TP].rearrange("p s n -> p (s n)").bitcast(F32)[:, 0:2 * TT * E * E].rearrange(
            "p (s t e f) -> p s t e f", s=2, t=TT, e=E)
        rank = sb("rank", [TP, TT, E])
        top = sb("top", [TP, 3, TT])
        gates = sb("gates", [TP, TT, E])
        gT = sb("gT", [E, N])
        moe = sb("moe", [128, 4 * DFF + CPE * N])
        w1s = [moe[:, DFF * i:DFF * (i + 1)] for i in range(2)]
        w2s = [moe[:, DFF * (2 + i):DFF * (3 + i)].rearrange("f (c d) -> f c d", d=D) for i in range(2)]
        h1 = moe[:, 4 * DFF:].rearrange("f (c n) -> f c n", c=CPE)
        shift_sa = moe[0:MROWS].bitcast(BF16)[:, 0:PAIRS * B * PC].rearrange("m (j c) -> m j c", c=PC)

        def bias_q(layer):
            return vec[:, WB * layer:WB * layer + 1]

        def bias_k(layer):
            return vec[:, WB * layer + 1:WB * layer + 2]

        def bias_v(layer):
            return vec[:, WB * layer + 2:WB * layer + 3]

        def ln_vec(n, which):
            at = 3 * WB + 2 * n + which
            return vec[:, at:at + 1]
        LN_SA, LN_CAQ, LN_CAKV, LN_MOE, LN_L1 = range(N_LN)
        X_LN = (LN_SA, LN_CAQ, LN_MOE, LN_L1)
        B1_AT = 3 * WB + 2 * N_LN

        ld_x, ld_vec, ld_w, ld_ones = sem("ld_x"), sem("ld_vec"), sem("ld_w"), sem("ld_ones")
        ld_ctx = [sem(f"ld_ctx{i}") for i in range(2)]
        ld_xT = [sem(f"ld_xT{i}") for i in range(2)]
        ld_exp = [sem(f"ld_exp{i}") for i in range(2)]
        consts_ready = sem("consts_ready")
        pool_consts, identb_ready = sem("pool_consts"), sem("identb_ready")
        xstat_ready, xmv_ready, xvar_ready, xrstd_ready, xn_ready = (
            sem("xstat_ready"), sem("xmv_ready"), sem("xvar_ready"), sem("xrstd_ready"), sem("xn_ready"))
        lnt_full, hT_ready, qp_full, qf_ready, qp_read, qr_ready, q2_ready, qsplit_ready = (
            sem("lnt_full"), sem("hT_ready"), sem("qp_full"), sem("qf_ready"), sem("qp_read"),
            sem("qr_ready"), sem("q2_ready"), sem("qsplit_ready"))
        qall_loaded = sem("qall_loaded")
        op_full, x_proj, x_added = sem("op_full"), sem("x_proj"), sem("x_added")
        sa_kp_full, sa_kf, sa_kp_read, sa_kr, sa_k2, sa_ksplit = (
            sem("sa_kp_full"), sem("sa_kf"), sem("sa_kp_read"), sem("sa_kr"), sem("sa_k2"), sem("sa_ksplit"))
        sa_kst, sa_vp_full, sa_v_evac, sa_sm_full, sa_red, sa_m1, sa_mparts = (
            sem("sa_kst"), sem("sa_vp_full"), sem("sa_v_evac"), sem("sa_sm_full"), sem("sa_red"),
            sem("sa_m1"), sem("sa_mparts"))
        sa_qst = sem("sa_qst")
        sa_mx_full, sa_mx_evac, sa_shift, sa_st, sa_exp, sa_pv, sa_po, sa_pot, sa_rden, sa_norm, sa_ont, sa_att = (
            sem("sa_mx_full"), sem("sa_mx_evac"), sem("sa_shift"), sem("sa_st"), sem("sa_exp"), sem("sa_pv"),
            sem("sa_po"), sem("sa_pot"), sem("sa_rden"), sem("sa_norm"), sem("sa_ont"), sem("sa_att"))
        wabs_ready, gam_full, gam_ready, thr_ready, tern1, tern2, tern3, wq_ready = (
            sem("wabs_ready"), sem("gam_full"), sem("gam_ready"), sem("thr_ready"), sem("tern1"), sem("tern2"),
            sem("tern3"), sem("wq_ready"))
        cstat_ready, cmv_ready, cvar_ready, crstd_ready, cn_ready = (
            sem("cstat_ready"), sem("cmv_ready"), sem("cvar_ready"), sem("crstd_ready"), sem("cn_ready"))
        xt_full, xt_evac, kp_full, k_evac, kr_done, k2_done, k3_done, vp_full, v_evac = (
            sem("xt_full"), sem("xt_evac"), sem("kp_full"), sem("k_evac"), sem("kr_done"), sem("k2_done"),
            sem("k3_done"), sem("vp_full"), sem("v_evac"))
        kst_loaded = [[sem(f"kst_loaded{h}{p}") for p in range(2)] for h in range(2)]
        qst_ready, sm_full, sm_red, nmx_ready, m1_ready, mparts_ready, mx_full, mx_evac = (
            sem("qst_ready"), sem("sm_full"), sem("sm_red"), sem("nmx_ready"), sem("m1_ready"),
            sem("mparts_ready"), sem("mx_full"), sem("mx_evac"))
        shift_loaded = [[sem(f"shift_loaded{h}{p}") for p in range(2)] for h in range(2)]
        st_full, exp_done, pv_done, po_evac, pot_full, rden_ready, norm_done, ont_full, ont_evac = (
            sem("st_full"), sem("exp_done"), sem("pv_done"), sem("po_evac"), sem("pot_full"),
            sem("rden_ready"), sem("norm_done"), sem("ont_full"), sem("ont_evac"))
        rt_full, lg_ready, cmp_ready, rank_ready, top_ready, gexp_in, gexp_done, gate_step, gates_ready = (
            sem("rt_full"), sem("lg_ready"), sem("cmp_ready"), sem("rank_ready"), sem("top_ready"),
            sem("gexp_in"), sem("gexp_done"), sem("gate_step"), sem("gates_ready"))
        gt_full, gT_ready, b2_full, b2_added = sem("gt_full"), sem("gT_ready"), sem("b2_full"), sem("b2_added")
        fc1_full, gelu_done, fc2_step, expert_added = (
            sem("fc1_full"), sem("gelu_done"), sem("fc2_step"), sem("expert_added"))
        stored = sem("stored")

        block = ctx.enter_context(nc.Block())

        @block.sync
        def _(sp):
            sp.dma_start(xt[:], x_in.rearrange("(t p) d -> p t d", p=TP)).then_inc(ld_x, 16)
            sp.dma_start(ident[:], ident_in).then_inc(ld_x, 16)
            sp.dma_start(vec[:], vec_in).then_inc(ld_vec, 16)
            sp.dma_start(watt[:], watt_in.rearrange("l w i o -> i l w o")).then_inc(ld_w, 16)

            def load_ctx(n):
                if n.it is not None or n.c >= 2:
                    sp.wait_ge(xt_full, (n + -2).count(3, 3))
                src = ctx_in[bass.ds(n.u, 1)].rearrange("a (p c) d -> (a p) c d", c=NCH)
                sp.dma_start(cx[n.par][:], src).then_inc(ld_ctx[n.par], 16)

            def load_xT(n):
                sp.wait_ge(vp_full, (n + -2).count(3, 3))
                src = ctxT_in[bass.ds(n.u, 1)].rearrange("a d t -> (a d) t")
                sp.dma_start(xT[n.par][:], src).then_inc(ld_xT[n.par], 16)

            load_ctx(Unit(0, None, 0))
            load_ctx(Unit(0, None, 1))
            sp.dma_start(rows[:], rows_in.partition_broadcast(TP)).then_inc(ld_vec, 16)
            sp.dma_start(rwT[:], rwT_in).then_inc(ld_vec, 16)
            sp.dma_start(b2[:], b2_in).then_inc(ld_vec, 16)

            def load_expert(e, j):
                sp.dma_start(w1s[j], w1T_in[bass.ds(e, 1)].rearrange("a i f -> (a i) f")).then_inc(ld_exp[j], 16)
                sp.dma_start(w2s[j], w2T_in[bass.ds(e, 1)].rearrange("a f c d -> (a f) c d")).then_inc(ld_exp[j], 16)

            def load_qall(n):
                sp.wait_ge(qsplit_ready, n + 1)
                for t in range(TERMS):
                    for hh in range(2):
                        dst = qall[t * PR + hh * DH:t * PR + (hh + 1) * DH, :, hh, :]
                        src = qsplit[hh * 64:(hh + 1) * 64, Q_PART[t], :]
                        sp.dma_start(dst, src).then_inc(qall_loaded, 16)

            sp.wait_ge(consts_ready, 1)
            for stack in kst:
                width = stack.shape[2]
                sp.dma_start(stack[SROWS:KROWS], ones_rows[:, 0:width].unsqueeze(1).broadcast_to(
                    [MROWS, PAIRS, width])).then_inc(ld_ones, 16)

            load_qall(0)
            sp.wait_ge(sa_ksplit, 1)
            for t in range(TERMS):
                for half in range(2):
                    sp.dma_start(kst_sa[t * PR:(t + 1) * PR, 4 * half:4 * half + 4, :],
                                 ks_sa[64 * half:64 * half + 64, K_PART[t], :]).then_inc(sa_kst, 16)
            sp.wait_ge(sa_mx_evac, 1)
            for m in range(MROWS):
                sp.dma_start(shift_sa[m:m + 1], mrow_sa[PAIRS * B * m:PAIRS * B * (m + 1), :]).then_inc(sa_shift, 16)

            def restack(n, half):
                split = n.count(3, 3) if n.it is None else sp.to_reg(n.count(3, 3))
                if n.s or n.it is not None or n.c >= 2:
                    sp.wait_ge(st_full, (n + -2).count(STEPS, HSTEP * (half + 1)))
                sp.wait_ge(k3_done, split)
                for t in range(TERMS):
                    sp.dma_start(kst[n.par][t * PR:(t + 1) * PR, 4 * half:4 * half + 4, 0:T],
                                 ksplit[n.par][64 * half:64 * half + 64, K_PART[t], :]
                                 ).then_inc(kst_loaded[half][n.par], 16)

            def shift(n, half):
                sp.wait_ge(mx_evac, n.count(2, half + 1))
                sp.dma_start(qst[n.par][SROWS:KROWS, 4 * half:4 * half + 4, :], mrow[:, half, :]
                             ).then_inc(shift_loaded[half][n.par], 16)

            def window(n):
                if n.s == 0 and (n + 3).exists():
                    load_ctx(n + 3)
                if (n + 1).exists():
                    restack(n + 1, 1)
                shift(n, 1)
                if n.s == 1 and (n + 3).exists():
                    load_xT(n + 3)
                if (n + 1).exists():
                    shift(n + 1, 0)
                if (n + 2).exists():
                    restack(n + 2, 0)

            u0, u1 = Unit(0, None, 0), Unit(0, None, 1)
            restack(u0, 0)
            restack(u0, 1)
            load_ctx(Unit(0, None, 2))
            restack(u1, 0)
            load_qall(1)
            shift(u0, 0)
            sp.wait_ge(x_added, 1)
            load_expert(0, 0)
            load_expert(1, 1)
            run_windows(sp, 0, window)
            v0 = Unit(1, None, 0)
            load_xT(v0)
            load_xT(v0 + 1)
            restack(v0, 0)
            restack(v0, 1)
            load_xT(v0 + 2)
            restack(v0 + 1, 0)
            sp.wait_ge(fc2_step, CPE)
            load_expert(2, 0)
            sp.wait_ge(fc2_step, 2 * CPE)
            load_expert(3, 1)
            with sp.Fori(1, 3) as it:
                for j in range(2):
                    sp.wait_ge(fc2_step, it * (2 * CPE) + (j + 1) * CPE)
                    load_expert(it * 2 + (j + 2), j)
            load_qall(2)
            shift(v0, 0)
            run_windows(sp, 1, window)
            sp.wait_ge(x_added, 3)
            sp.dma_start(out.rearrange("(t p) d -> p t d", p=TP), xt[:]).then_inc(stored, 16)
            sp.wait_ge(stored, 16)

        @block.gpsimd
        def _(pool):
            nc.gpsimd.memset(half_neg[:], -0.5).then_inc(pool_consts, 1)
            nc.gpsimd.memset(mean_w[:], 1.0 / (D * D))
            nc.gpsimd.memset(ones_rows[:], 1.0)
            nc.gpsimd.memset(qall[:].bitcast(F32), 0.0).then_inc(consts_ready, 1)
            for s in range(2):
                nc.gpsimd.memset(kst[s][0:SROWS, :, T:TPAD], 0.0)
            nc.gpsimd.memset(vaug_sa[:], 1.0).then_inc(consts_ready, 1)

            def token_rstd(n):
                pool.wait_ge(xvar_ready, n + 1)
                nc.gpsimd.tensor_tensor(xrstd[:], xvar[:], half_neg[0:TP, 0:TT], ALU.pow).then_inc(xrstd_ready, 1)

            def ctx_rstd(n):
                pool.wait_ge(cvar_ready, n.count(1, 1))
                nc.gpsimd.tensor_tensor(crstd[:], cvar[:], half_neg[0:KC, 0:NCH], ALU.pow).then_inc(crstd_ready, 1)

            def k_rest(n, i):
                wait(pool, k3_done, n.count(3, i - 2))
                pool.wait_ge(k_evac, n.count(6, 2 * i + 2))
                c = slice(THIRD * i, THIRD * (i + 1))
                nc.gpsimd.tensor_tensor(kr[:, c], kf[:, c], ksplit[n.par][:, 0, c], ALU.subtract).then_inc(kr_done, 1)

            def k_third_part(n, i):
                pool.wait_ge(k2_done, n.count(3, i + 1))
                c = slice(THIRD * i, THIRD * (i + 1))
                nc.gpsimd.tensor_tensor(ksplit[n.par][:, 2, c], kr[:, c], ksplit[n.par][:, 1, c],
                                        ALU.subtract).then_inc(k3_done, 1)

            def k_parts(n, ln_unit):
                k_rest(n, 0)
                k_rest(n, 1)
                k_third_part(n, 0)
                k_rest(n, 2)
                k_third_part(n, 1)
                k_third_part(n, 2)
                if ln_unit is not None:
                    ctx_rstd(ln_unit)

            def window(n):
                ln_unit = n + 3 if n.s == 0 and (n + 3).exists() else None
                if (n + 2).exists():
                    k_parts(n + 2, ln_unit)

            pool.wait_ge(pool_consts, 1)
            token_rstd(0)
            u0, u1 = Unit(0, None, 0), Unit(0, None, 1)
            nc.gpsimd.memset(vaug[0][:], 1.0)
            nc.gpsimd.memset(vaug[1][:], 1.0).then_inc(consts_ready, 1)
            ctx_rstd(u0)
            for i in range(3):
                k_rest(u0, i)
            ctx_rstd(u1)
            for i in range(3):
                k_third_part(u0, i)
            for i in range(3):
                k_rest(u1, i)
            ctx_rstd(u0 + 2)
            for i in range(3):
                k_third_part(u1, i)
            token_rstd(1)
            run_windows(pool, 0, window)
            token_rstd(2)
            v0 = Unit(1, None, 0)
            k_parts(v0, None)
            k_parts(v0 + 1, None)
            token_rstd(3)
            run_windows(pool, 1, window)

        @block.scalar
        def _(act):
            def evac_sa_v():
                for i in range(2):
                    act.wait_ge(sa_vp_full, i + 1)
                    if i == 0:
                        act.wait_ge(consts_ready, 2)
                    dst = vaug_sa[:, 4 * i:4 * i + 4, 0:H * VW].rearrange("k b (h c) -> k b h c", c=VW)[:, :, :, 0:DH]
                    nc.scalar.activation(dst, MI[0:L, :].rearrange("k (b h c) -> k b h c", b=4, c=DH),
                                         ACT.Copy).then_inc(sa_v_evac, 1)

            def evac_xT(n, thirds=range(3)):
                for i in thirds:
                    act.wait_ge(xt_full, n.count(3, i + 1))
                    if i == 0 and (n.it is not None or n.c >= 2):
                        act.wait_ge(vp_full, (n + -2).count(3, 3))
                    nc.scalar.activation(xT[n.par][:, THIRD * i:THIRD * (i + 1)], MI[:, 0:THIRD], ACT.Identity,
                                         bias=ln_vec(LN_CAKV, 1), scale=ln_vec(LN_CAKV, 0)).then_inc(xt_evac, 1)

            def evac_k(n, i):
                act.wait_ge(kp_full, n.count(3, i + 1))
                if i == 0:
                    for half in range(2):
                        wait(act, kst_loaded[half][n.par], n.par_count(16 * TERMS, 0))
                wait(act, kr_done, n.count(3, i - 2))
                c = slice(THIRD * i, THIRD * (i + 1))
                nc.scalar.activation(kf[:, c], MI[:, 0:THIRD], ACT.Identity, bias=bias_k(n.s + 1)).then_inc(k_evac, 1)
                nc.scalar.activation(ksplit[n.par][:, 0, c], MI[:, 0:THIRD], ACT.Identity,
                                     bias=bias_k(n.s + 1)).then_inc(k_evac, 1)

            def evac_v(n, i):
                act.wait_ge(vp_full, n.count(3, i + 1))
                if i == 0:
                    if n.s == 0 and n.it is None and n.c < 2:
                        act.wait_ge(consts_ready, 3)
                    else:
                        act.wait_ge(pv_done, (n + -2).count(STEPS, STEPS))
                dst = vaug[n.par][:, CPT * i:CPT * (i + 1), 0:H * VW].rearrange(
                    "k b (h c) -> k b h c", c=VW)[:, :, :, 0:DH]
                nc.scalar.activation(dst, MI[0:KC, :].rearrange("k (b h c) -> k b h c", b=CPT, c=DH),
                                     ACT.Copy).then_inc(v_evac, 1)

            def evac_mx(n, half):
                act.wait_ge(mx_full, n.count(2, half + 1))
                prev = n + -1
                if n.s or n.it is not None or n.c >= 1:
                    act.wait_ge(shift_loaded[half][prev.par], prev.par_count(16, 16))
                nc.scalar.activation(mrow[:, half, :], MX[half], ACT.Copy
                                     ).then_inc(mx_evac, 1)

            def exp_step(n, k):
                act.wait_ge(st_full, n.count(STEPS, k + 1))
                wait(act, pv_done, n.count(STEPS, k - 1))
                nc.scalar.activation(PT[:, k % 2], ST[:, k % 2, :, 0:4 * PC], ACT.Exp, scale=SCALE
                                     ).then_inc(exp_done, 1)

            def evac_po(n):
                act.wait_ge(pv_done, n.count(STEPS, STEPS))
                nc.scalar.activation(po[:], PO[:, 0:2 * PC], ACT.Copy).then_inc(po_evac, 1)

            def evac_on(n):
                act.wait_ge(ld_vec, 64)
                act.wait_ge(ont_full, n.count(1, 1))
                nc.scalar.activation(attnT[:, bass.ds(n.u * L, L)], OT, ACT.Identity,
                                     bias=bias_v(n.s + 1)).then_inc(ont_evac, 1)

            def window(n):
                for k in range(STEPS):
                    if k == 1:
                        evac_mx(n, 1)
                    if k == MX_STEP and (n + 1).exists():
                        evac_mx(n + 1, 0)
                    if k == FORTH_STEP and (n + -1).exists():
                        evac_on(n + -1)
                    exp_step(n, k)
                    if k == 0 and (n + -1).exists():
                        evac_po(n + -1)
                    if 0 <= k - K_STEP < 3 and (n + 2).exists():
                        evac_k(n + 2, k - K_STEP)
                    if 0 <= k - V_STEP < 3 and (n + 1).exists():
                        evac_v(n + 1, k - V_STEP)
                    if 0 <= k - CTX_STEP < 3 and n.s == 0 and (n + 3).exists():
                        evac_xT(n + 3, (k - CTX_STEP,))

            def finish_pass(s):
                last = Unit(s, None, B - 1)
                evac_po(last)
                evac_on(last)

            act.wait_ge(ld_vec, 64)
            evac_sa_v()
            u0, u1 = Unit(0, None, 0), Unit(0, None, 1)
            evac_xT(u0)
            for i in range(3):
                evac_k(u0, i)
            act.wait_ge(sa_mx_full, 1)
            nc.scalar.activation(mrow_sa[:], MI[:].bitcast(BF16)[:, 0:PC], ACT.Copy).then_inc(sa_mx_evac, 1)
            for i in range(3):
                evac_v(u0, i)
            evac_xT(u1)
            for b in range(B + 3):
                if b < B:
                    act.wait_ge(sa_st, b + 1)
                    wait(act, sa_pv, b - 1)
                    nc.scalar.activation(PT[0:L, b % 2], ST[0:L, b % 2, :, 0:4 * PC], ACT.Exp, scale=SCALE
                                         ).then_inc(sa_exp, 1)
                if 0 <= b - 1 < B:
                    act.wait_ge(sa_pv, b)
                    wait(act, sa_pot, b - 1)
                    nc.scalar.activation(po[:], PO[:, 0:2 * PC], ACT.Copy).then_inc(sa_po, 1)
                if 0 <= b - 3 < B:
                    act.wait_ge(sa_ont, b - 2)
                    nc.scalar.activation(attnT[:, L * (b - 3):L * (b - 2)], MI[:, 0:L], ACT.Identity,
                                         bias=bias_v(0)).then_inc(sa_att, 1)
            for i in range(3):
                evac_k(u1, i)
            evac_xT(u0 + 2)
            evac_mx(u0, 0)
            run_windows(act, 0, window)
            finish_pass(0)

            v0 = Unit(1, None, 0)
            for i in range(3):
                evac_k(v0, i)
            for i in range(3):
                evac_v(v0, i)
            for i in range(3):
                evac_k(v0 + 1, i)
            act.wait_ge(gexp_in, 1)
            nc.scalar.activation(gates[:], lg[:], ACT.Exp).then_inc(gexp_done, 1)

            def gelus(it):
                for i in range(2 * CPE):
                    act.wait_ge(ld_vec, 64)
                    act.wait_ge(fc1_full, it * (2 * CPE) + (i + 1))
                    if not isinstance(it, int) or i >= CPE:
                        act.wait_ge(fc2_step, it * (2 * CPE) + (i + 1 - CPE))
                    c = i % CPE
                    nc.scalar.activation(h1[:, c], ST[:, c // 2, c % 2, 0:N], ACT.Gelu,
                                         bias=vec[:, bass.ds(it * (2 * CPE) + (B1_AT + i), 1)]).then_inc(gelu_done, 1)
            gelus(0)
            with act.Fori(1, E // 2) as it:
                gelus(it)
            evac_mx(v0, 0)
            run_windows(act, 1, window)
            finish_pass(1)

        @block.vector
        def _(dve):
            def token_ln(n):
                if n == 0:
                    dve.wait_ge(ld_x, 32)
                elif n == 3:
                    dve.wait_ge(expert_added, E)
                else:
                    dve.wait_ge(x_added, n)
                for t in range(TT):
                    last = nc.vector.bn_stats(xstat[:, t], xt[:, t])
                last.then_inc(xstat_ready, 1)
                dve.wait_ge(xstat_ready, n + 1)
                for t in range(TT):
                    last = nc.vector.bn_aggr(xmv[:, t], xstat[:, t])
                last.then_inc(xmv_ready, 1)
                dve.wait_ge(xmv_ready, n + 1)
                nc.vector.tensor_scalar(xvar[:], xmv[:, :, 1], EPS, None, ALU.add).then_inc(xvar_ready, 1)
                dve.wait_ge(xrstd_ready, n + 1)
                for t in range(TT):
                    last = nc.vector.tensor_scalar(xn[:, t], xt[:, t], xmv[:, t, 0:1], xrstd[:, t:t + 1],
                                                   ALU.subtract, ALU.mult)
                last.then_inc(xn_ready, 1)
                dve.wait_ge(lnt_full, n + 1)
                if n == 0:
                    dve.wait_ge(ld_vec, 64)
                nc.vector.tensor_scalar(hT[:], MI[:, 0:N], ln_vec(X_LN[n], 0), ln_vec(X_LN[n], 1),
                                        ALU.mult, ALU.add).then_inc(hT_ready, 1)

            def split_q(n):
                dve.wait_ge(qp_full, n + 1)
                if n:
                    dve.wait_ge(qall_loaded, 16 * 2 * TERMS * n)
                nc.vector.tensor_scalar(qf[:], MI[:, 0:N], bias_q(n), None, ALU.add).then_inc(qf_ready, 1)
                nc.vector.tensor_scalar(qsplit[:, 0], MI[:, 0:N], bias_q(n), None, ALU.add).then_inc(qp_read, 1)
                dve.wait_ge(qf_ready, n + 1)
                dve.wait_ge(qp_read, n + 1)
                nc.vector.tensor_tensor(qr[:], qf[:], qsplit[:, 0], ALU.subtract).then_inc(qr_ready, 1)
                dve.wait_ge(qr_ready, n + 1)
                nc.vector.tensor_copy(qsplit[:, 1], qr[:]).then_inc(q2_ready, 1)
                dve.wait_ge(q2_ready, n + 1)
                nc.vector.tensor_tensor(qsplit[:, 2], qr[:], qsplit[:, 1], ALU.subtract).then_inc(qsplit_ready, 1)

            def split_k_sa():
                dve.wait_ge(sa_kp_full, 1)
                dve.wait_ge(qsplit_ready, 1)
                nc.vector.tensor_scalar(qf[:], MI[:, 0:N], bias_k(0), None, ALU.add).then_inc(sa_kf, 1)
                nc.vector.tensor_scalar(ks_sa[:, 0], MI[:, 0:N], bias_k(0), None, ALU.add).then_inc(sa_kp_read, 1)
                dve.wait_ge(sa_kf, 1)
                dve.wait_ge(sa_kp_read, 1)
                nc.vector.tensor_tensor(qr[:], qf[:], ks_sa[:, 0], ALU.subtract).then_inc(sa_kr, 1)
                dve.wait_ge(sa_kr, 1)
                nc.vector.tensor_copy(ks_sa[:, 1], qr[:]).then_inc(sa_k2, 1)
                dve.wait_ge(sa_k2, 1)
                nc.vector.tensor_tensor(ks_sa[:, 2], qr[:], ks_sa[:, 1], ALU.subtract).then_inc(sa_ksplit, 1)

            def ctx_stats(n, chunks):
                if chunks[0] == 0:
                    dve.wait_ge(ld_ctx[n.par], n.par_count(16, 16))
                for c in chunks:
                    last = nc.vector.bn_stats(cstat[:, c], cx[n.par][:, c])
                if chunks[-1] == NCH - 1:
                    last.then_inc(cstat_ready, 1)

            def ctx_aggregate(n):
                for c in range(NCH):
                    last = nc.vector.bn_aggr(cmv[:, c], cstat[:, c])
                last.then_inc(cmv_ready, 1)
                dve.wait_ge(cmv_ready, n.count(1, 1))
                nc.vector.tensor_scalar(cvar[:], cmv[:, :, 1], EPS, None, ALU.add).then_inc(cvar_ready, 1)

            def ctx_normalise(n, thirds=range(3)):
                dve.wait_ge(crstd_ready, n.count(1, 1))
                for i in thirds:
                    for c in range(CPT * i, CPT * (i + 1)):
                        last = nc.vector.tensor_scalar(cx[n.par][:, c], cx[n.par][:, c], cmv[:, c, 0:1],
                                                       crstd[:, c:c + 1], ALU.subtract, ALU.mult)
                    last.then_inc(cn_ready, 1)

            def k_second_part(n, i):
                dve.wait_ge(kr_done, n.count(3, i + 1))
                c = slice(THIRD * i, THIRD * (i + 1))
                nc.vector.tensor_copy(ksplit[n.par][:, 1, c], kr[:, c]).then_inc(k2_done, 1)

            def reduce_tile(n, j):
                dve.wait_ge(sm_full, n.count(TILES, j + 1))
                nc.vector.tensor_reduce(mxp[:, j // 3, j % 3:j % 3 + 1], SM[0:PC, j % 2, 0:THIRD], AX.X,
                                        ALU.max).then_inc(sm_red, 1)

            def max_parts(n, half):
                dve.wait_ge(sm_red, n.count(TILES, TILES // 2 * (half + 1)))
                nc.vector.tensor_reduce(nmx[:], mxp[:, 4 * half:4 * half + 4], AX.X, ALU.max, negate=True
                                        ).then_inc(nmx_ready, 1)
                wait(dve, mx_full, n.count(2, half))
                dve.wait_ge(nmx_ready, n.count(2, half + 1))
                nc.vector.tensor_copy(mparts[:, 0], nmx[:]).then_inc(m1_ready, 1)
                dve.wait_ge(m1_ready, n.count(2, half + 1))
                nc.vector.tensor_tensor(mparts[:, 1], nmx[:], mparts[:, 0], ALU.subtract).then_inc(mparts_ready, 1)

            def copy_q(par, u):
                src = qall[0:SROWS, :, :, bass.ds(u * L, L)].rearrange("r p h q -> r (p h) q")
                return nc.vector.tensor_copy(qst[par][0:SROWS].rearrange("r p (h q) -> r (p h) q", h=2), src)

            def place_q(n):
                if n.s == 0 and n.it is None and n.c == 0:
                    dve.wait_ge(qall_loaded, 16 * 2 * TERMS * 2)
                if n.s == 1 and n.it is None and n.c == 0:
                    dve.wait_ge(qall_loaded, 16 * 2 * TERMS * 3)
                if n.s or n.it is not None or n.c >= 2:
                    dve.wait_ge(st_full, (n + -2).count(STEPS, STEPS))
                copy_q(n.par, n.u).then_inc(qst_ready, 1)

            def normalise(full, rden_sem, done, full_at, rden_at, par):
                dve.wait_ge(full, full_at)
                heads = MI[0:L, :].rearrange("q (h x) -> q h x", x=32)
                nc.vector.reciprocal(rden[:], heads[:, :, DH]).then_inc(rden_sem, 1)
                dve.wait_ge(rden_sem, rden_at)
                nc.vector.tensor_tensor(on[:, par], heads[:, :, 0:DH],
                                        rden[:].unsqueeze(2).broadcast_to([L, H, DH]), ALU.mult).then_inc(done, 1)

            def normalise_unit(n):
                normalise(pot_full, rden_ready, norm_done, n.count(1, 1), n.count(1, 1), n.par)

            def add_projection(n):
                dve.wait_ge(op_full, n + 1)
                nc.vector.tensor_tensor(xt[:], xt[:], MI[0:TP, :].rearrange("p (t d) -> p t d", t=TT), ALU.add
                                        ).then_inc(x_proj, 1)
                dve.wait_ge(x_proj, n + 1)
                bo = rows[:, D * n:D * (n + 1)].unsqueeze(1).broadcast_to([TP, TT, D])
                nc.vector.tensor_tensor(xt[:], xt[:], bo, ALU.add).then_inc(x_added, 1)

            def window(n):
                nxt, k_unit = n + 1, n + 2
                ln_unit = n + 3 if n.s == 0 and (n + 3).exists() else None
                if not nxt.exists():
                    max_parts(n, 1)
                for k in range(STEPS):
                    if nxt.exists():
                        first, rest = STEP_TILES[k][0], STEP_TILES[k][1:]
                        if k == 5 and ln_unit is not None:
                            dve.wait_ge(cstat_ready, ln_unit.count(1, 1))
                        reduce_tile(nxt, first)
                        if k == 0:
                            max_parts(n, 1)
                    if k == BACK_STEP and (n + -1).exists():
                        normalise_unit(n + -1)
                    if nxt.exists():
                        if k == STEPS - 1 and k_unit.exists():
                            place_q(k_unit)
                        for j in rest:
                            reduce_tile(nxt, j)
                        if TILES // 2 - 1 in STEP_TILES[k]:
                            max_parts(nxt, 0)
                    if 0 <= k - K_STEP - 1 < 3 and k_unit.exists():
                        k_second_part(k_unit, k - K_STEP - 1)
                    if ln_unit is not None:
                        if k in (2, 3, 4):
                            ctx_stats(ln_unit, range(4 * (k - 2), 4 * (k - 1)))
                        if k == 5:
                            ctx_aggregate(ln_unit)
                        if k in (8, 9, 10):
                            ctx_normalise(ln_unit, (k - 8,))

            every = range(NCH)
            u0, u1 = Unit(0, None, 0), Unit(0, None, 1)
            token_ln(0)
            nc.vector.tensor_copy(identb[:], ident[:]).then_inc(identb_ready, 1)
            split_q(0)
            split_k_sa()
            ctx_stats(u0, every)
            dve.wait_ge(cstat_ready, u0.count(1, 1))
            ctx_aggregate(u0)
            nc.vector.tensor_reduce(wabs[:], watt[:, 2], AX.X, ALU.add, apply_absolute_value=True
                                    ).then_inc(wabs_ready, 1)
            ctx_normalise(u0)
            dve.wait_ge(gam_full, 1)
            nc.vector.tensor_copy(gam[:], MI[:, 0:4]).then_inc(gam_ready, 1)
            dve.wait_ge(qall_loaded, 16 * 2 * TERMS)
            copy_q(0, 0).then_inc(sa_qst, 1)
            copy_q(1, 1).then_inc(sa_qst, 1)
            for b in range(B):
                dve.wait_ge(sa_sm_full, b + 1)
                nc.vector.tensor_reduce(nmx_sa[:, :, b], SM[0:PC, b % 2, 0:N].rearrange("q (p k) -> q p k", p=PAIRS),
                                        AX.X, ALU.max, negate=True).then_inc(sa_red, 1)
                if b + 2 < B:
                    copy_q(b % 2, b + 2).then_inc(sa_qst, 1)
            dve.wait_ge(sa_red, B)
            flat = nmx_sa[:].rearrange("q p b -> q (p b)")
            nc.vector.tensor_copy(mparts_sa[:, 0], flat).then_inc(sa_m1, 1)
            dve.wait_ge(sa_m1, 1)
            nc.vector.tensor_tensor(mparts_sa[:, 1], flat, mparts_sa[:, 0], ALU.subtract).then_inc(sa_mparts, 1)
            ctx_stats(u1, every)
            dve.wait_ge(cstat_ready, u1.count(1, 1))
            ctx_aggregate(u1)
            for i in range(3):
                k_second_part(u0, i)
            ctx_normalise(u1)

            dve.wait_ge(gam_ready, 1)
            nc.vector.tensor_scalar(thr[:, 0], gam[:], EPS, 0.5, ALU.add, ALU.mult)
            nc.vector.tensor_scalar(thr[:, 1], gam[:], EPS, -0.5, ALU.add, ALU.mult).then_inc(thr_ready, 1)
            dve.wait_ge(thr_ready, 1)
            for w in range(4):
                nc.vector.tensor_scalar(wt[:, 0, w], watt[:, 2, w], thr[:, 0, w:w + 1], None, ALU.is_gt)
                last = nc.vector.tensor_scalar(wt[:, 1, w], watt[:, 2, w], thr[:, 1, w:w + 1], None, ALU.is_lt)
            last.then_inc(tern1, 1)
            dve.wait_ge(tern1, 1)
            nc.vector.tensor_tensor(wt[:, 0], wt[:, 0], wt[:, 1], ALU.subtract).then_inc(tern2, 1)
            dve.wait_ge(tern2, 1)
            for w in range(4):
                last = nc.vector.scalar_tensor_tensor(out=wt[:, 1, w], in0=wt[:, 0, w], scalar=gam[:, w:w + 1],
                                                      in1=watt[:, 2, w], op0=ALU.mult, op1=ALU.subtract)
            last.then_inc(tern3, 1)
            dve.wait_ge(tern3, 1)
            nc.vector.tensor_tensor(watt[:, 2], watt[:, 2], wt[:, 1], ALU.add).then_inc(wq_ready, 1)

            for b in range(B):
                normalise(sa_pot, sa_rden, sa_norm, b + 1, b + 1, b % 2)
            ctx_stats(u0 + 2, every)
            dve.wait_ge(cstat_ready, (u0 + 2).count(1, 1))
            ctx_aggregate(u0 + 2)
            for i in range(3):
                k_second_part(u1, i)
            ctx_normalise(u0 + 2)
            add_projection(0)
            token_ln(1)
            split_q(1)

            def start_pass(s):
                first = Unit(s, None, 0)
                place_q(first)
                place_q(first + 1)
                for j in range(TILES):
                    reduce_tile(first, j)
                    if j == TILES // 2 + 1:
                        max_parts(first, 0)

            def finish_pass(s):
                normalise_unit(Unit(s, None, B - 1))
                add_projection(s + 1)

            start_pass(0)
            run_windows(dve, 0, window)
            finish_pass(0)

            v0 = Unit(1, None, 0)
            token_ln(2)
            for i in range(3):
                k_second_part(v0, i)
            dve.wait_ge(rt_full, 1)
            rb = rows[:, RB0:RB0 + E].unsqueeze(1).broadcast_to([TP, TT, E])
            nc.vector.tensor_tensor(lg[:], MI[0:TP, 0:TT * E].rearrange("p (t e) -> p t e", t=TT), rb, ALU.add
                                    ).then_inc(lg_ready, 1)
            dve.wait_ge(lg_ready, 1)
            mine = lg[:].unsqueeze(3).broadcast_to([TP, TT, E, E])
            other = lg[:].unsqueeze(2).broadcast_to([TP, TT, E, E])
            tri = rows[:, TRI0:TRI0 + E * E].unsqueeze(1).broadcast_to([TP, TT, E * E])
            nc.vector.tensor_tensor(cmp[:, 0], other, mine, ALU.is_gt)
            nc.vector.tensor_tensor(cmp[:, 1], other, mine, ALU.is_equal)
            nc.vector.tensor_reduce(top[:, 0], lg[:], AX.X, ALU.max).then_inc(cmp_ready, 1)
            dve.wait_ge(cmp_ready, 1)
            eq = cmp[:, 1].rearrange("p t e f -> p t (e f)")
            nc.vector.tensor_tensor(eq, eq, tri, ALU.mult).then_inc(cmp_ready, 1)
            dve.wait_ge(cmp_ready, 2)
            both = cmp[:, 0].rearrange("p t e f -> p t (e f)")
            nc.vector.tensor_tensor(both, both, eq, ALU.add).then_inc(cmp_ready, 1)
            dve.wait_ge(cmp_ready, 3)
            nc.vector.tensor_reduce(rank[:], cmp[:, 0], AX.X, ALU.add)
            nc.vector.tensor_tensor(lg[:], lg[:], top[:, 0].unsqueeze(2).broadcast_to([TP, TT, E]), ALU.subtract
                                    ).then_inc(gexp_in, 1)
            dve.wait_ge(gexp_in, 1)
            nc.vector.tensor_scalar(rank[:], rank[:], 1.5, None, ALU.is_lt).then_inc(rank_ready, 1)
            dve.wait_ge(gexp_done, 1)
            dve.wait_ge(rank_ready, 1)
            nc.vector.tensor_tensor(gates[:], gates[:], rank[:], ALU.mult).then_inc(gate_step, 1)
            dve.wait_ge(gate_step, 1)
            nc.vector.tensor_reduce(top[:, 1], gates[:], AX.X, ALU.add).then_inc(gate_step, 1)
            dve.wait_ge(gate_step, 2)
            nc.vector.reciprocal(top[:, 2], top[:, 1]).then_inc(gate_step, 1)
            dve.wait_ge(gate_step, 3)
            nc.vector.tensor_tensor(gates[:], gates[:], top[:, 2].unsqueeze(2).broadcast_to([TP, TT, E]), ALU.mult
                                    ).then_inc(gates_ready, 1)
            for i in range(3):
                k_second_part(v0 + 1, i)
            dve.wait_ge(gt_full, 1)
            nc.vector.tensor_copy(gT[:], MI[0:E, 0:N]).then_inc(gT_ready, 1)
            dve.wait_ge(b2_full, 1)
            nc.vector.tensor_tensor(xt[:], xt[:], MI[0:TP, :].rearrange("p (t d) -> p t d", t=TT), ALU.add
                                    ).then_inc(b2_added, 1)
            dve.wait_ge(b2_added, 1)

            def add_experts(it):
                for j in range(2):
                    dve.wait_ge(fc2_step, it * (2 * CPE) + (j + 1) * CPE)
                    wait(dve, expert_added, it * 2 + j)
                    for t in range(TT):
                        last = nc.vector.scalar_tensor_tensor(
                            out=xt[:, t], in0=SM[0:TP, j, D * t:D * (t + 1)], scalar=gates[:, t, bass.ds(it * 2 + j, 1)],
                            in1=xt[:, t], op0=ALU.mult, op1=ALU.add)
                    last.then_inc(expert_added, 1)
            add_experts(0)
            with dve.Fori(1, E // 2) as it:
                add_experts(it)
            token_ln(3)
            split_q(2)
            start_pass(1)
            run_windows(dve, 1, window)
            finish_pass(1)

        @block.tensor
        def _(pe):
            mm = nc.tensor.matmul

            def misc_free(prev):
                if prev is not None:
                    pe.wait_ge(*prev)

            def transpose_tokens(n, prev):
                misc_free(prev)
                pe.wait_ge(xn_ready, n + 1)
                for t in range(TT):
                    last = nc.tensor.transpose(MI[:, TP * t:TP * (t + 1)], xn[:, t], ident[0:TP, 0:TP])
                last.then_inc(lnt_full, 1)
                return hT_ready, n + 1

            def project_q(n, ln):
                pe.wait_ge(hT_ready, ln + 1)
                mm(MI[:, 0:N], watt[:, n, 0], hT[:], start=True, stop=True).then_inc(qp_full, 1)
                return qp_read, n + 1

            def project_out(n, prev, done):
                misc_free(prev)
                pe.wait_ge(*done)
                for t in range(TT):
                    last = mm(MI[0:TP, D * t:D * (t + 1)], attnT[:, TP * t:TP * (t + 1)], watt[:, n, 3],
                              start=True, stop=True)
                last.then_inc(op_full, 1)
                return x_added, n + 1

            def transpose_ctx(n, i, prev):
                misc_free(prev)
                pe.wait_ge(cn_ready, n.count(3, i + 1))
                for c in range(CPT):
                    last = nc.tensor.transpose(MI[:, KC * c:KC * (c + 1)], cx[n.par][:, CPT * i + c],
                                               ident[0:KC, 0:KC])
                last.then_inc(xt_full, 1)
                return xt_evac, n.count(3, i + 1)

            def project_k(n, i, prev):
                misc_free(prev)
                if n.s == 0:
                    pe.wait_ge(xt_evac, n.count(3, i + 1))
                else:
                    pe.wait_ge(ld_xT[n.par], n.pass_par_count(16, 16))
                mm(MI[:, 0:THIRD], watt[:, n.s + 1, 1], xT[n.par][:, THIRD * i:THIRD * (i + 1)],
                   start=True, stop=True).then_inc(kp_full, 1)
                return k_evac, n.count(6, 2 * i + 2)

            def project_v(n, i, prev):
                misc_free(prev)
                if i == 0 and n.s == 0:
                    pe.wait_ge(xt_evac, n.count(3, 3))
                for c in range(CPT):
                    at = KC * (CPT * i + c)
                    last = mm(MI[0:KC, D * c:D * (c + 1)], xT[n.par][:, at:at + KC], watt[:, n.s + 1, 2],
                              start=True, stop=True)
                last.then_inc(vp_full, 1)
                return v_evac, n.count(3, i + 1)

            def transpose_max(n, half):
                pe.wait_ge(mparts_ready, n.count(2, half + 1))
                nc.tensor.transpose(MX[half], mparts[:].rearrange("q m p -> q (m p)"),
                                    identb[0:PC, 0:PC]).then_inc(mx_full, 1)

            def transpose_po():
                for half in range(2):
                    for hh in range(2):
                        at = 256 * half + (128 - VW) * hh
                        last = mm(MI[0:L, at:at + 128], po[:, PC * half + L * hh:PC * half + L * (hh + 1)],
                                  ident[:], start=True, stop=True, skip_group_check=True)
                return last

            def output_back(n, prev):
                misc_free(prev)
                pe.wait_ge(po_evac, n.count(1, 1))
                transpose_po().then_inc(pot_full, 1)
                return norm_done, n.count(1, 1)

            def output_forth(n):
                pe.wait_ge(norm_done, n.count(1, 1))
                mm(OT, on[:, n.par].rearrange("q h d -> q (h d)"), ident[0:L, 0:L], start=True, stop=True
                   ).then_inc(ont_full, 1)

            def scores(n, k):
                half = k // HSTEP
                if k % HSTEP == 0:
                    pe.wait_ge(shift_loaded[half][n.par], n.par_count(16, 16))
                wait(pe, exp_done, n.count(STEPS, k - 1))
                for cc in range(2):
                    at = KC * (2 * (k % HSTEP) + cc)
                    for p in range(4):
                        last = mm(ST[:, k % 2, cc, PC * p:PC * (p + 1)], kst[n.par][:, 4 * half + p, at:at + 128],
                                  qst[n.par][:, 4 * half + p], start=True, stop=True)
                last.then_inc(st_full, 1)
                if k == 1:
                    transpose_max(n, 1)
                if k == MX_STEP and (n + 1).exists():
                    transpose_max(n + 1, 0)
                if k == FORTH_STEP and (n + -1).exists():
                    output_forth(n + -1)

            def max_tile(n, j):
                if j == 0:
                    pe.wait_ge(qst_ready, n.count(1, 1))
                    pe.wait_ge(kst_loaded[0][n.par], n.par_count(16 * TERMS, 16 * TERMS))
                if j == TILES // 2:
                    pe.wait_ge(kst_loaded[1][n.par], n.par_count(16 * TERMS, 16 * TERMS))
                wait(pe, sm_red, n.count(TILES, j - 1))
                at = THIRD * (j % 3)
                mm(SM[0:PC, j % 2, 0:THIRD], qst[n.par][0:SROWS, j // 3], kst[n.par][0:SROWS, j // 3, at:at + THIRD],
                   start=True, stop=True).then_inc(sm_full, 1)

            def values(n, k):
                half = k // HSTEP
                pe.wait_ge(exp_done, n.count(STEPS, k + 1))
                if k == 0:
                    wait(pe, po_evac, n.count(1, 0))
                if k < HSTEP:
                    pe.wait_ge(v_evac, n.count(3, (2 * k + 1) // CPT + 1))
                for cc in range(2):
                    c = 2 * (k % HSTEP) + cc
                    for p in range(4):
                        at = 2 * VW * (4 * half + p)
                        last = mm(PO[32 * p:32 * p + 32, PC * half:PC * (half + 1)], vaug[n.par][:, c, at:at + 32],
                                  PT[0:KC, k % 2, cc, PC * p:PC * (p + 1)], start=(k == 0 and cc == 0),
                                  stop=(k % HSTEP == HSTEP - 1 and cc == 1), skip_group_check=True)
                last.then_inc(pv_done, 1)

            def window(n):
                nxt, k_unit, prv = n + 1, n + 2, n + -1
                ln_unit = n + 3 if n.s == 0 and (n + 3).exists() else None
                if not prv.exists():
                    prev = (qp_read, n.s + 2)
                elif n.s == 0 and k_unit.exists():
                    prev = (xt_evac, k_unit.count(3, 3))
                else:
                    prev = (v_evac, n.count(3, 3))
                for k in range(STEPS):
                    scores(n, k)
                    tiles = list(STEP_TILES[k]) if nxt.exists() else []
                    if tiles:
                        max_tile(nxt, tiles[0])
                    if k:
                        values(n, k - 1)
                    elif prv.exists():
                        values(prv, STEPS - 1)
                    for j in tiles[1:-1]:
                        max_tile(nxt, j)
                    if 0 <= k - K_STEP < 3 and k_unit.exists():
                        prev = project_k(k_unit, k - K_STEP, prev)
                    if k == BACK_STEP and prv.exists():
                        prev = output_back(prv, prev)
                    if 0 <= k - V_STEP < 3 and nxt.exists():
                        prev = project_v(nxt, k - V_STEP, prev)
                    if 0 <= k - CTX_STEP < 3 and ln_unit is not None:
                        prev = transpose_ctx(ln_unit, k - CTX_STEP, prev)
                    if len(tiles) > 1:
                        max_tile(nxt, tiles[-1])
                return prev

            u0, u1 = Unit(0, None, 0), Unit(0, None, 1)
            pe.wait_ge(ld_x, 32)
            prev = transpose_tokens(0, None)
            pe.wait_ge(ld_w, 16)
            prev = project_q(0, 0)
            misc_free(prev)
            mm(MI[:, 0:N], watt[:, 0, 1], hT[:], start=True, stop=True).then_inc(sa_kp_full, 1)
            prev = (sa_kp_read, 1)
            for i in range(2):
                misc_free(prev)
                for c in range(4):
                    b = 4 * i + c
                    last = mm(MI[0:L, D * c:D * (c + 1)], hT[:, L * b:L * (b + 1)], watt[:, 0, 2], start=True, stop=True)
                last.then_inc(sa_vp_full, 1)
                prev = (sa_v_evac, i + 1)
            misc_free(prev)
            pe.wait_ge(wabs_ready, 1)
            pe.wait_ge(consts_ready, 1)
            mm(MI[:, 0:4], mean_w[:], wabs[:], start=True, stop=True).then_inc(gam_full, 1)
            prev = (gam_ready, 1)
            for i in range(3):
                prev = transpose_ctx(u0, i, prev)
            pe.wait_ge(sa_kst, 16 * 2 * TERMS)
            for b in range(B):
                pe.wait_ge(sa_qst, b + 1)
                wait(pe, sa_red, b - 1)
                for p in range(PAIRS):
                    last = mm(SM[0:PC, b % 2, L * p:L * (p + 1)], qst[b % 2][0:SROWS, p],
                              kst_sa[0:SROWS, p, L * b:L * (b + 1)], start=True, stop=True)
                last.then_inc(sa_sm_full, 1)
            for i in range(3):
                prev = project_k(u0, i, prev)
            misc_free(prev)
            pe.wait_ge(sa_mparts, 1)
            pe.wait_ge(identb_ready, 1)
            nc.tensor.transpose(MI[:].bitcast(BF16)[:, 0:PC], mparts_sa[:].rearrange("q m c -> q (m c)"),
                                identb[0:PC, 0:PC]).then_inc(sa_mx_full, 1)
            prev = (sa_mx_evac, 1)
            for i in range(3):
                prev = project_v(u0, i, prev)
            for i in range(3):
                prev = transpose_ctx(u1, i, prev)
            pe.wait_ge(sa_shift, 16 * MROWS)
            pe.wait_ge(ld_ones, 32)
            pe.wait_ge(consts_ready, 2)
            for b in range(B + 3):
                if b < B:
                    wait(pe, sa_exp, b - 1)
                    for p in range(PAIRS):
                        at = ST[0:L, b % 2, p // 4, PC * (p % 4):PC * (p % 4 + 1)]
                        mm(at, kst_sa[:, p, L * b:L * (b + 1)], qall[:, p, :, L * b:L * (b + 1)],
                           start=True, stop=False)
                        last = mm(at, ones_rows[:, 0:L], shift_sa[:, B * p + b], start=False, stop=True)
                    last.then_inc(sa_st, 1)
                if 0 <= b - 1 < B:
                    v = b - 1
                    pe.wait_ge(sa_exp, v + 1)
                    wait(pe, sa_po, v)
                    for p in range(PAIRS):
                        half, q = p // 4, p % 4
                        last = mm(PO[32 * q:32 * q + 32, PC * half:PC * (half + 1)],
                                  vaug_sa[:, v, 2 * VW * p:2 * VW * p + 32],
                                  PT[0:L, v % 2, half, PC * q:PC * (q + 1)], start=(half == 0), stop=True,
                                  skip_group_check=True)
                    last.then_inc(sa_pv, 1)
                if 0 <= b - 2 < B:
                    misc_free(prev)
                    pe.wait_ge(sa_po, b - 1)
                    transpose_po().then_inc(sa_pot, 1)
                    prev = (sa_norm, b - 1)
                if 0 <= b - 3 < B:
                    misc_free(prev)
                    pe.wait_ge(sa_norm, b - 2)
                    nc.tensor.transpose(MI[:, 0:L], on[:, (b - 3) % 2].rearrange("q h d -> q (h d)"),
                                        ident[0:L, 0:L]).then_inc(sa_ont, 1)
                    prev = (sa_att, b - 2)
            for i in range(3):
                prev = project_k(u1, i, prev)
            for i in range(3):
                prev = transpose_ctx(u0 + 2, i, prev)
            prev = project_out(0, prev, (sa_att, B))
            prev = transpose_tokens(1, prev)
            prev = project_q(1, 1)

            def start_pass(s):
                first = Unit(s, None, 0)
                for j in range(TILES):
                    max_tile(first, j)
                    if j == TILES - 4:
                        transpose_max(first, 0)

            def finish_pass(s):
                last = Unit(s, None, B - 1)
                values(last, STEPS - 1)
                prev = output_back(last, (v_evac, last.count(3, 3)))
                output_forth(last)
                return prev

            start_pass(0)
            run_windows(pe, 0, window)
            prev = finish_pass(0)
            prev = project_out(1, prev, (ont_evac, B))

            v0 = Unit(1, None, 0)
            pe.wait_ge(wq_ready, 1)
            for i in range(3):
                prev = project_k(v0, i, prev)
            prev = transpose_tokens(2, prev)
            misc_free(prev)
            for t in range(TT):
                last = mm(MI[0:TP, E * t:E * (t + 1)], hT[:, TP * t:TP * (t + 1)], rwT[:], start=True, stop=True)
            last.then_inc(rt_full, 1)
            prev = (lg_ready, 1)
            for i in range(3):
                prev = project_v(v0, i, prev)
            for i in range(3):
                prev = project_k(v0 + 1, i, prev)
            misc_free(prev)
            pe.wait_ge(gates_ready, 1)
            for t in range(TT):
                last = nc.tensor.transpose(MI[0:E, TP * t:TP * (t + 1)], gates[:, t], ident[0:TP, 0:TP])
            last.then_inc(gt_full, 1)
            pe.wait_ge(gT_ready, 1)
            for t in range(TT):
                last = mm(MI[0:TP, D * t:D * (t + 1)], gT[:, TP * t:TP * (t + 1)], b2[:], start=True, stop=True)
            last.then_inc(b2_full, 1)

            def experts(it):
                def fc1(i):
                    j, c = i // CPE, i % CPE
                    if c == 0:
                        pe.wait_ge(ld_exp[j], it * 32 + 32)
                    if not isinstance(it, int) or i >= CPE:
                        pe.wait_ge(gelu_done, it * (2 * CPE) + (i + 1 - CPE))
                    mm(ST[:, c // 2, c % 2, 0:N], w1s[j][:, D * c:D * (c + 1)], hT[:], start=True, stop=True
                       ).then_inc(fc1_full, 1)

                def fc2(i):
                    j, c = i // CPE, i % CPE
                    pe.wait_ge(gelu_done, it * (2 * CPE) + (i + 1))
                    if c == 0 and not isinstance(it, int):
                        pe.wait_ge(expert_added, it * 2 + (j - 1))
                    for t in range(TT):
                        last = mm(SM[0:TP, j, D * t:D * (t + 1)], h1[:, c, TP * t:TP * (t + 1)], w2s[j][:, c],
                                  start=(c == 0 and t == 0), stop=(c == CPE - 1), skip_group_check=True)
                    last.then_inc(fc2_step, 1)
                fc1(0)
                for i in range(2 * CPE):
                    if i + 1 < 2 * CPE:
                        fc1(i + 1)
                    fc2(i)
            experts(0)
            with pe.Fori(1, E // 2) as it:
                experts(it)
            prev = transpose_tokens(3, (b2_added, 1))
            prev = project_q(2, 3)
            start_pass(1)
            run_windows(pe, 1, window)
            prev = finish_pass(1)
            project_out(2, prev, (ont_evac, 2 * B))


def _orders():
    n = np.arange(D)
    q_order = (n % PAIRS) * PR + n // PAIRS
    k_order = ((n // 64) * 4 + n % 4) * PR + n % 64 // 4
    half, member, pair, dim = n // 64, n // 32 % 2, n // 8 % 4, n % 8
    o_order = (8 * half + 2 * pair + member) * DH + dim
    return q_order, k_order, o_order


def kernel(**inputs):
    import concourse.bacc as _bacc
    from concourse.bass_utils import run_bass_kernel_spmd as _run

    a = {k: np.asarray(v) for k, v in inputs.items()}
    q_order, k_order, o_order = _orders()

    def attention(wq, wk, wv, wo):
        return np.stack([wq.T[:, q_order], wk.T[:, k_order], wv.T, wo.T[o_order]])

    weights, columns = [], []
    for p in ("L0_xattn_sa_", "L0_xattn_ca_"):
        w, b = a[p + "in_w"], a[p + "in_b"]
        weights.append(attention(w[:D], w[D:2 * D], w[2 * D:], a[p + "out_w"]))
        columns += [b[:D][q_order], b[D:2 * D][k_order], b[2 * D:][o_order]]
    p = "L1_xattn_"
    weights.append(attention(a[p + "Wq"], a[p + "Wk"], a[p + "Wv"], a[p + "Wo"]))
    columns += [a[p + "bq"][q_order], a[p + "bk"][k_order], a[p + "bv"][o_order]]
    for ln in ("L0_xattn_sa_ln_", "L0_xattn_ca_q_ln_", "L0_xattn_ca_kv_ln_", "L0_xattn_moe_ln_"):
        columns += [a[ln + "g"], a[ln + "b"]]
    columns += [a["L1_xattn_ln_gamma"], a["L1_xattn_ln_beta"]]
    columns += list(a["L0_xattn_e_fc1_b"].reshape(E * CPE, D))
    before = np.tril(np.ones((E, E), np.float32), -1)
    arrays = {
        "x": a["x"].reshape(N, D),
        "ctx": a["ctx_1024"],
        "ctxT": a["ctx_1024"].transpose(0, 2, 1),
        "watt": np.stack(weights),
        "vec": np.stack(columns, axis=1),
        "rows": np.concatenate([a["L0_xattn_sa_out_b"], a["L0_xattn_ca_out_b"], a["L1_xattn_bo"],
                                a["L0_xattn_router_b"], before.reshape(-1)]),
        "rwT": a["L0_xattn_router_w"].T,
        "w1T": a["L0_xattn_e_fc1_w"].transpose(0, 2, 1),
        "w2T": a["L0_xattn_e_fc2_w"].transpose(0, 2, 1).reshape(E, CPE, D, D).transpose(0, 2, 1, 3),
        "b2": a["L0_xattn_e_fc2_b"],
        "ident": np.eye(D, dtype=np.float32),
    }
    nc = _bacc.Bacc("TRN2", target_bir_lowering=False, num_devices=1)
    feeds, args = {}, []
    for name, array in arrays.items():
        feeds[f"in_{name}"] = np.ascontiguousarray(array)
        args.append(nc.dram_tensor(f"in_{name}", array.shape, F32, kind="ExternalInput").ap())
    args.append(nc.dram_tensor("out_x", (N, D), F32, kind="ExternalOutput").ap())
    build_kernel(nc, *args)
    result = _run(nc, [feeds], core_ids=[0])
    return result.results[0]["out_x"].reshape(B, L, D)
```

```python
from contextlib import ExitStack

import numpy as np

import concourse.bass as bass
from concourse import mybir

ALU = mybir.AluOpType
ACT = mybir.ActivationFunctionType
AX = mybir.AxisListType
F32 = mybir.dt.float32
BF16 = mybir.dt.bfloat16

B, L, D, T = 8, 56, 128, 1500
H, DH = 16, 8
E, DFF = 8, 512
EPS = 1e-5
N = B * L
TT, TP = 4, 112
PAIRS = H // 2
PR = 2 * DH
K_PART = (0, 0, 0, 1, 1, 2)
Q_PART = (0, 1, 2, 0, 1, 0)
TERMS = len(K_PART)
SROWS = TERMS * PR
MROWS = 2
KROWS = SROWS + MROWS
PC = 2 * L
KC = 125
NCH = T // KC
STEPS = NCH
HSTEP = STEPS // 2
TPAD = KC * (NCH - 1) + 128
THIRD = T // 3
CPT = NCH // 3
VW = 9
VCOLS = 160
SCALE = float(DH) ** -0.5
TILES = PAIRS * 3
CPE = DFF // D
WB = 3
N_LN = 5
RB0, TRI0 = 3 * D, 3 * D + E


K_STEP, BACK_STEP, V_STEP, MX_STEP, FORTH_STEP, CTX_STEP = 0, 3, 4, 6, 7, STEPS - 3


def tiles_of_step():
    per = (3, 3, 3, 2, 2, 2, 2, 1, 1, 1, 2, 2)
    at = [sum(per[:k]) for k in range(STEPS + 1)]
    assert at[-1] == TILES and at[MX_STEP] >= TILES // 2
    return [range(at[k], at[k + 1]) for k in range(STEPS)]


STEP_TILES = tiles_of_step()
SA_STEPS = B + 4
SA_PIECES = {1: (("t", 0, 0), ("t", 0, 1)), 2: (("t", 0, 2), ("k", 0, 0)), 3: (("k", 0, 1), ("k", 0, 2)),
             4: (("v", 0, 0), ("v", 0, 1)), 5: (("v", 0, 2), ("t", 1, 0)), 6: (("t", 1, 1),), 7: (("t", 1, 2),)}


class Unit:

    def __init__(self, s, it, c):
        self.s, self.it, self.c = s, it, c
        self.par = c % 2
        self.u = c if it is None else it * 2 + c

    def __add__(self, d):
        return Unit(self.s, self.it, self.c + d)

    def exists(self):
        return self.it is not None or 0 <= self.c < B

    def count(self, per, off):
        base = (B * self.s + self.c) * per + off
        return base if self.it is None else self.it * (2 * per) + base

    def pass_par_count(self, per, off):
        base = self.c // 2 * per + off
        return base if self.it is None else self.it * per + base

    def par_count(self, per, off):
        base = (B // 2 * self.s + self.c // 2) * per + off
        return base if self.it is None else self.it * per + base


def wait(eng, sem, value):
    if not isinstance(value, int) or value > 0:
        eng.wait_ge(sem, value)


def run_windows(eng, s, window):
    window(Unit(s, None, 0))
    with eng.Fori(0, 2) as it:
        window(Unit(s, it, 1))
        window(Unit(s, it, 2))
    for u in range(5, B):
        window(Unit(s, None, u))


def build_kernel(nc, x_in, ctx_in, ctxT_in, watt_in, vec_in, rows_in, rwT_in, w1T_in, w2T_in, b2_in,
                 ident_in, mask_in, out):
    with ExitStack() as ctx:
        def sb(name, shape, dt=F32):
            return ctx.enter_context(nc.sbuf_tensor(name, shape, dt))

        def sem(name):
            return ctx.enter_context(nc.semaphore(name))

        ST = ctx.enter_context(nc.psum_tensor("ST", [128, 2, 2, 512], F32))
        SM = ctx.enter_context(nc.psum_tensor("SM", [128, 2, 512], F32))
        PO = ctx.enter_context(nc.psum_tensor("PO", [128, 512], F32))
        MI = ctx.enter_context(nc.psum_tensor("MI", [128, 512], F32))
        MX = [ST[0:MROWS * 4, k % 2, 0, 4 * PC:4 * PC + L].bitcast(BF16) for k in (MX_STEP, 1)]
        OT = ST[:, FORTH_STEP % 2, 1, 4 * PC:4 * PC + L]

        ident = sb("ident", [128, 128])
        identb = sb("identb", [128, 128], BF16)
        vec = sb("vec", [128, 3 * WB + 2 * N_LN + E * CPE])
        rows = sb("rows", [TP, 3 * D + E + E * E])
        watt = sb("watt", [128, 3, 4, 128])
        rwT = sb("rwT", [128, E])
        b2 = sb("b2", [E, 128])
        xt = sb("xt", [TP, TT, D])
        xn = sb("xn", [TP, TT, D])
        hT = sb("hT", [128, N])
        xstat = sb("xstat", [TP, TT, 6])
        xmv = sb("xmv", [TP, TT, 2])
        xvar = sb("xvar", [TP, TT])
        xrstd = sb("xrstd", [TP, TT])
        half_neg = sb("half_neg", [128, 16])
        ones_rows = sb("ones_rows", [MROWS, TPAD], BF16)
        qf = sb("qf", [128, N])
        qr = sb("qr", [128, N])
        qsplit = sb("qsplit", [128, 3, N], BF16)
        qall = sb("qall", [SROWS, PAIRS, N], BF16)
        qst = [sb(f"qst{i}", [KROWS, PAIRS, PC], BF16) for i in range(2)]
        kf = sb("kf", [128, T])
        kr = sb("kr", [128, T])
        ksplit = [sb(f"ksplit{i}", [128, 3, T], BF16) for i in range(2)]
        kst = [sb(f"kst{i}", [KROWS, PAIRS, TPAD], BF16) for i in range(2)]
        cx = [sb(f"cx{i}", [KC, NCH, D]) for i in range(2)]
        cstat = sb("cstat", [KC, NCH, 6])
        cmv = sb("cmv", [KC, NCH, 2])
        cvar = sb("cvar", [KC, NCH])
        crstd = sb("crstd", [KC, NCH])
        xT = [sb(f"xT{i}", [128, T]) for i in range(2)]
        vaug = [sb(f"vaug{i}", [KC, NCH, VCOLS]) for i in range(2)]
        PT = sb("PT", [128, 2, 2, 4 * PC])
        po = sb("po", [128, 2 * PC])
        on = sb("on", [L, 2, H, DH])
        rden = sb("rden", [L, H])
        attnT = sb("attnT", [128, N])
        mxp = sb("mxp", [PC, PAIRS, 3])
        nmx = sb("nmx", [PC, 4])
        mparts = sb("mparts", [PC, MROWS, 4], BF16)
        mrow = sb("mrow", [MROWS * 4, 2, PC], BF16)
        mask = sb("mask", [128, H + 2])
        q_sa, k_sa = qf, qr
        qbd = sb("qbd", [128, 2, H, L])
        p_sa = sb("p_sa", [PC, 2, PAIRS, L])
        vaug_sa = sb("vaug_sa", [L, B, VCOLS])
        nmx_sa = sb("nmx_sa", [PC, PAIRS])
        wabs = sb("wabs", [128, 4])
        mean_w = sb("mean_w", [128, 128])
        gam = sb("gam", [128, 4])
        wt = sb("wt", [128, 2, 4, 128])
        thr = sb("thr", [128, 2, 4])
        lg = sb("lg", [TP, TT, E])
        cmp = qbd[0:TP].rearrange("p s h q -> p (s h q)")[:, 0:2 * TT * E * E].rearrange(
            "p (s t e f) -> p s t e f", s=2, t=TT, e=E)
        rank = sb("rank", [TP, TT, E])
        top = sb("top", [TP, 3, TT])
        gates = sb("gates", [TP, TT, E])
        gT = sb("gT", [E, N])
        moe = sb("moe", [128, 4 * DFF + CPE * N])
        w1s = [moe[:, DFF * i:DFF * (i + 1)] for i in range(2)]
        w2s = [moe[:, DFF * (2 + i):DFF * (3 + i)].rearrange("f (c d) -> f c d", d=D) for i in range(2)]
        h1 = moe[:, 4 * DFF:].rearrange("f (c n) -> f c n", c=CPE)


        def tile_bank(j, banks):
            if j % banks < banks - 2:
                return ST[0:PC, 1, j % banks, 0:THIRD]
            return SM[0:PC, j % 2, 0:THIRD]

        def bias_q(layer):
            return vec[:, WB * layer:WB * layer + 1]

        def bias_k(layer):
            return vec[:, WB * layer + 1:WB * layer + 2]

        def bias_v(layer):
            return vec[:, WB * layer + 2:WB * layer + 3]

        def ln_vec(n, which):
            at = 3 * WB + 2 * n + which
            return vec[:, at:at + 1]
        LN_SA, LN_CAQ, LN_CAKV, LN_MOE, LN_L1 = range(N_LN)
        X_LN = (LN_SA, LN_CAQ, LN_MOE, LN_L1)
        B1_AT = 3 * WB + 2 * N_LN

        ld_mask = sem("ld_mask")
        ld_x, ld_vec, ld_w, ld_ones = sem("ld_x"), sem("ld_vec"), sem("ld_w"), sem("ld_ones")
        ld_ctx = [sem(f"ld_ctx{i}") for i in range(2)]
        ld_xT = [sem(f"ld_xT{i}") for i in range(2)]
        ld_exp = [sem(f"ld_exp{i}") for i in range(2)]
        padded, v_ones = sem("padded"), sem("v_ones")
        identb_ready = sem("identb_ready")
        xstat_ready, xmv_ready, xvar_ready, xrstd_ready, xn_ready = (
            sem("xstat_ready"), sem("xmv_ready"), sem("xvar_ready"), sem("xrstd_ready"), sem("xn_ready"))
        lnt_full, hT_ready, qp_full, qf_ready, qp_read, qr_ready, q2_ready, qsplit_ready = (
            sem("lnt_full"), sem("hT_ready"), sem("qp_full"), sem("qf_ready"), sem("qp_read"),
            sem("qr_ready"), sem("q2_ready"), sem("qsplit_ready"))
        qall_loaded = sem("qall_loaded")
        op_full, x_proj, x_added = sem("op_full"), sem("x_proj"), sem("x_added")
        sa_qp_full, sa_q, sa_kp_full, sa_k, sa_qbd, sa_vp_full, sa_v_evac, sa_sm_full, sa_max, sa_sub = (
            sem("sa_qp_full"), sem("sa_q"), sem("sa_kp_full"), sem("sa_k"), sem("sa_qbd"), sem("sa_vp_full"),
            sem("sa_v_evac"), sem("sa_sm_full"), sem("sa_max"), sem("sa_sub"))
        sa_exp, sa_tp_full, sa_pt, sa_pv, sa_po, sa_pot, sa_rden, sa_norm, sa_ont, sa_att = (
            sem("sa_exp"), sem("sa_tp_full"), sem("sa_pt"), sem("sa_pv"), sem("sa_po"), sem("sa_pot"),
            sem("sa_rden"), sem("sa_norm"), sem("sa_ont"), sem("sa_att"))
        wabs_ready, gam_full, gam_ready, thr_ready, tern1, tern2, tern3, wq_ready = (
            sem("wabs_ready"), sem("gam_full"), sem("gam_ready"), sem("thr_ready"), sem("tern1"), sem("tern2"),
            sem("tern3"), sem("wq_ready"))
        cstat_ready, cmv_ready, cvar_ready, crstd_ready, cn_ready = (
            sem("cstat_ready"), sem("cmv_ready"), sem("cvar_ready"), sem("crstd_ready"), sem("cn_ready"))
        xt_full, xt_evac, kp_full, k_evac, kr_done, k2_done, k3_done, vp_full, v_evac = (
            sem("xt_full"), sem("xt_evac"), sem("kp_full"), sem("k_evac"), sem("kr_done"), sem("k2_done"),
            sem("k3_done"), sem("vp_full"), sem("v_evac"))
        kst_loaded = [[sem(f"kst_loaded{h}{p}") for p in range(2)] for h in range(2)]
        qst_ready, sm_full, sm_red, nmx_ready, m1_ready, mparts_ready, mx_full, mx_evac = (
            sem("qst_ready"), sem("sm_full"), sem("sm_red"), sem("nmx_ready"), sem("m1_ready"),
            sem("mparts_ready"), sem("mx_full"), sem("mx_evac"))
        shift_loaded = [[sem(f"shift_loaded{h}{p}") for p in range(2)] for h in range(2)]
        st_full, exp_done, pv_done, po_evac, pot_full, rden_ready, norm_done, ont_full, ont_evac = (
            sem("st_full"), sem("exp_done"), sem("pv_done"), sem("po_evac"), sem("pot_full"),
            sem("rden_ready"), sem("norm_done"), sem("ont_full"), sem("ont_evac"))
        rt_full, lg_ready, cmp_ready, rank_ready, top_ready, gexp_in, gexp_done, gate_step, gates_ready = (
            sem("rt_full"), sem("lg_ready"), sem("cmp_ready"), sem("rank_ready"), sem("top_ready"),
            sem("gexp_in"), sem("gexp_done"), sem("gate_step"), sem("gates_ready"))
        gt_full, gT_ready, b2_full, b2_added = sem("gt_full"), sem("gT_ready"), sem("b2_full"), sem("b2_added")
        fc1_full, gelu_done, fc2_step, expert_added = (
            sem("fc1_full"), sem("gelu_done"), sem("fc2_step"), sem("expert_added"))
        stored = sem("stored")

        block = ctx.enter_context(nc.Block())

        @block.sync
        def _(sp):
            sp.dma_start(xt[:], x_in.rearrange("(t p) d -> p t d", p=TP)).then_inc(ld_x, 16)
            sp.dma_start(ident[:], ident_in).then_inc(ld_x, 16)
            sp.dma_start(vec[:], vec_in).then_inc(ld_vec, 16)
            sp.dma_start(watt[:], watt_in.rearrange("l w i o -> i l w o")).then_inc(ld_w, 16)

            def load_ctx(n):
                if n.it is not None or n.c >= 2:
                    sp.wait_ge(xt_full, (n + -2).count(3, 3))
                src = ctx_in[bass.ds(n.u, 1)].rearrange("a (p c) d -> (a p) c d", c=NCH)
                sp.dma_start(cx[n.par][:], src).then_inc(ld_ctx[n.par], 16)

            def load_xT(n):
                sp.wait_ge(vp_full, (n + -2).count(3, 3))
                src = ctxT_in[bass.ds(n.u, 1)].rearrange("a d t -> (a d) t")
                sp.dma_start(xT[n.par][:], src).then_inc(ld_xT[n.par], 16)

            load_ctx(Unit(0, None, 0))
            load_ctx(Unit(0, None, 1))
            sp.dma_start(mask[:], mask_in).then_inc(ld_mask, 16)
            sp.dma_start(rows[:], rows_in.partition_broadcast(TP)).then_inc(ld_vec, 16)
            sp.dma_start(rwT[:], rwT_in).then_inc(ld_vec, 16)
            sp.dma_start(b2[:], b2_in).then_inc(ld_vec, 16)

            def load_expert(e, j):
                sp.dma_start(w1s[j], w1T_in[bass.ds(e, 1)].rearrange("a i f -> (a i) f")).then_inc(ld_exp[j], 16)
                sp.dma_start(w2s[j], w2T_in[bass.ds(e, 1)].rearrange("a f c d -> (a f) c d")).then_inc(ld_exp[j], 16)

            def load_qall(n):
                sp.wait_ge(qsplit_ready, n + 1)
                for t in range(TERMS):
                    sp.dma_start(qall[t * PR:(t + 1) * PR], qsplit[:, Q_PART[t], :]).then_inc(qall_loaded, 16)

            sp.wait_ge(padded, 1)
            for stack in kst:
                width = stack.shape[2]
                sp.dma_start(stack[SROWS:KROWS], ones_rows[:, 0:width].unsqueeze(1).broadcast_to(
                    [MROWS, PAIRS, width])).then_inc(ld_ones, 16)

            def restack(n, half):
                split = n.count(3, 3) if n.it is None else sp.to_reg(n.count(3, 3))
                if n.s or n.it is not None or n.c >= 2:
                    sp.wait_ge(st_full, (n + -2).count(STEPS, HSTEP * (half + 1)))
                sp.wait_ge(k3_done, split)
                for t in range(TERMS):
                    sp.dma_start(kst[n.par][t * PR:(t + 1) * PR, 4 * half:4 * half + 4, 0:T],
                                 ksplit[n.par][64 * half:64 * half + 64, K_PART[t], :]
                                 ).then_inc(kst_loaded[half][n.par], 16)

            def shift(n, half):
                sp.wait_ge(mx_evac, n.count(2, half + 1))
                sp.dma_start(qst[n.par][SROWS:KROWS, 4 * half:4 * half + 4, :], mrow[:, half, :]
                             ).then_inc(shift_loaded[half][n.par], 16)

            def window(n):
                if n.s == 0 and (n + 3).exists():
                    load_ctx(n + 3)
                if (n + 1).exists():
                    restack(n + 1, 1)
                shift(n, 1)
                if (n + 2).exists():
                    restack(n + 2, 0)
                if (n + 1).exists():
                    shift(n + 1, 0)
                if n.s == 1 and (n + 3).exists():
                    load_xT(n + 3)

            u0, u1 = Unit(0, None, 0), Unit(0, None, 1)
            load_ctx(Unit(0, None, 2))
            restack(u0, 0)
            restack(u0, 1)
            load_expert(0, 0)
            load_expert(1, 1)
            load_qall(0)
            restack(u1, 0)
            shift(u0, 0)
            run_windows(sp, 0, window)
            v0 = Unit(1, None, 0)
            load_xT(v0)
            load_xT(v0 + 1)
            restack(v0, 0)
            restack(v0, 1)
            sp.wait_ge(fc2_step, CPE)
            load_expert(2, 0)
            sp.wait_ge(fc2_step, 2 * CPE)
            load_expert(3, 1)
            with sp.Fori(1, 3) as it:
                for j in range(2):
                    sp.wait_ge(fc2_step, it * (2 * CPE) + (j + 1) * CPE)
                    load_expert(it * 2 + (j + 2), j)
            load_qall(1)
            load_xT(v0 + 2)
            restack(v0 + 1, 0)
            shift(v0, 0)
            run_windows(sp, 1, window)
            sp.wait_ge(x_added, 3)
            sp.dma_start(out.rearrange("(t p) d -> p t d", p=TP), xt[:]).then_inc(stored, 16)
            sp.wait_ge(stored, 16)

        @block.gpsimd
        def _(pool):
            nc.gpsimd.memset(half_neg[:], -0.5)
            nc.gpsimd.memset(mean_w[:], 1.0 / (D * D))
            nc.gpsimd.memset(ones_rows[:], 1.0)
            for s in range(2):
                last = nc.gpsimd.memset(kst[s][0:SROWS, :, T:TPAD], 0.0)
            last.then_inc(padded, 1)

            def spread_q(b):
                pool.wait_ge(sa_q, 1)
                wait(pool, sa_sm_full, b - 1)
                nc.gpsimd.tensor_tensor(
                    qbd[:, b % 2], q_sa[:, L * b:L * (b + 1)].unsqueeze(1).broadcast_to([128, H, L]),
                    mask[:, 0:H].unsqueeze(2).broadcast_to([128, H, L]), ALU.mult).then_inc(sa_qbd, 1)

            def token_rstd(n):
                pool.wait_ge(xvar_ready, n + 1)
                nc.gpsimd.tensor_tensor(xrstd[:], xvar[:], half_neg[0:TP, 0:TT], ALU.pow).then_inc(xrstd_ready, 1)

            def ctx_rstd(n):
                pool.wait_ge(cvar_ready, n.count(1, 1))
                nc.gpsimd.tensor_tensor(crstd[:], cvar[:], half_neg[0:KC, 0:NCH], ALU.pow).then_inc(crstd_ready, 1)

            def k_rest(n, i):
                wait(pool, k3_done, n.count(3, i - 2))
                pool.wait_ge(k_evac, n.count(6, 2 * i + 2))
                c = slice(THIRD * i, THIRD * (i + 1))
                nc.gpsimd.tensor_tensor(kr[:, c], kf[:, c], ksplit[n.par][:, 0, c], ALU.subtract).then_inc(kr_done, 1)

            def k_third_part(n, i):
                pool.wait_ge(k2_done, n.count(3, i + 1))
                c = slice(THIRD * i, THIRD * (i + 1))
                nc.gpsimd.tensor_tensor(ksplit[n.par][:, 2, c], kr[:, c], ksplit[n.par][:, 1, c],
                                        ALU.subtract).then_inc(k3_done, 1)

            def k_parts(n, ln_unit):
                k_rest(n, 0)
                k_rest(n, 1)
                k_third_part(n, 0)
                k_rest(n, 2)
                k_third_part(n, 1)
                k_third_part(n, 2)
                if ln_unit is not None:
                    ctx_rstd(ln_unit)

            def window(n):
                ln_unit = n + 3 if n.s == 0 and (n + 3).exists() else None
                if (n + 2).exists():
                    k_parts(n + 2, ln_unit)

            pool.wait_ge(padded, 1)
            token_rstd(0)
            u0, u1 = Unit(0, None, 0), Unit(0, None, 1)
            pool.wait_ge(ld_mask, 16)
            spread_q(0)
            spread_q(1)
            for i in range(SA_STEPS):
                if i + 2 < B:
                    spread_q(i + 2)
                if i == 0:
                    ctx_rstd(u0)
                if i == 3:
                    ctx_rstd(u1)
                if i == 8:
                    ctx_rstd(u0 + 2)
                for kind, unit, third in SA_PIECES.get(i - 1, ()):
                    if kind == "k":
                        k_rest(u0, third)
                for kind, unit, third in SA_PIECES.get(i - 3, ()):
                    if kind == "k":
                        k_third_part(u0, third)
            token_rstd(1)
            k_parts(u1, None)
            run_windows(pool, 0, window)
            token_rstd(2)
            v0 = Unit(1, None, 0)
            k_parts(v0, None)
            token_rstd(3)
            k_parts(v0 + 1, None)
            run_windows(pool, 1, window)

        @block.scalar
        def _(act):
            def evac_sa_v():
                for i in range(2):
                    act.wait_ge(sa_vp_full, i + 1)
                    if i == 0:
                        act.wait_ge(v_ones, 1)
                    dst = vaug_sa[:, 4 * i:4 * i + 4, 0:H * VW].rearrange("k b (h c) -> k b h c", c=VW)[:, :, :, 0:DH]
                    nc.scalar.activation(dst, ST[0:L, 0, i].rearrange("k (b h c) -> k b h c", b=4, c=DH),
                                         ACT.Copy).then_inc(sa_v_evac, 1)

            def evac_xT(n, thirds=range(3)):
                for i in thirds:
                    act.wait_ge(xt_full, n.count(3, i + 1))
                    if i == 0 and (n.it is not None or n.c >= 2):
                        act.wait_ge(vp_full, (n + -2).count(3, 3))
                    nc.scalar.activation(xT[n.par][:, THIRD * i:THIRD * (i + 1)], MI[:, 0:THIRD], ACT.Identity,
                                         bias=ln_vec(LN_CAKV, 1), scale=ln_vec(LN_CAKV, 0)).then_inc(xt_evac, 1)

            def evac_k(n, i):
                act.wait_ge(kp_full, n.count(3, i + 1))
                if i == 0:
                    for half in range(2):
                        wait(act, kst_loaded[half][n.par], n.par_count(16 * TERMS, 0))
                wait(act, kr_done, n.count(3, i - 2))
                c = slice(THIRD * i, THIRD * (i + 1))
                nc.scalar.activation(kf[:, c], MI[:, 0:THIRD], ACT.Identity, bias=bias_k(n.s + 1)).then_inc(k_evac, 1)
                nc.scalar.activation(ksplit[n.par][:, 0, c], MI[:, 0:THIRD], ACT.Identity,
                                     bias=bias_k(n.s + 1)).then_inc(k_evac, 1)

            def evac_v(n, i):
                act.wait_ge(vp_full, n.count(3, i + 1))
                if i == 0:
                    if n.s == 0 and n.it is None and n.c < 2:
                        act.wait_ge(v_ones, 1)
                    else:
                        act.wait_ge(pv_done, (n + -2).count(STEPS, STEPS))
                dst = vaug[n.par][:, CPT * i:CPT * (i + 1), 0:H * VW].rearrange(
                    "k b (h c) -> k b h c", c=VW)[:, :, :, 0:DH]
                nc.scalar.activation(dst, MI[0:KC, :].rearrange("k (b h c) -> k b h c", b=CPT, c=DH),
                                     ACT.Copy).then_inc(v_evac, 1)

            def evac_mx(n, half):
                act.wait_ge(mx_full, n.count(2, half + 1))
                prev = n + -1
                if n.s or n.it is not None or n.c >= 1:
                    act.wait_ge(shift_loaded[half][prev.par], prev.par_count(16, 16))
                nc.scalar.activation(mrow[:, half, :], MX[half], ACT.Copy
                                     ).then_inc(mx_evac, 1)

            def exp_step(n, k):
                act.wait_ge(st_full, n.count(STEPS, k + 1))
                wait(act, pv_done, n.count(STEPS, k - 1))
                nc.scalar.activation(PT[:, k % 2], ST[:, k % 2, :, 0:4 * PC], ACT.Exp, scale=SCALE
                                     ).then_inc(exp_done, 1)

            def evac_po(n):
                act.wait_ge(pv_done, n.count(STEPS, STEPS))
                nc.scalar.activation(po[:], PO[:, 0:2 * PC], ACT.Copy).then_inc(po_evac, 1)

            def evac_on(n):
                act.wait_ge(ld_vec, 64)
                act.wait_ge(ont_full, n.count(1, 1))
                nc.scalar.activation(attnT[:, bass.ds(n.u * L, L)], OT, ACT.Identity,
                                     bias=bias_v(n.s + 1)).then_inc(ont_evac, 1)

            def window(n):
                for k in range(STEPS):
                    if k == 1:
                        evac_mx(n, 1)
                    if k == MX_STEP and (n + 1).exists():
                        evac_mx(n + 1, 0)
                    if k == FORTH_STEP and (n + -1).exists():
                        evac_on(n + -1)
                    exp_step(n, k)
                    if k == 0 and (n + -1).exists():
                        evac_po(n + -1)
                    if 0 <= k - K_STEP < 3 and (n + 2).exists():
                        evac_k(n + 2, k - K_STEP)
                    if 0 <= k - V_STEP < 3 and (n + 1).exists():
                        evac_v(n + 1, k - V_STEP)
                    if 0 <= k - CTX_STEP < 3 and n.s == 0 and (n + 3).exists():
                        evac_xT(n + 3, (k - CTX_STEP,))

            def finish_pass(s):
                last = Unit(s, None, B - 1)
                evac_po(last)
                evac_on(last)

            act.wait_ge(ld_vec, 64)
            act.wait_ge(sa_kp_full, 1)
            nc.scalar.activation(k_sa[:], PO[:, 0:N], ACT.Identity, bias=bias_k(0)).then_inc(sa_k, 1)
            evac_sa_v()
            u0, u1 = Unit(0, None, 0), Unit(0, None, 1)

            def evac_piece(kind, unit, third):
                n = Unit(0, None, unit)
                if kind == "t":
                    evac_xT(n, (third,))
                elif kind == "k":
                    evac_k(n, third)
                else:
                    evac_v(n, third)

            for i in range(SA_STEPS):
                pieces = SA_PIECES.get(i, ())
                if pieces:
                    evac_piece(*pieces[0])
                if 0 <= i - 4 < B:
                    b = i - 4
                    act.wait_ge(sa_ont, b + 1)
                    nc.scalar.activation(attnT[:, L * b:L * (b + 1)], ST[:, (i - 1) % 2, 1, 4 * PC:4 * PC + L],
                                         ACT.Identity, bias=bias_v(0)).then_inc(sa_att, 1)
                if 0 <= i - 1 < B:
                    b = i - 1
                    act.wait_ge(sa_tp_full, b + 1)
                    wait(act, sa_pv, b - 1)
                    nc.scalar.activation(PT[0:L, b % 2], ST[0:L, b % 2, :, 0:4 * PC], ACT.Copy).then_inc(sa_pt, 1)
                if i < B:
                    act.wait_ge(sa_sub, i + 1)
                    nc.scalar.activation(p_sa[:, i % 2], p_sa[:, i % 2], ACT.Exp, scale=SCALE).then_inc(sa_exp, 1)
                if 0 <= i - 2 < B:
                    b = i - 2
                    act.wait_ge(sa_pv, b + 1)
                    wait(act, sa_pot, b)
                    nc.scalar.activation(po[:], PO[:, 0:2 * PC], ACT.Copy).then_inc(sa_po, 1)
                if len(pieces) > 1:
                    evac_piece(*pieces[1])
            evac_xT(u0 + 2)
            for i in range(3):
                evac_k(u1, i)
            evac_mx(u0, 0)
            run_windows(act, 0, window)
            finish_pass(0)

            v0 = Unit(1, None, 0)
            for i in range(3):
                evac_k(v0, i)
            act.wait_ge(gexp_in, 1)
            nc.scalar.activation(gates[:], lg[:], ACT.Exp).then_inc(gexp_done, 1)

            def gelus(it):
                for i in range(2 * CPE):
                    act.wait_ge(ld_vec, 64)
                    act.wait_ge(fc1_full, it * (2 * CPE) + (i + 1))
                    if not isinstance(it, int) or i >= CPE:
                        act.wait_ge(fc2_step, it * (2 * CPE) + (i + 1 - CPE))
                    c = i % CPE
                    nc.scalar.activation(h1[:, c], ST[:, c // 2, c % 2, 0:N], ACT.Gelu,
                                         bias=vec[:, bass.ds(it * (2 * CPE) + (B1_AT + i), 1)]).then_inc(gelu_done, 1)
            gelus(0)
            with act.Fori(1, E // 2) as it:
                gelus(it)
            for i in range(3):
                evac_v(v0, i)
            for i in range(3):
                evac_k(v0 + 1, i)
            evac_mx(v0, 0)
            run_windows(act, 1, window)
            finish_pass(1)

        @block.vector
        def _(dve):
            def token_ln(n):
                if n == 0:
                    dve.wait_ge(ld_x, 32)
                elif n == 3:
                    dve.wait_ge(expert_added, E)
                else:
                    dve.wait_ge(x_added, n)
                for t in range(TT):
                    last = nc.vector.bn_stats(xstat[:, t], xt[:, t])
                last.then_inc(xstat_ready, 1)
                dve.wait_ge(xstat_ready, n + 1)
                for t in range(TT):
                    last = nc.vector.bn_aggr(xmv[:, t], xstat[:, t])
                last.then_inc(xmv_ready, 1)
                dve.wait_ge(xmv_ready, n + 1)
                nc.vector.tensor_scalar(xvar[:], xmv[:, :, 1], EPS, None, ALU.add).then_inc(xvar_ready, 1)
                dve.wait_ge(xrstd_ready, n + 1)
                for t in range(TT):
                    last = nc.vector.tensor_scalar(xn[:, t], xt[:, t], xmv[:, t, 0:1], xrstd[:, t:t + 1],
                                                   ALU.subtract, ALU.mult)
                last.then_inc(xn_ready, 1)

            def token_gain(n):
                dve.wait_ge(lnt_full, n + 1)
                if n == 0:
                    dve.wait_ge(ld_vec, 64)
                nc.vector.tensor_scalar(hT[:], MI[:, 0:N], ln_vec(X_LN[n], 0), ln_vec(X_LN[n], 1),
                                        ALU.mult, ALU.add).then_inc(hT_ready, 1)

            def split_q(n):
                dve.wait_ge(qp_full, n + 1)
                if n:
                    dve.wait_ge(qall_loaded, 16 * TERMS * n)
                nc.vector.tensor_scalar(qf[:], MI[:, 0:N], bias_q(n + 1), None, ALU.add).then_inc(qf_ready, 1)
                nc.vector.tensor_scalar(qsplit[:, 0], MI[:, 0:N], bias_q(n + 1), None, ALU.add).then_inc(qp_read, 1)
                dve.wait_ge(qf_ready, n + 1)
                dve.wait_ge(qp_read, n + 1)
                nc.vector.tensor_tensor(qr[:], qf[:], qsplit[:, 0], ALU.subtract).then_inc(qr_ready, 1)
                dve.wait_ge(qr_ready, n + 1)
                nc.vector.tensor_copy(qsplit[:, 1], qr[:]).then_inc(q2_ready, 1)
                dve.wait_ge(q2_ready, n + 1)
                nc.vector.tensor_tensor(qsplit[:, 2], qr[:], qsplit[:, 1], ALU.subtract).then_inc(qsplit_ready, 1)

            def ctx_stats(n, chunks):
                if chunks[0] == 0:
                    dve.wait_ge(ld_ctx[n.par], n.par_count(16, 16))
                for c in chunks:
                    last = nc.vector.bn_stats(cstat[:, c], cx[n.par][:, c])
                if chunks[-1] == NCH - 1:
                    last.then_inc(cstat_ready, 1)

            def ctx_aggregate(n):
                for c in range(NCH):
                    last = nc.vector.bn_aggr(cmv[:, c], cstat[:, c])
                last.then_inc(cmv_ready, 1)
                dve.wait_ge(cmv_ready, n.count(1, 1))
                nc.vector.tensor_scalar(cvar[:], cmv[:, :, 1], EPS, None, ALU.add).then_inc(cvar_ready, 1)

            def ctx_normalise(n, thirds=range(3)):
                dve.wait_ge(crstd_ready, n.count(1, 1))
                for i in thirds:
                    for c in range(CPT * i, CPT * (i + 1)):
                        last = nc.vector.tensor_scalar(cx[n.par][:, c], cx[n.par][:, c], cmv[:, c, 0:1],
                                                       crstd[:, c:c + 1], ALU.subtract, ALU.mult)
                    last.then_inc(cn_ready, 1)

            def k_second_part(n, i):
                dve.wait_ge(kr_done, n.count(3, i + 1))
                c = slice(THIRD * i, THIRD * (i + 1))
                nc.vector.tensor_copy(ksplit[n.par][:, 1, c], kr[:, c]).then_inc(k2_done, 1)

            def reduce_tile(n, j, banks=2):
                dve.wait_ge(sm_full, n.count(TILES, j + 1))
                nc.vector.tensor_reduce(mxp[:, j // 3, j % 3:j % 3 + 1], tile_bank(j, banks), AX.X,
                                        ALU.max).then_inc(sm_red, 1)

            def max_parts(n, half):
                dve.wait_ge(sm_red, n.count(TILES, TILES // 2 * (half + 1)))
                nc.vector.tensor_reduce(nmx[:], mxp[:, 4 * half:4 * half + 4], AX.X, ALU.max, negate=True
                                        ).then_inc(nmx_ready, 1)
                wait(dve, mx_full, n.count(2, half))
                dve.wait_ge(nmx_ready, n.count(2, half + 1))
                nc.vector.tensor_copy(mparts[:, 0], nmx[:]).then_inc(m1_ready, 1)
                dve.wait_ge(m1_ready, n.count(2, half + 1))
                nc.vector.tensor_tensor(mparts[:, 1], nmx[:], mparts[:, 0], ALU.subtract).then_inc(mparts_ready, 1)

            def place_q(n):
                if n.s == 0 and n.it is None and n.c == 0:
                    dve.wait_ge(qall_loaded, 16 * TERMS)
                if n.s == 1 and n.it is None and n.c == 0:
                    dve.wait_ge(qall_loaded, 16 * TERMS * 2)
                if n.s or n.it is not None or n.c >= 2:
                    dve.wait_ge(st_full, (n + -2).count(STEPS, STEPS))
                for hh in range(2):
                    last = nc.vector.tensor_scalar(
                        qst[n.par][0:SROWS, :, L * hh:L * (hh + 1)], qall[:, :, bass.ds(n.u * L, L)],
                        mask[0:SROWS, H + hh:H + hh + 1], None, ALU.mult)
                last.then_inc(qst_ready, 1)

            def normalise(bank, full, rden_sem, done, full_at, rden_at, par):
                dve.wait_ge(full, full_at)
                heads = bank[0:L].rearrange("q (h x) -> q h x", x=32)
                nc.vector.reciprocal(rden[:], heads[:, :, DH]).then_inc(rden_sem, 1)
                dve.wait_ge(rden_sem, rden_at)
                nc.vector.tensor_tensor(on[:, par], heads[:, :, 0:DH],
                                        rden[:].unsqueeze(2).broadcast_to([L, H, DH]), ALU.mult).then_inc(done, 1)

            def normalise_unit(n):
                normalise(MI, pot_full, rden_ready, norm_done, n.count(1, 1), n.count(1, 1), n.par)

            def add_projection(n):
                dve.wait_ge(op_full, n + 1)
                nc.vector.tensor_tensor(xt[:], xt[:], PO[0:TP, :].rearrange("p (t d) -> p t d", t=TT), ALU.add
                                        ).then_inc(x_proj, 1)
                dve.wait_ge(x_proj, n + 1)
                bo = rows[:, D * n:D * (n + 1)].unsqueeze(1).broadcast_to([TP, TT, D])
                nc.vector.tensor_tensor(xt[:], xt[:], bo, ALU.add).then_inc(x_added, 1)

            def window(n):
                nxt, k_unit = n + 1, n + 2
                ln_unit = n + 3 if n.s == 0 and (n + 3).exists() else None
                if not nxt.exists():
                    max_parts(n, 1)
                for k in range(STEPS):
                    if nxt.exists():
                        first, rest = STEP_TILES[k][0], STEP_TILES[k][1:]
                        if k == 5 and ln_unit is not None:
                            dve.wait_ge(cstat_ready, ln_unit.count(1, 1))
                        reduce_tile(nxt, first)
                        if k == 0:
                            max_parts(n, 1)
                    if k == BACK_STEP and (n + -1).exists():
                        normalise_unit(n + -1)
                    if nxt.exists():
                        if k == STEPS - 1 and k_unit.exists():
                            place_q(k_unit)
                        for j in rest:
                            reduce_tile(nxt, j)
                        if TILES // 2 - 1 in STEP_TILES[k]:
                            max_parts(nxt, 0)
                    if 0 <= k - K_STEP - 1 < 3 and k_unit.exists():
                        k_second_part(k_unit, k - K_STEP - 1)
                    if ln_unit is not None:
                        if k in (1, 2, 3, 4):
                            ctx_stats(ln_unit, range(3 * (k - 1), 3 * k))
                        if k == 5:
                            ctx_aggregate(ln_unit)
                        if k in (7, 8, 9):
                            ctx_normalise(ln_unit, (k - 7,))

            every = range(NCH)
            u0, u1 = Unit(0, None, 0), Unit(0, None, 1)
            for buf in (vaug_sa, vaug[0], vaug[1]):
                last = nc.vector.memset(buf[:], 1.0)
            last.then_inc(v_ones, 1)
            token_ln(0)
            ctx_stats(u0, every)
            token_gain(0)
            nc.vector.tensor_copy(identb[:], ident[:]).then_inc(identb_ready, 1)
            dve.wait_ge(ld_mask, 16)
            dve.wait_ge(sa_qp_full, 1)
            nc.vector.tensor_scalar(q_sa[:], MI[:, 0:N], bias_q(0), None, ALU.add).then_inc(sa_q, 1)
            dve.wait_ge(cstat_ready, u0.count(1, 1))
            ctx_aggregate(u0)
            nc.vector.tensor_reduce(wabs[:], watt[:, 2], AX.X, ALU.add, apply_absolute_value=True
                                    ).then_inc(wabs_ready, 1)
            for i in range(SA_STEPS):
                if i < B:
                    dve.wait_ge(sa_sm_full, i + 1)
                    wait(dve, sa_sub, i)
                    scores = SM[0:PC, 0, 0:N].rearrange("q (p k) -> q p k", p=PAIRS)
                    nc.vector.tensor_reduce(nmx_sa[:], scores, AX.X, ALU.max, negate=True).then_inc(sa_max, 1)
                    dve.wait_ge(sa_max, i + 1)
                    wait(dve, sa_tp_full, i - 1)
                    nc.vector.tensor_tensor(p_sa[:, i % 2], scores,
                                            nmx_sa[:].unsqueeze(2).broadcast_to([PC, PAIRS, L]), ALU.add
                                            ).then_inc(sa_sub, 1)
                if 0 <= i - 3 < B:
                    normalise(SM[:, 1], sa_pot, sa_rden, sa_norm, i - 2, i - 2, (i - 3) % 2)
                for kind, unit, third in SA_PIECES.get(i - 2, ()):
                    if kind == "k":
                        k_second_part(u0, third)
                if i == 0:
                    dve.wait_ge(gam_full, 1)
                    nc.vector.tensor_copy(gam[:], MI[:, 0:4]).then_inc(gam_ready, 1)
                    ctx_normalise(u0, (0, 1))
                if i == 1:
                    ctx_normalise(u0, (2,))
                    ctx_stats(u1, every)
                if i == 2:
                    dve.wait_ge(cstat_ready, u1.count(1, 1))
                    ctx_aggregate(u1)
                if i == 4:
                    ctx_normalise(u1, (0,))
                if i == 5:
                    ctx_normalise(u1, (1, 2))
                if i == 6:
                    ctx_stats(u0 + 2, every)
                if i == 7:
                    dve.wait_ge(cstat_ready, (u0 + 2).count(1, 1))
                    ctx_aggregate(u0 + 2)
                if i in (9, 10, 11):
                    ctx_normalise(u0 + 2, (i - 9,))
            add_projection(0)
            token_ln(1)
            token_gain(1)
            split_q(0)

            dve.wait_ge(gam_ready, 1)
            nc.vector.tensor_scalar(thr[:, 0], gam[:], EPS, 0.5, ALU.add, ALU.mult)
            nc.vector.tensor_scalar(thr[:, 1], gam[:], EPS, -0.5, ALU.add, ALU.mult).then_inc(thr_ready, 1)
            dve.wait_ge(thr_ready, 1)
            for w in range(4):
                nc.vector.tensor_scalar(wt[:, 0, w], watt[:, 2, w], thr[:, 0, w:w + 1], None, ALU.is_gt)
                last = nc.vector.tensor_scalar(wt[:, 1, w], watt[:, 2, w], thr[:, 1, w:w + 1], None, ALU.is_lt)
            last.then_inc(tern1, 1)
            dve.wait_ge(tern1, 1)
            nc.vector.tensor_tensor(wt[:, 0], wt[:, 0], wt[:, 1], ALU.subtract).then_inc(tern2, 1)
            dve.wait_ge(tern2, 1)
            for w in range(4):
                last = nc.vector.scalar_tensor_tensor(out=wt[:, 1, w], in0=wt[:, 0, w], scalar=gam[:, w:w + 1],
                                                      in1=watt[:, 2, w], op0=ALU.mult, op1=ALU.subtract)
            last.then_inc(tern3, 1)
            dve.wait_ge(tern3, 1)
            nc.vector.tensor_tensor(watt[:, 2], watt[:, 2], wt[:, 1], ALU.add).then_inc(wq_ready, 1)

            def start_pass(s):
                first = Unit(s, None, 0)
                place_q(first)
                place_q(first + 1)
                for j in range(TILES):
                    reduce_tile(first, j, banks=4)
                    if j in (1, 4, 7):
                        k_second_part(first + 1, j // 3)
                    if j == TILES // 2 + 1:
                        max_parts(first, 0)

            def finish_pass(s):
                normalise_unit(Unit(s, None, B - 1))
                add_projection(s + 1)

            start_pass(0)
            run_windows(dve, 0, window)
            finish_pass(0)

            v0 = Unit(1, None, 0)
            token_ln(2)
            token_gain(2)
            dve.wait_ge(rt_full, 1)
            rb = rows[:, RB0:RB0 + E].unsqueeze(1).broadcast_to([TP, TT, E])
            nc.vector.tensor_tensor(lg[:], MI[0:TP, 0:TT * E].rearrange("p (t e) -> p t e", t=TT), rb, ALU.add
                                    ).then_inc(lg_ready, 1)
            dve.wait_ge(lg_ready, 1)
            mine = lg[:].unsqueeze(3).broadcast_to([TP, TT, E, E])
            other = lg[:].unsqueeze(2).broadcast_to([TP, TT, E, E])
            tri = rows[:, TRI0:TRI0 + E * E].unsqueeze(1).broadcast_to([TP, TT, E * E])
            nc.vector.tensor_tensor(cmp[:, 0], other, mine, ALU.is_gt)
            nc.vector.tensor_tensor(cmp[:, 1], other, mine, ALU.is_equal)
            nc.vector.tensor_reduce(top[:, 0], lg[:], AX.X, ALU.max).then_inc(cmp_ready, 1)
            dve.wait_ge(cmp_ready, 1)
            eq = cmp[:, 1].rearrange("p t e f -> p t (e f)")
            nc.vector.tensor_tensor(eq, eq, tri, ALU.mult).then_inc(cmp_ready, 1)
            dve.wait_ge(cmp_ready, 2)
            both = cmp[:, 0].rearrange("p t e f -> p t (e f)")
            nc.vector.tensor_tensor(both, both, eq, ALU.add).then_inc(cmp_ready, 1)
            dve.wait_ge(cmp_ready, 3)
            nc.vector.tensor_reduce(rank[:], cmp[:, 0], AX.X, ALU.add)
            nc.vector.tensor_tensor(lg[:], lg[:], top[:, 0].unsqueeze(2).broadcast_to([TP, TT, E]), ALU.subtract
                                    ).then_inc(gexp_in, 1)
            dve.wait_ge(gexp_in, 1)
            nc.vector.tensor_scalar(rank[:], rank[:], 1.5, None, ALU.is_lt).then_inc(rank_ready, 1)
            dve.wait_ge(gexp_done, 1)
            dve.wait_ge(rank_ready, 1)
            nc.vector.tensor_tensor(gates[:], gates[:], rank[:], ALU.mult).then_inc(gate_step, 1)
            dve.wait_ge(gate_step, 1)
            nc.vector.tensor_reduce(top[:, 1], gates[:], AX.X, ALU.add).then_inc(gate_step, 1)
            dve.wait_ge(gate_step, 2)
            nc.vector.reciprocal(top[:, 2], top[:, 1]).then_inc(gate_step, 1)
            dve.wait_ge(gate_step, 3)
            nc.vector.tensor_tensor(gates[:], gates[:], top[:, 2].unsqueeze(2).broadcast_to([TP, TT, E]), ALU.mult
                                    ).then_inc(gates_ready, 1)
            for i in range(3):
                k_second_part(v0, i)

            def add_experts(it):
                for j in range(2):
                    dve.wait_ge(fc2_step, it * (2 * CPE) + (j + 1) * CPE)
                    wait(dve, expert_added, it * 2 + j)
                    for t in range(TT):
                        last = nc.vector.scalar_tensor_tensor(
                            out=xt[:, t], in0=SM[0:TP, j, D * t:D * (t + 1)], scalar=gates[:, t, bass.ds(it * 2 + j, 1)],
                            in1=xt[:, t], op0=ALU.mult, op1=ALU.add)
                    last.then_inc(expert_added, 1)
            add_experts(0)
            dve.wait_ge(gt_full, 1)
            nc.vector.tensor_copy(gT[:], MI[0:E, 0:N]).then_inc(gT_ready, 1)
            dve.wait_ge(b2_full, 1)
            dve.wait_ge(expert_added, 2)
            nc.vector.tensor_tensor(xt[:], xt[:], MI[0:TP, :].rearrange("p (t d) -> p t d", t=TT), ALU.add
                                    ).then_inc(b2_added, 1)
            dve.wait_ge(b2_added, 1)
            with dve.Fori(1, E // 2) as it:
                add_experts(it)
            token_ln(3)
            token_gain(3)
            split_q(1)
            start_pass(1)
            run_windows(dve, 1, window)
            finish_pass(1)

        @block.tensor
        def _(pe):
            mm = nc.tensor.matmul

            def misc_free(prev):
                if prev is not None:
                    pe.wait_ge(*prev)

            def transpose_tokens(n, prev):
                misc_free(prev)
                pe.wait_ge(xn_ready, n + 1)
                for t in range(TT):
                    last = nc.tensor.transpose(MI[:, TP * t:TP * (t + 1)], xn[:, t], ident[0:TP, 0:TP])
                last.then_inc(lnt_full, 1)
                return hT_ready, n + 1

            def project_q(n, ln):
                pe.wait_ge(hT_ready, ln + 1)
                mm(MI[:, 0:N], watt[:, n + 1, 0], hT[:], start=True, stop=True).then_inc(qp_full, 1)
                return qp_read, n + 1

            def project_out(n, done):
                pe.wait_ge(*done)
                for t in range(TT):
                    last = mm(PO[0:TP, D * t:D * (t + 1)], attnT[:, TP * t:TP * (t + 1)], watt[:, n, 3],
                              start=True, stop=True)
                last.then_inc(op_full, 1)

            def transpose_ctx(n, i, prev):
                misc_free(prev)
                pe.wait_ge(cn_ready, n.count(3, i + 1))
                for c in range(CPT):
                    last = nc.tensor.transpose(MI[:, KC * c:KC * (c + 1)], cx[n.par][:, CPT * i + c],
                                               ident[0:KC, 0:KC])
                last.then_inc(xt_full, 1)
                return xt_evac, n.count(3, i + 1)

            def project_k(n, i, prev):
                misc_free(prev)
                if n.s == 0:
                    pe.wait_ge(xt_evac, n.count(3, i + 1))
                else:
                    pe.wait_ge(ld_xT[n.par], n.pass_par_count(16, 16))
                mm(MI[:, 0:THIRD], watt[:, n.s + 1, 1], xT[n.par][:, THIRD * i:THIRD * (i + 1)],
                   start=True, stop=True).then_inc(kp_full, 1)
                return k_evac, n.count(6, 2 * i + 2)

            def project_v(n, i, prev):
                misc_free(prev)
                if i == 0 and n.s == 0:
                    pe.wait_ge(xt_evac, n.count(3, 3))
                for c in range(CPT):
                    at = KC * (CPT * i + c)
                    last = mm(MI[0:KC, D * c:D * (c + 1)], xT[n.par][:, at:at + KC], watt[:, n.s + 1, 2],
                              start=True, stop=True)
                last.then_inc(vp_full, 1)
                return v_evac, n.count(3, i + 1)

            def transpose_max(n, half):
                pe.wait_ge(mparts_ready, n.count(2, half + 1))
                nc.tensor.transpose(MX[half], mparts[:].rearrange("q m p -> q (m p)"),
                                    identb[0:PC, 0:PC]).then_inc(mx_full, 1)

            def transpose_po(bank):
                for half in range(2):
                    for hh in range(2):
                        at = 256 * half + (128 - VW) * hh
                        last = mm(bank[0:L, at:at + 128], po[:, PC * half + L * hh:PC * half + L * (hh + 1)],
                                  ident[:], start=True, stop=True, skip_group_check=True)
                return last

            def output_back(n, prev):
                misc_free(prev)
                pe.wait_ge(po_evac, n.count(1, 1))
                transpose_po(MI).then_inc(pot_full, 1)
                return norm_done, n.count(1, 1)

            def output_forth(n):
                pe.wait_ge(norm_done, n.count(1, 1))
                mm(OT, on[:, n.par].rearrange("q h d -> q (h d)"), ident[0:L, 0:L], start=True, stop=True
                   ).then_inc(ont_full, 1)

            def scores(n, k):
                half = k // HSTEP
                if k % HSTEP == 0:
                    pe.wait_ge(shift_loaded[half][n.par], n.par_count(16, 16))
                wait(pe, exp_done, n.count(STEPS, k - 1))
                for cc in range(2):
                    at = KC * (2 * (k % HSTEP) + cc)
                    for p in range(4):
                        last = mm(ST[:, k % 2, cc, PC * p:PC * (p + 1)], kst[n.par][:, 4 * half + p, at:at + 128],
                                  qst[n.par][:, 4 * half + p], start=True, stop=True)
                last.then_inc(st_full, 1)
                if k == 1:
                    transpose_max(n, 1)
                if k == MX_STEP and (n + 1).exists():
                    transpose_max(n + 1, 0)
                if k == FORTH_STEP and (n + -1).exists():
                    output_forth(n + -1)

            def max_tile(n, j, banks=2):
                if j == 0:
                    pe.wait_ge(qst_ready, n.count(1, 1))
                    pe.wait_ge(kst_loaded[0][n.par], n.par_count(16 * TERMS, 16 * TERMS))
                if j == TILES // 2:
                    pe.wait_ge(kst_loaded[1][n.par], n.par_count(16 * TERMS, 16 * TERMS))
                wait(pe, sm_red, n.count(TILES, j + 1 - banks))
                at = THIRD * (j % 3)
                mm(tile_bank(j, banks), qst[n.par][0:SROWS, j // 3], kst[n.par][0:SROWS, j // 3, at:at + THIRD],
                   start=True, stop=True).then_inc(sm_full, 1)

            def values(n, k):
                half = k // HSTEP
                pe.wait_ge(exp_done, n.count(STEPS, k + 1))
                if k == 0:
                    wait(pe, po_evac, n.count(1, 0))
                if k < HSTEP:
                    pe.wait_ge(v_evac, n.count(3, (2 * k + 1) // CPT + 1))
                for cc in range(2):
                    c = 2 * (k % HSTEP) + cc
                    for p in range(4):
                        at = 2 * VW * (4 * half + p)
                        last = mm(PO[32 * p:32 * p + 32, PC * half:PC * (half + 1)], vaug[n.par][:, c, at:at + 32],
                                  PT[0:KC, k % 2, cc, PC * p:PC * (p + 1)], start=(k == 0 and cc == 0),
                                  stop=(k % HSTEP == HSTEP - 1 and cc == 1), skip_group_check=True)
                last.then_inc(pv_done, 1)

            def window(n):
                nxt, k_unit, prv = n + 1, n + 2, n + -1
                ln_unit = n + 3 if n.s == 0 and (n + 3).exists() else None
                if not prv.exists():
                    prev = (k_evac, nxt.count(6, 6))
                elif n.s == 0 and k_unit.exists():
                    prev = (xt_evac, k_unit.count(3, 3))
                else:
                    prev = (v_evac, n.count(3, 3))
                for k in range(STEPS):
                    scores(n, k)
                    tiles = list(STEP_TILES[k]) if nxt.exists() else []
                    if tiles:
                        max_tile(nxt, tiles[0])
                    if k:
                        values(n, k - 1)
                    elif prv.exists():
                        values(prv, STEPS - 1)
                    for j in tiles[1:-1]:
                        max_tile(nxt, j)
                    if 0 <= k - K_STEP < 3 and k_unit.exists():
                        prev = project_k(k_unit, k - K_STEP, prev)
                    if k == BACK_STEP and prv.exists():
                        prev = output_back(prv, prev)
                    if 0 <= k - V_STEP < 3 and nxt.exists():
                        prev = project_v(nxt, k - V_STEP, prev)
                    if 0 <= k - CTX_STEP < 3 and ln_unit is not None:
                        prev = transpose_ctx(ln_unit, k - CTX_STEP, prev)
                    if len(tiles) > 1:
                        max_tile(nxt, tiles[-1])
                return prev

            u0, u1 = Unit(0, None, 0), Unit(0, None, 1)
            pe.wait_ge(ld_x, 32)
            prev = transpose_tokens(0, None)
            pe.wait_ge(ld_w, 16)
            pe.wait_ge(hT_ready, 1)
            mm(MI[:, 0:N], watt[:, 0, 0], hT[:], start=True, stop=True).then_inc(sa_qp_full, 1)
            mm(PO[:, 0:N], watt[:, 0, 1], hT[:], start=True, stop=True).then_inc(sa_kp_full, 1)
            for i in range(2):
                for c in range(4):
                    b = 4 * i + c
                    last = mm(ST[0:L, 0, i, D * c:D * (c + 1)], hT[:, L * b:L * (b + 1)], watt[:, 0, 2],
                              start=True, stop=True)
                last.then_inc(sa_vp_full, 1)
            pe.wait_ge(sa_q, 1)
            pe.wait_ge(wabs_ready, 1)
            pe.wait_ge(padded, 1)
            mm(MI[:, 0:4], mean_w[:], wabs[:], start=True, stop=True).then_inc(gam_full, 1)
            prev = (gam_ready, 1)

            def piece(kind, unit, third, prev):
                n = Unit(0, None, unit)
                if kind == "t":
                    return transpose_ctx(n, third, prev)
                if kind == "k":
                    return project_k(n, third, prev)
                return project_v(n, third, prev)

            for i in range(SA_STEPS):
                pieces = SA_PIECES.get(i, ())
                if i < B:
                    pe.wait_ge(sa_qbd, i + 1)
                    if i == 0:
                        pe.wait_ge(sa_k, 1)
                    wait(pe, sa_sub, i)
                    for p in range(PAIRS):
                        last = mm(SM[0:PC, 0, L * p:L * (p + 1)],
                                  qbd[:, i % 2, 2 * p:2 * p + 2].rearrange("n h q -> n (h q)"),
                                  k_sa[:, L * i:L * (i + 1)], start=True, stop=True)
                    last.then_inc(sa_sm_full, 1)
                if pieces:
                    prev = piece(*pieces[0], prev)
                if 0 <= i - 1 < B:
                    b = i - 1
                    pe.wait_ge(sa_exp, b + 1)
                    if b == 0:
                        pe.wait_ge(sa_v_evac, 2)
                    wait(pe, sa_pt, b - 1)
                    for p in range(PAIRS):
                        last = nc.tensor.transpose(ST[0:L, b % 2, p // 4, PC * (p % 4):PC * (p % 4 + 1)],
                                                   p_sa[:, b % 2, p], ident[0:PC, 0:PC])
                    last.then_inc(sa_tp_full, 1)
                if 0 <= i - 4 < B:
                    b = i - 4
                    pe.wait_ge(sa_norm, b + 1)
                    if i - 1 >= B:
                        pe.wait_ge(sa_pt, min(i - 2, B))
                        pe.wait_ge(sa_att, b - 1)
                    nc.tensor.transpose(ST[:, (i - 1) % 2, 1, 4 * PC:4 * PC + L],
                                        on[:, b % 2].rearrange("q h d -> q (h d)"), ident[0:L, 0:L]
                                        ).then_inc(sa_ont, 1)
                if 0 <= i - 2 < B:
                    b = i - 2
                    pe.wait_ge(sa_pt, b + 1)
                    if b == 0:
                        pe.wait_ge(sa_k, 1)
                    wait(pe, sa_po, b)
                    for p in range(PAIRS):
                        half, q = p // 4, p % 4
                        last = mm(PO[32 * q:32 * q + 32, PC * half:PC * (half + 1)],
                                  vaug_sa[:, b, 2 * VW * p:2 * VW * p + 32],
                                  PT[0:L, b % 2, half, PC * q:PC * (q + 1)], start=(half == 0), stop=True,
                                  skip_group_check=True)
                    last.then_inc(sa_pv, 1)
                if len(pieces) > 1:
                    prev = piece(*pieces[1], prev)
                if 0 <= i - 3 < B:
                    b = i - 3
                    pe.wait_ge(sa_po, b + 1)
                    wait(pe, sa_norm, b)
                    transpose_po(SM[:, 1]).then_inc(sa_pot, 1)
            project_out(0, (sa_att, B))
            for i in range(3):
                prev = transpose_ctx(u0 + 2, i, prev)
            prev = transpose_tokens(1, prev)
            pe.wait_ge(padded, 1)
            pe.wait_ge(ld_ones, 32)
            prev = project_q(0, 1)
            for i in range(3):
                prev = project_k(u1, i, prev)

            def start_pass(s):
                first = Unit(s, None, 0)
                for j in range(TILES):
                    max_tile(first, j, banks=4)
                    if j == TILES // 2 + 4:
                        transpose_max(first, 0)

            def finish_pass(s):
                last = Unit(s, None, B - 1)
                values(last, STEPS - 1)
                prev = output_back(last, (v_evac, last.count(3, 3)))
                output_forth(last)
                return prev

            start_pass(0)
            run_windows(pe, 0, window)
            prev = finish_pass(0)
            project_out(1, (ont_evac, B))

            v0 = Unit(1, None, 0)
            pe.wait_ge(wq_ready, 1)
            for i in range(3):
                prev = project_k(v0, i, prev)
            prev = transpose_tokens(2, prev)
            misc_free(prev)
            for t in range(TT):
                last = mm(MI[0:TP, E * t:E * (t + 1)], hT[:, TP * t:TP * (t + 1)], rwT[:], start=True, stop=True)
            last.then_inc(rt_full, 1)
            prev = (lg_ready, 1)

            def experts(it):
                def fc1(i):
                    j, c = i // CPE, i % CPE
                    if c == 0:
                        pe.wait_ge(ld_exp[j], it * 32 + 32)
                    if not isinstance(it, int) or i >= CPE:
                        pe.wait_ge(gelu_done, it * (2 * CPE) + (i + 1 - CPE))
                    mm(ST[:, c // 2, c % 2, 0:N], w1s[j][:, D * c:D * (c + 1)], hT[:], start=True, stop=True
                       ).then_inc(fc1_full, 1)

                def fc2(i):
                    j, c = i // CPE, i % CPE
                    pe.wait_ge(gelu_done, it * (2 * CPE) + (i + 1))
                    if c == 0 and not isinstance(it, int):
                        pe.wait_ge(expert_added, it * 2 + (j - 1))
                    for t in range(TT):
                        last = mm(SM[0:TP, j, D * t:D * (t + 1)], h1[:, c, TP * t:TP * (t + 1)], w2s[j][:, c],
                                  start=(c == 0 and t == 0), stop=(c == CPE - 1), skip_group_check=True)
                    last.then_inc(fc2_step, 1)
                fc1(0)
                for i in range(2 * CPE):
                    if i + 1 < 2 * CPE:
                        fc1(i + 1)
                    fc2(i)
            experts(0)
            misc_free(prev)
            pe.wait_ge(gates_ready, 1)
            for t in range(TT):
                last = nc.tensor.transpose(MI[0:E, TP * t:TP * (t + 1)], gates[:, t], ident[0:TP, 0:TP])
            last.then_inc(gt_full, 1)
            pe.wait_ge(gT_ready, 1)
            for t in range(TT):
                last = mm(MI[0:TP, D * t:D * (t + 1)], gT[:, TP * t:TP * (t + 1)], b2[:], start=True, stop=True)
            last.then_inc(b2_full, 1)
            with pe.Fori(1, E // 2) as it:
                experts(it)
            prev = (b2_added, 1)
            for i in range(3):
                prev = project_v(v0, i, prev)
            prev = transpose_tokens(3, prev)
            prev = project_q(1, 3)
            for i in range(3):
                prev = project_k(v0 + 1, i, prev)
            start_pass(1)
            run_windows(pe, 1, window)
            prev = finish_pass(1)
            project_out(2, (ont_evac, 2 * B))


def _orders():
    n = np.arange(D)
    q_order = (n % PAIRS) * PR + n // PAIRS
    k_order = ((n // 64) * 4 + n % 4) * PR + n % 64 // 4
    half, member, pair, dim = n // 64, n // 32 % 2, n // 8 % 4, n % 8
    o_order = (8 * half + 2 * pair + member) * DH + dim
    return q_order, k_order, o_order


def kernel(**inputs):
    import concourse.bacc as _bacc
    from concourse.bass_utils import run_bass_kernel_spmd as _run

    a = {k: np.asarray(v) for k, v in inputs.items()}
    q_order, k_order, o_order = _orders()
    n = np.arange(D)

    def attention(wq, wk, wv, wo, k_order):
        return np.stack([wq.T[:, q_order], wk.T[:, k_order], wv.T, wo.T[o_order]])

    weights, columns = [], []
    for p, order in (("L0_xattn_sa_", q_order), ("L0_xattn_ca_", k_order)):
        w, b = a[p + "in_w"], a[p + "in_b"]
        weights.append(attention(w[:D], w[D:2 * D], w[2 * D:], a[p + "out_w"], order))
        columns += [b[:D][q_order], b[D:2 * D][order], b[2 * D:][o_order]]
    p = "L1_xattn_"
    weights.append(attention(a[p + "Wq"], a[p + "Wk"], a[p + "Wv"], a[p + "Wo"], k_order))
    columns += [a[p + "bq"][q_order], a[p + "bk"][k_order], a[p + "bv"][o_order]]
    for ln in ("L0_xattn_sa_ln_", "L0_xattn_ca_q_ln_", "L0_xattn_ca_kv_ln_", "L0_xattn_moe_ln_"):
        columns += [a[ln + "g"], a[ln + "b"]]
    columns += [a["L1_xattn_ln_gamma"], a["L1_xattn_ln_beta"]]
    columns += list(a["L0_xattn_e_fc1_b"].reshape(E * CPE, D))
    before = np.tril(np.ones((E, E), np.float32), -1)
    arrays = {
        "x": a["x"].reshape(N, D),
        "ctx": a["ctx_1024"],
        "ctxT": a["ctx_1024"].transpose(0, 2, 1),
        "watt": np.stack(weights),
        "vec": np.stack(columns, axis=1),
        "rows": np.concatenate([a["L0_xattn_sa_out_b"], a["L0_xattn_ca_out_b"], a["L1_xattn_bo"],
                                a["L0_xattn_router_b"], before.reshape(-1)]),
        "rwT": a["L0_xattn_router_w"].T,
        "w1T": a["L0_xattn_e_fc1_w"].transpose(0, 2, 1),
        "w2T": a["L0_xattn_e_fc2_w"].transpose(0, 2, 1).reshape(E, CPE, D, D).transpose(0, 2, 1, 3),
        "b2": a["L0_xattn_e_fc2_b"],
        "ident": np.eye(D, dtype=np.float32),
        "mask": np.concatenate([q_order[:, None] // DH == np.arange(H),
                                n[:, None] % PR // DH == np.arange(2)], axis=1).astype(np.float32),
    }
    nc = _bacc.Bacc("TRN2", target_bir_lowering=False, num_devices=1)
    feeds, args = {}, []
    for name, array in arrays.items():
        feeds[f"in_{name}"] = np.ascontiguousarray(array)
        args.append(nc.dram_tensor(f"in_{name}", array.shape, F32, kind="ExternalInput").ap())
    args.append(nc.dram_tensor("out_x", (N, D), F32, kind="ExternalOutput").ap())
    build_kernel(nc, *args)
    result = _run(nc, [feeds], core_ids=[0])
    return result.results[0]["out_x"].reshape(B, L, D)
```

```python
from contextlib import ExitStack

import numpy as np

import concourse.bass as bass
from concourse import mybir

ALU = mybir.AluOpType
ACT = mybir.ActivationFunctionType
AX = mybir.AxisListType
F32 = mybir.dt.float32
BF16 = mybir.dt.bfloat16

B, L, D, T = 8, 56, 128, 1500
H, DH = 16, 8
E, DFF = 8, 512
EPS = 1e-5
N = B * L
TT, TP = 4, 112
PAIRS = H // 2
PR = 2 * DH
K_PART = (0, 0, 0, 1, 1, 2)
Q_PART = (0, 1, 2, 0, 1, 0)
TERMS = len(K_PART)
SROWS = TERMS * PR
MROWS = 2
KROWS = SROWS + MROWS
PC = 2 * L
KC = 125
NCH = T // KC
STEPS = NCH
HSTEP = STEPS // 2
TPAD = KC * (NCH - 1) + 128
THIRD = T // 3
CPT = NCH // 3
VW = 9
VCOLS = 160
SCALE = float(DH) ** -0.5
TILES = PAIRS * 3
CPE = DFF // D
FC1_AHEAD = 2
WB = 3
N_LN = 5
RB0, TRI0 = 3 * D, 3 * D + E


K_STEP, BACK_STEP, V_STEP, FORTH_STEP, CTX_STEP = 0, 3, 4, 7, STEPS - 3
Q2_STEP, Q1_STEP = 1, 10
START_TILES = 18


def spread_tiles(own, per):
    tiles = [(0, j) for j in range(TILES - own, TILES)] + [(1, j) for j in range(TILES)]
    assert sum(per) == len(tiles)
    return [tiles[sum(per[:k]):sum(per[:k + 1])] for k in range(STEPS)]


STEP_TILES = spread_tiles(0, (3, 3, 3, 2, 2, 2, 2, 2, 1, 1, 2, 1))
OWN_MX_STEP, NEXT_MX_STEP = 1, 6
FIRST_TILES = spread_tiles(TILES - START_TILES, (3, 3, 3, 3, 2, 2, 3, 3, 2, 2, 2, 2))
FIRST_OWN_MX_STEP, FIRST_NEXT_MX_STEP = 3, 8


SA_STEPS = B + 4
SA_PIECES = {1: (("t", 0, 0), ("t", 0, 1)), 2: (("t", 0, 2),), 3: (("k", 0, 0),), 4: (("k", 0, 1),),
             5: (("k", 0, 2),), 7: (("t", 1, 0),), 8: (("t", 1, 1),), 9: (("t", 1, 2),)}


class Unit:

    def __init__(self, s, it, c):
        self.s, self.it, self.c = s, it, c
        self.par = c % 2
        self.u = c if it is None else it * 2 + c

    def __add__(self, d):
        return Unit(self.s, self.it, self.c + d)

    def exists(self):
        return self.it is not None or 0 <= self.c < B

    def first(self):
        return self.it is None and self.c == 0

    def tiles(self, k):
        if not (self + 1).exists():
            return []
        return FIRST_TILES[k] if self.first() else STEP_TILES[k]

    def mx_steps(self):
        return (FIRST_OWN_MX_STEP, FIRST_NEXT_MX_STEP) if self.first() else (OWN_MX_STEP, NEXT_MX_STEP)

    def count(self, per, off):
        base = (B * self.s + self.c) * per + off
        return base if self.it is None else self.it * (2 * per) + base

    def pass_par_count(self, per, off):
        base = self.c // 2 * per + off
        return base if self.it is None else self.it * per + base

    def par_count(self, per, off):
        base = (B // 2 * self.s + self.c // 2) * per + off
        return base if self.it is None else self.it * per + base


def wait(eng, sem, value):
    if not isinstance(value, int) or value > 0:
        eng.wait_ge(sem, value)


def run_windows(eng, s, window):
    window(Unit(s, None, 0))
    with eng.Fori(0, 2) as it:
        window(Unit(s, it, 1))
        window(Unit(s, it, 2))
    for u in range(5, B):
        window(Unit(s, None, u))


def build_kernel(nc, x_in, ctx_in, ctxT_in, watt_in, vec_in, rows_in, rwT_in, w1T_in, w2T_in, b2_in,
                 ident_in, mask_in, out):
    with ExitStack() as ctx:
        def sb(name, shape, dt=F32):
            return ctx.enter_context(nc.sbuf_tensor(name, shape, dt))

        def sem(name):
            return ctx.enter_context(nc.semaphore(name))

        ST = ctx.enter_context(nc.psum_tensor("ST", [128, 2, 2, 512], F32))
        SM = ctx.enter_context(nc.psum_tensor("SM", [128, 2, 512], F32))
        PO = ctx.enter_context(nc.psum_tensor("PO", [128, 512], F32))
        MI = ctx.enter_context(nc.psum_tensor("MI", [128, 512], F32))
        MX = [ST[0:MROWS * 4, k % 2, 0, 4 * PC:4 * PC + L].bitcast(BF16) for k in (NEXT_MX_STEP, OWN_MX_STEP)]
        OT = ST[:, FORTH_STEP % 2, 1, 4 * PC:4 * PC + L]

        ident = sb("ident", [128, 128])
        identb = sb("identb", [128, 128], BF16)
        vec = sb("vec", [128, 3 * WB + 2 * N_LN + E * CPE])
        rows = sb("rows", [TP, 3 * D + E + E * E])
        watt = sb("watt", [128, 3, 4, 128])
        rwT = sb("rwT", [128, E])
        b2 = sb("b2", [E, 128])
        xt = sb("xt", [TP, TT, D])
        xn = sb("xn", [TP, TT, D])
        hT = sb("hT", [128, N])
        xstat = sb("xstat", [TP, TT, 6])
        xmv = sb("xmv", [TP, TT, 2])
        xvar = sb("xvar", [TP, TT])
        xrstd = sb("xrstd", [TP, TT])
        half_neg = sb("half_neg", [128, 16])
        euler = sb("euler", [TP, TT, E])
        ones_rows = sb("ones_rows", [MROWS, TPAD], BF16)
        ones_row = sb("ones_row", [1, TP])
        qf = sb("qf", [128, N])
        qr = sb("qr", [128, N])
        qsplit = sb("qsplit", [128, 3, N], BF16)
        qall = sb("qall", [SROWS, PAIRS, N], BF16)
        qst = [sb(f"qst{i}", [KROWS, PAIRS, PC], BF16) for i in range(2)]
        kf = sb("kf", [128, T])
        kr = sb("kr", [128, T])
        ksplit = [sb(f"ksplit{i}", [128, 3, T], BF16) for i in range(2)]
        kst = [sb(f"kst{i}", [KROWS, PAIRS, TPAD], BF16) for i in range(2)]
        cx = [sb(f"cx{i}", [KC, NCH, D]) for i in range(2)]
        cstat = sb("cstat", [KC, NCH, 6])
        cmv = sb("cmv", [KC, NCH, 2])
        cvar = sb("cvar", [KC, NCH])
        crstd = sb("crstd", [KC, NCH])
        xT = [sb(f"xT{i}", [128, T]) for i in range(2)]
        vaug = [sb(f"vaug{i}", [KC, NCH, VCOLS]) for i in range(2)]
        PT = sb("PT", [128, 2, 2, 4 * PC])
        po = sb("po", [128, 2 * PC])
        on = sb("on", [L, 2, H, DH])
        rden = sb("rden", [L, H])
        attnT = sb("attnT", [128, N])
        mxp = sb("mxp", [PC, PAIRS, 3])
        nmx = sb("nmx", [PC, 4])
        mparts = sb("mparts", [PC, MROWS, 4], BF16)
        mrow = sb("mrow", [MROWS * 4, 2, PC], BF16)
        mask = sb("mask", [128, H + 2])
        q_sa, k_sa = qf, qr
        qbd = sb("qbd", [128, 2, H, L])
        p_sa = sb("p_sa", [PC, 2, PAIRS, L])
        vaug_sa = sb("vaug_sa", [L, B, VCOLS])
        nmx_sa = sb("nmx_sa", [PC, PAIRS])
        wabs = sb("wabs", [128, 4])
        mean_w = sb("mean_w", [128, 128])
        gam = sb("gam", [128, 4])
        wt = sb("wt", [128, 2, 4, 128])
        thr = sb("thr", [128, 2, 4])
        lg = sb("lg", [TP, TT, E])
        cmp = qbd[0:TP].rearrange("p s h q -> p (s h q)")[:, 0:2 * TT * E * E].rearrange(
            "p (s t e f) -> p s t e f", s=2, t=TT, e=E)
        rank = sb("rank", [TP, TT, E])
        top = sb("top", [TP, 3, TT])
        gates = sb("gates", [TP, TT, E])
        gT = sb("gT", [E, N])
        moe = sb("moe", [128, 4 * DFF + CPE * N])
        w1s = [moe[:, DFF * i:DFF * (i + 1)] for i in range(2)]
        w2s = [moe[:, DFF * (2 + i):DFF * (3 + i)].rearrange("f (c d) -> f c d", d=D) for i in range(2)]
        h1 = moe[:, 4 * DFF:].rearrange("f (c n) -> f c n", c=CPE)

        K_BANKS = (ST[:, 0, 0], ST[:, 0, 1], MI)

        def tile_bank(j, banks):
            if j % banks < banks - 2:
                return ST[0:PC, 1, j % banks, 0:THIRD]
            return SM[0:PC, j % 2, 0:THIRD]

        def bias_q(layer):
            return vec[:, WB * layer:WB * layer + 1]

        def bias_k(layer):
            return vec[:, WB * layer + 1:WB * layer + 2]

        def bias_v(layer):
            return vec[:, WB * layer + 2:WB * layer + 3]

        def ln_vec(n, which):
            at = 3 * WB + 2 * n + which
            return vec[:, at:at + 1]
        LN_SA, LN_CAQ, LN_CAKV, LN_MOE, LN_L1 = range(N_LN)
        X_LN = (LN_SA, LN_CAQ, LN_MOE, LN_L1)
        B1_AT = 3 * WB + 2 * N_LN

        ld_mask, ld_rows = sem("ld_mask"), sem("ld_rows")
        ld_x, ld_vec, ld_w, ld_ones = sem("ld_x"), sem("ld_vec"), sem("ld_w"), sem("ld_ones")
        ld_ctx = [sem(f"ld_ctx{i}") for i in range(2)]
        ld_xT = [sem(f"ld_xT{i}") for i in range(2)]
        ld_exp = [sem(f"ld_exp{i}") for i in range(2)]
        padded, v_ones = sem("padded"), sem("v_ones")
        identb_ready = sem("identb_ready")
        xstat_ready, xmv_ready, xvar_ready, xrstd_ready, xn_ready = (
            sem("xstat_ready"), sem("xmv_ready"), sem("xvar_ready"), sem("xrstd_ready"), sem("xn_ready"))
        lnt_full, hT_ready, qp_full, qf_ready, q1_ready, qr_ready, q2_ready, q3_ready = (
            sem("lnt_full"), sem("hT_ready"), sem("qp_full"), sem("qf_ready"), sem("q1_ready"),
            sem("qr_ready"), sem("q2_ready"), sem("q3_ready"))
        qall_loaded = sem("qall_loaded")
        op_full, x_added = sem("op_full"), sem("x_added")
        sa_qp_full, sa_q, sa_kp_full, sa_k, sa_qbd, sa_vp_full, sa_v_evac, sa_sm_full, sa_max, sa_sub = (
            sem("sa_qp_full"), sem("sa_q"), sem("sa_kp_full"), sem("sa_k"), sem("sa_qbd"), sem("sa_vp_full"),
            sem("sa_v_evac"), sem("sa_sm_full"), sem("sa_max"), sem("sa_sub"))
        sa_exp, sa_tp_full, sa_pt, sa_pv, sa_po, sa_pot, sa_rden, sa_norm, sa_ont, sa_att = (
            sem("sa_exp"), sem("sa_tp_full"), sem("sa_pt"), sem("sa_pv"), sem("sa_po"), sem("sa_pot"),
            sem("sa_rden"), sem("sa_norm"), sem("sa_ont"), sem("sa_att"))
        wabs_ready, gam_full, gam_ready, thr_ready, tern1, tern2, tern3, wq_ready = (
            sem("wabs_ready"), sem("gam_full"), sem("gam_ready"), sem("thr_ready"), sem("tern1"), sem("tern2"),
            sem("tern3"), sem("wq_ready"))
        cstat_ready, cmv_ready, cvar_ready, crstd_ready, cn_ready = (
            sem("cstat_ready"), sem("cmv_ready"), sem("cvar_ready"), sem("crstd_ready"), sem("cn_ready"))
        xt_full, xt_evac, kp_full, k_evac, kr_done, k2_done, k3_done, vp_full, v_evac = (
            sem("xt_full"), sem("xt_evac"), sem("kp_full"), sem("k_evac"), sem("kr_done"), sem("k2_done"),
            sem("k3_done"), sem("vp_full"), sem("v_evac"))
        kst_loaded = [[sem(f"kst_loaded{h}{p}") for p in range(2)] for h in range(2)]
        qst_ready, sm_full, sm_red, nmx_ready, m1_ready, mparts_ready, mx_full, mx_evac = (
            sem("qst_ready"), sem("sm_full"), sem("sm_red"), sem("nmx_ready"), sem("m1_ready"),
            sem("mparts_ready"), sem("mx_full"), sem("mx_evac"))
        shift_loaded = [[sem(f"shift_loaded{h}{p}") for p in range(2)] for h in range(2)]
        st_full, exp_done, pv_done, po_evac, pot_full, rden_ready, norm_done, ont_full, ont_evac = (
            sem("st_full"), sem("exp_done"), sem("pv_done"), sem("po_evac"), sem("pot_full"),
            sem("rden_ready"), sem("norm_done"), sem("ont_full"), sem("ont_evac"))
        rt_full, lg_ready, cmp_ready, rank_ready, gexp_in, gexp_done, gate_step, gates_ready = (
            sem("rt_full"), sem("lg_ready"), sem("cmp_ready"), sem("rank_ready"),
            sem("gexp_in"), sem("gexp_done"), sem("gate_step"), sem("gates_ready"))
        gt_full, gT_ready, b2_full, b2_added = sem("gt_full"), sem("gT_ready"), sem("b2_full"), sem("b2_added")
        fc1_full, gelu_done, fc2_step, expert_added = (
            sem("fc1_full"), sem("gelu_done"), sem("fc2_step"), sem("expert_added"))
        stored = sem("stored")

        block = ctx.enter_context(nc.Block())

        @block.sync
        def _(sp):
            sp.dma_start(xt[:], x_in.rearrange("(t p) d -> p t d", p=TP)).then_inc(ld_x, 16)
            sp.dma_start(ident[:], ident_in).then_inc(ld_x, 16)
            sp.dma_start(vec[:], vec_in).then_inc(ld_vec, 16)
            sp.dma_start(watt[:], watt_in.rearrange("l w i o -> i l w o")).then_inc(ld_w, 16)

            def load_ctx(n):
                if n.it is not None or n.c >= 2:
                    sp.wait_ge(xt_full, (n + -2).count(3, 3))
                src = ctx_in[bass.ds(n.u, 1)].rearrange("a (p c) d -> (a p) c d", c=NCH)
                sp.dma_start(cx[n.par][:], src).then_inc(ld_ctx[n.par], 16)

            def load_xT(n):
                sp.wait_ge(vp_full, (n + -2).count(3, 3))
                src = ctxT_in[bass.ds(n.u, 1)].rearrange("a d t -> (a d) t")
                sp.dma_start(xT[n.par][:], src).then_inc(ld_xT[n.par], 16)

            sp.dma_start(mask[:], mask_in).then_inc(ld_mask, 16)
            load_ctx(Unit(0, None, 0))
            load_ctx(Unit(0, None, 1))
            sp.dma_start(rows[:], rows_in.partition_broadcast(TP)).then_inc(ld_rows, 16)
            sp.dma_start(rwT[:], rwT_in).then_inc(ld_rows, 16)
            sp.dma_start(b2[:], b2_in).then_inc(ld_rows, 16)

            def load_expert(e, j):
                sp.dma_start(w1s[j], w1T_in[bass.ds(e, 1)].rearrange("a i f -> (a i) f")).then_inc(ld_exp[j], 16)
                sp.dma_start(w2s[j], w2T_in[bass.ds(e, 1)].rearrange("a f c d -> (a f) c d")).then_inc(ld_exp[j], 16)

            def load_qall(n):
                for part, ready in enumerate((q1_ready, q2_ready, q3_ready)):
                    sp.wait_ge(ready, n + 1)
                    for t in range(TERMS):
                        if Q_PART[t] == part:
                            sp.dma_start(qall[t * PR:(t + 1) * PR], qsplit[:, part, :]).then_inc(qall_loaded, 16)

            sp.wait_ge(padded, 1)
            for stack in kst:
                width = stack.shape[2]
                sp.dma_start(stack[SROWS:KROWS], ones_rows[:, 0:width].unsqueeze(1).broadcast_to(
                    [MROWS, PAIRS, width])).then_inc(ld_ones, 16)

            def restack(n, half):
                split = n.count(3, 3) if n.it is None else sp.to_reg(n.count(3, 3))
                if n.s or n.it is not None or n.c >= 2:
                    sp.wait_ge(st_full, (n + -2).count(STEPS, HSTEP * (half + 1)))
                sp.wait_ge(k3_done, split)
                for t in range(TERMS):
                    sp.dma_start(kst[n.par][t * PR:(t + 1) * PR, 4 * half:4 * half + 4, 0:T],
                                 ksplit[n.par][64 * half:64 * half + 64, K_PART[t], :]
                                 ).then_inc(kst_loaded[half][n.par], 16)

            def shift(n, half):
                sp.wait_ge(mx_evac, n.count(2, half + 1))
                sp.dma_start(qst[n.par][SROWS:KROWS, 4 * half:4 * half + 4, :], mrow[:, half, :]
                             ).then_inc(shift_loaded[half][n.par], 16)

            def window(n):
                if n.s == 0 and (n + 3).exists():
                    load_ctx(n + 3)
                if (n + 1).exists():
                    restack(n + 1, 1)
                shift(n, 1)
                if (n + 2).exists():
                    restack(n + 2, 0)
                if (n + 1).exists():
                    shift(n + 1, 0)
                if n.s == 1 and (n + 3).exists():
                    load_xT(n + 3)

            u0, u1 = Unit(0, None, 0), Unit(0, None, 1)
            load_ctx(Unit(0, None, 2))
            restack(u0, 0)
            restack(u0, 1)
            load_expert(0, 0)
            load_expert(1, 1)
            load_qall(0)
            shift(u0, 0)
            restack(u1, 0)
            run_windows(sp, 0, window)
            v0 = Unit(1, None, 0)
            load_xT(v0)
            load_xT(v0 + 1)
            sp.wait_ge(fc2_step, CPE)
            load_expert(2, 0)
            sp.wait_ge(fc2_step, 2 * CPE)
            load_expert(3, 1)
            restack(v0, 0)
            restack(v0, 1)
            with sp.Fori(1, 3) as it:
                for j in range(2):
                    sp.wait_ge(fc2_step, it * (2 * CPE) + (j + 1) * CPE)
                    load_expert(it * 2 + (j + 2), j)
            load_qall(1)
            load_xT(v0 + 2)
            shift(v0, 0)
            restack(v0 + 1, 0)
            run_windows(sp, 1, window)
            sp.wait_ge(x_added, 3)
            sp.dma_start(out.rearrange("(t p) d -> p t d", p=TP), xt[:]).then_inc(stored, 16)
            sp.wait_ge(stored, 16)

        @block.gpsimd
        def _(pool):
            nc.gpsimd.memset(half_neg[:], -0.5)
            nc.gpsimd.memset(euler[:], float(np.e))
            nc.gpsimd.memset(mean_w[:], 1.0 / (D * D))
            nc.gpsimd.memset(ones_rows[:], 1.0)
            nc.gpsimd.memset(ones_row[:], 1.0)
            for s in range(2):
                last = nc.gpsimd.memset(kst[s][0:SROWS, :, T:TPAD], 0.0)
            last.then_inc(padded, 1)

            def spread_q(b):
                pool.wait_ge(sa_q, 1)
                wait(pool, sa_sm_full, b - 1)
                nc.gpsimd.tensor_tensor(
                    qbd[:, b % 2], q_sa[:, L * b:L * (b + 1)].unsqueeze(1).broadcast_to([128, H, L]),
                    mask[:, 0:H].unsqueeze(2).broadcast_to([128, H, L]), ALU.mult).then_inc(sa_qbd, 1)

            def token_rstd(n):
                pool.wait_ge(xvar_ready, n + 1)
                nc.gpsimd.tensor_tensor(xrstd[:], xvar[:], half_neg[0:TP, 0:TT], ALU.pow).then_inc(xrstd_ready, 1)

            def ctx_rstd(n):
                pool.wait_ge(cvar_ready, n.count(1, 1))
                nc.gpsimd.tensor_tensor(crstd[:], cvar[:], half_neg[0:KC, 0:NCH], ALU.pow).then_inc(crstd_ready, 1)

            def k_rest(n, i):
                wait(pool, k3_done, n.count(3, i - 2))
                pool.wait_ge(k_evac, n.count(6, 2 * i + 2))
                c = slice(THIRD * i, THIRD * (i + 1))
                nc.gpsimd.tensor_tensor(kr[:, c], kf[:, c], ksplit[n.par][:, 0, c], ALU.subtract).then_inc(kr_done, 1)

            def k_third_part(n, i):
                pool.wait_ge(k2_done, n.count(3, i + 1))
                c = slice(THIRD * i, THIRD * (i + 1))
                nc.gpsimd.tensor_tensor(ksplit[n.par][:, 2, c], kr[:, c], ksplit[n.par][:, 1, c],
                                        ALU.subtract).then_inc(k3_done, 1)

            def gates_exp():
                pool.wait_ge(gexp_in, 1)
                nc.gpsimd.tensor_tensor(gates[:], euler[:], lg[:], ALU.pow).then_inc(gexp_done, 1)

            def k_parts(n, ln_unit, between=None):
                k_rest(n, 0)
                k_rest(n, 1)
                if between is not None:
                    between()
                k_third_part(n, 0)
                k_rest(n, 2)
                k_third_part(n, 1)
                k_third_part(n, 2)
                if ln_unit is not None:
                    ctx_rstd(ln_unit)

            def window(n):
                ln_unit = n + 3 if n.s == 0 and (n + 3).exists() else None
                if (n + 2).exists():
                    k_parts(n + 2, ln_unit)

            pool.wait_ge(padded, 1)
            token_rstd(0)
            u0, u1 = Unit(0, None, 0), Unit(0, None, 1)
            pool.wait_ge(ld_mask, 16)
            spread_q(0)
            spread_q(1)
            for i in range(SA_STEPS):
                if i + 2 < B:
                    spread_q(i + 2)
                if i == 0:
                    ctx_rstd(u0)
                if i == 3:
                    ctx_rstd(u1)
                if i == 8:
                    ctx_rstd(u0 + 2)
                for kind, unit, third in SA_PIECES.get(i - 1, ()):
                    if kind == "k":
                        k_rest(u0, third)
                for kind, unit, third in SA_PIECES.get(i - 3, ()):
                    if kind == "k":
                        k_third_part(u0, third)
            token_rstd(1)
            k_parts(u1, None)
            run_windows(pool, 0, window)
            token_rstd(2)
            v0 = Unit(1, None, 0)
            k_parts(v0, None, gates_exp)
            token_rstd(3)
            k_parts(v0 + 1, None)
            run_windows(pool, 1, window)

        @block.scalar
        def _(act):
            def evac_sa_v():
                for i in range(2):
                    act.wait_ge(sa_vp_full, i + 1)
                    if i == 0:
                        act.wait_ge(v_ones, 1)
                    dst = vaug_sa[:, 4 * i:4 * i + 4, 0:H * VW].rearrange("k b (h c) -> k b h c", c=VW)[:, :, :, 0:DH]
                    nc.scalar.activation(dst, ST[0:L, 0, i].rearrange("k (b h c) -> k b h c", b=4, c=DH),
                                         ACT.Copy).then_inc(sa_v_evac, 1)

            def evac_xT(n, thirds=range(3)):
                for i in thirds:
                    act.wait_ge(xt_full, n.count(3, i + 1))
                    if i == 0 and (n.it is not None or n.c >= 2):
                        act.wait_ge(vp_full, (n + -2).count(3, 3))
                    nc.scalar.activation(xT[n.par][:, THIRD * i:THIRD * (i + 1)], MI[:, 0:THIRD], ACT.Identity,
                                         bias=ln_vec(LN_CAKV, 1), scale=ln_vec(LN_CAKV, 0)).then_inc(xt_evac, 1)

            def evac_k(n, i, bank=MI):
                act.wait_ge(kp_full, n.count(3, i + 1))
                if i == 0:
                    for half in range(2):
                        wait(act, kst_loaded[half][n.par], n.par_count(16 * TERMS, 0))
                wait(act, kr_done, n.count(3, i - 2))
                c = slice(THIRD * i, THIRD * (i + 1))
                nc.scalar.activation(kf[:, c], bank[:, 0:THIRD], ACT.Identity, bias=bias_k(n.s + 1)).then_inc(k_evac, 1)
                nc.scalar.activation(ksplit[n.par][:, 0, c], bank[:, 0:THIRD], ACT.Identity,
                                     bias=bias_k(n.s + 1)).then_inc(k_evac, 1)

            def evac_v(n, i):
                act.wait_ge(vp_full, n.count(3, i + 1))
                if i == 0:
                    if n.s == 0 and n.it is None and n.c < 2:
                        act.wait_ge(v_ones, 1)
                    else:
                        act.wait_ge(pv_done, (n + -2).count(STEPS, STEPS))
                dst = vaug[n.par][:, CPT * i:CPT * (i + 1), 0:H * VW].rearrange(
                    "k b (h c) -> k b h c", c=VW)[:, :, :, 0:DH]
                nc.scalar.activation(dst, MI[0:KC, :].rearrange("k (b h c) -> k b h c", b=CPT, c=DH),
                                     ACT.Copy).then_inc(v_evac, 1)

            def evac_mx(n, half):
                act.wait_ge(mx_full, n.count(2, half + 1))
                prev = n + -1
                if n.s or n.it is not None or n.c >= 1:
                    act.wait_ge(shift_loaded[half][prev.par], prev.par_count(16, 16))
                nc.scalar.activation(mrow[:, half, :], MX[half], ACT.Copy
                                     ).then_inc(mx_evac, 1)

            def exp_step(n, k):
                act.wait_ge(st_full, n.count(STEPS, k + 1))
                wait(act, pv_done, n.count(STEPS, k - 1))
                nc.scalar.activation(PT[:, k % 2], ST[:, k % 2, :, 0:4 * PC], ACT.Exp, scale=SCALE
                                     ).then_inc(exp_done, 1)

            def evac_po(n):
                act.wait_ge(pv_done, n.count(STEPS, STEPS))
                nc.scalar.activation(po[:], PO[:, 0:2 * PC], ACT.Copy).then_inc(po_evac, 1)

            def evac_on(n):
                act.wait_ge(ld_vec, 16)
                act.wait_ge(ont_full, n.count(1, 1))
                nc.scalar.activation(attnT[:, bass.ds(n.u * L, L)], OT, ACT.Identity,
                                     bias=bias_v(n.s + 1)).then_inc(ont_evac, 1)

            def window(n):
                own_mx, next_mx = n.mx_steps()
                for k in range(STEPS):
                    if k == own_mx:
                        evac_mx(n, 1)
                    if k == next_mx and (n + 1).exists():
                        evac_mx(n + 1, 0)
                    if k == FORTH_STEP and (n + -1).exists():
                        evac_on(n + -1)
                    exp_step(n, k)
                    if k == 0 and (n + -1).exists():
                        evac_po(n + -1)
                    if 0 <= k - K_STEP < 3 and (n + 2).exists():
                        evac_k(n + 2, k - K_STEP)
                    if 0 <= k - V_STEP < 3 and (n + 1).exists():
                        evac_v(n + 1, k - V_STEP)
                    if 0 <= k - CTX_STEP < 3 and n.s == 0 and (n + 3).exists():
                        evac_xT(n + 3, (k - CTX_STEP,))

            def start_pass(s):
                first = Unit(s, None, 0)
                for i in range(3):
                    evac_v(first, i)
                if s == 0:
                    evac_xT(first + 2, (0, 1))
                evac_mx(first, 0)
                if s == 0:
                    evac_xT(first + 2, (2,))

            def finish_pass(s):
                last = Unit(s, None, B - 1)
                evac_po(last)
                evac_on(last)

            act.wait_ge(ld_x, 32)
            nc.scalar.activation(identb[:], ident[:], ACT.Copy).then_inc(identb_ready, 1)
            act.wait_ge(ld_vec, 16)
            act.wait_ge(sa_kp_full, 1)
            nc.scalar.activation(k_sa[:], PO[:, 0:N], ACT.Identity, bias=bias_k(0)).then_inc(sa_k, 1)
            evac_sa_v()
            u0, u1 = Unit(0, None, 0), Unit(0, None, 1)

            def evac_piece(kind, unit, third):
                n = Unit(0, None, unit)
                if kind == "t":
                    evac_xT(n, (third,))
                else:
                    evac_k(n, third)

            for i in range(SA_STEPS):
                pieces = SA_PIECES.get(i, ())
                if pieces:
                    evac_piece(*pieces[0])
                if 0 <= i - 4 < B:
                    b = i - 4
                    act.wait_ge(sa_ont, b + 1)
                    nc.scalar.activation(attnT[:, L * b:L * (b + 1)], ST[:, (i - 1) % 2, 1, 4 * PC:4 * PC + L],
                                         ACT.Identity, bias=bias_v(0)).then_inc(sa_att, 1)
                if 0 <= i - 1 < B:
                    b = i - 1
                    act.wait_ge(sa_tp_full, b + 1)
                    wait(act, sa_pv, b - 1)
                    nc.scalar.activation(PT[0:L, b % 2], ST[0:L, b % 2, :, 0:4 * PC], ACT.Copy).then_inc(sa_pt, 1)
                if i < B:
                    act.wait_ge(sa_sub, i + 1)
                    nc.scalar.activation(p_sa[:, i % 2], p_sa[:, i % 2], ACT.Exp, scale=SCALE).then_inc(sa_exp, 1)
                if 0 <= i - 2 < B:
                    b = i - 2
                    act.wait_ge(sa_pv, b + 1)
                    wait(act, sa_pot, b)
                    nc.scalar.activation(po[:], PO[:, 0:2 * PC], ACT.Copy).then_inc(sa_po, 1)
                if len(pieces) > 1:
                    evac_piece(*pieces[1])
            for i in range(3):
                evac_k(u1, i, K_BANKS[i])
            start_pass(0)
            run_windows(act, 0, window)
            finish_pass(0)

            v0 = Unit(1, None, 0)
            for i in range(3):
                evac_k(v0, i, K_BANKS[i])

            def gelus(it):
                for i in range(2 * CPE):
                    act.wait_ge(ld_vec, 16)
                    act.wait_ge(fc1_full, it * (2 * CPE) + (i + 1))
                    if not isinstance(it, int) or i >= CPE:
                        act.wait_ge(fc2_step, it * (2 * CPE) + (i + 1 - CPE))
                    c = i % CPE
                    nc.scalar.activation(h1[:, c], ST[:, c // 2, c % 2, 0:N], ACT.Gelu,
                                         bias=vec[:, bass.ds(it * (2 * CPE) + (B1_AT + i), 1)]).then_inc(gelu_done, 1)
            gelus(0)
            with act.Fori(1, E // 2) as it:
                gelus(it)
            for i in range(3):
                evac_k(v0 + 1, i, K_BANKS[i])
            start_pass(1)
            run_windows(act, 1, window)
            finish_pass(1)

        @block.vector
        def _(dve):
            def token_ln(n):
                if n == 0:
                    dve.wait_ge(ld_x, 32)
                elif n == 3:
                    dve.wait_ge(expert_added, E)
                else:
                    dve.wait_ge(x_added, n)
                for t in range(TT):
                    last = nc.vector.bn_stats(xstat[:, t], xt[:, t])
                last.then_inc(xstat_ready, 1)
                dve.wait_ge(xstat_ready, n + 1)
                for t in range(TT):
                    last = nc.vector.bn_aggr(xmv[:, t], xstat[:, t])
                last.then_inc(xmv_ready, 1)
                dve.wait_ge(xmv_ready, n + 1)
                nc.vector.tensor_scalar(xvar[:], xmv[:, :, 1], EPS, None, ALU.add).then_inc(xvar_ready, 1)
                dve.wait_ge(xrstd_ready, n + 1)
                for t in range(TT):
                    last = nc.vector.tensor_scalar(xn[:, t], xt[:, t], xmv[:, t, 0:1], xrstd[:, t:t + 1],
                                                   ALU.subtract, ALU.mult)
                last.then_inc(xn_ready, 1)

            def token_gain(n):
                dve.wait_ge(lnt_full, n + 1)
                if n == 0:
                    dve.wait_ge(ld_vec, 16)
                nc.vector.tensor_scalar(hT[:], SM[:, 0, 0:N], ln_vec(X_LN[n], 0), ln_vec(X_LN[n], 1),
                                        ALU.mult, ALU.add).then_inc(hT_ready, 1)

            def split_q(n):
                dve.wait_ge(qp_full, n + 1)
                if n:
                    dve.wait_ge(qall_loaded, 16 * TERMS * n)
                nc.vector.tensor_scalar(qf[:], SM[:, 0, 0:N], bias_q(n + 1), None, ALU.add).then_inc(qf_ready, 1)
                dve.wait_ge(qf_ready, n + 1)
                nc.vector.tensor_copy(qsplit[:, 0], qf[:]).then_inc(q1_ready, 1)
                dve.wait_ge(q1_ready, n + 1)
                nc.vector.tensor_tensor(qr[:], qf[:], qsplit[:, 0], ALU.subtract).then_inc(qr_ready, 1)
                dve.wait_ge(qr_ready, n + 1)
                nc.vector.tensor_copy(qsplit[:, 1], qr[:]).then_inc(q2_ready, 1)
                dve.wait_ge(q2_ready, n + 1)
                nc.vector.tensor_tensor(qsplit[:, 2], qr[:], qsplit[:, 1], ALU.subtract).then_inc(q3_ready, 1)

            def ctx_stats(n, chunks):
                if chunks[0] == 0:
                    dve.wait_ge(ld_ctx[n.par], n.par_count(16, 16))
                for c in chunks:
                    last = nc.vector.bn_stats(cstat[:, c], cx[n.par][:, c])
                if chunks[-1] == NCH - 1:
                    last.then_inc(cstat_ready, 1)

            def ctx_aggregate(n):
                for c in range(NCH):
                    last = nc.vector.bn_aggr(cmv[:, c], cstat[:, c])
                last.then_inc(cmv_ready, 1)
                dve.wait_ge(cmv_ready, n.count(1, 1))
                nc.vector.tensor_scalar(cvar[:], cmv[:, :, 1], EPS, None, ALU.add).then_inc(cvar_ready, 1)

            def ctx_normalise(n, thirds=range(3)):
                dve.wait_ge(crstd_ready, n.count(1, 1))
                for i in thirds:
                    for c in range(CPT * i, CPT * (i + 1)):
                        last = nc.vector.tensor_scalar(cx[n.par][:, c], cx[n.par][:, c], cmv[:, c, 0:1],
                                                       crstd[:, c:c + 1], ALU.subtract, ALU.mult)
                    last.then_inc(cn_ready, 1)

            def k_second_part(n, i):
                dve.wait_ge(kr_done, n.count(3, i + 1))
                c = slice(THIRD * i, THIRD * (i + 1))
                nc.vector.tensor_copy(ksplit[n.par][:, 1, c], kr[:, c]).then_inc(k2_done, 1)

            def reduce_tile(n, j, banks=2):
                dve.wait_ge(sm_full, n.count(TILES, j + 1))
                nc.vector.tensor_reduce(mxp[:, j // 3, j % 3:j % 3 + 1], tile_bank(j, banks), AX.X,
                                        ALU.max).then_inc(sm_red, 1)

            def max_parts(n, half):
                dve.wait_ge(sm_red, n.count(TILES, TILES // 2 * (half + 1)))
                nc.vector.tensor_reduce(nmx[:], mxp[:, 4 * half:4 * half + 4], AX.X, ALU.max, negate=True
                                        ).then_inc(nmx_ready, 1)
                wait(dve, mx_full, n.count(2, half))
                dve.wait_ge(nmx_ready, n.count(2, half + 1))
                nc.vector.tensor_copy(mparts[:, 0], nmx[:]).then_inc(m1_ready, 1)
                dve.wait_ge(m1_ready, n.count(2, half + 1))
                nc.vector.tensor_tensor(mparts[:, 1], nmx[:], mparts[:, 0], ALU.subtract).then_inc(mparts_ready, 1)

            def place_q(n, half):
                if n.it is None and n.c == 0 and half == 0:
                    dve.wait_ge(qall_loaded, 16 * TERMS * (n.s + 1))
                if n.s or n.it is not None or n.c >= 2:
                    dve.wait_ge(st_full, (n + -2).count(STEPS, HSTEP * (half + 1)))
                pairs = slice(4 * half, 4 * half + 4)
                for hh in range(2):
                    last = nc.vector.tensor_scalar(
                        qst[n.par][0:SROWS, pairs, L * hh:L * (hh + 1)], qall[:, pairs, bass.ds(n.u * L, L)],
                        mask[0:SROWS, H + hh:H + hh + 1], None, ALU.mult)
                last.then_inc(qst_ready, 1)

            def normalise(bank, full, rden_sem, done, full_at, rden_at, par):
                dve.wait_ge(full, full_at)
                heads = bank[0:L].rearrange("q (h x) -> q h x", x=32)
                nc.vector.reciprocal(rden[:], heads[:, :, DH]).then_inc(rden_sem, 1)
                dve.wait_ge(rden_sem, rden_at)
                nc.vector.tensor_tensor(on[:, par], heads[:, :, 0:DH],
                                        rden[:].unsqueeze(2).broadcast_to([L, H, DH]), ALU.mult).then_inc(done, 1)

            def normalise_unit(n):
                normalise(MI, pot_full, rden_ready, norm_done, n.count(1, 1), n.count(1, 1), n.par)

            def add_projection(n):
                dve.wait_ge(op_full, n + 1)
                nc.vector.tensor_tensor(xt[:], xt[:], PO[0:TP, :].rearrange("p (t d) -> p t d", t=TT), ALU.add
                                        ).then_inc(x_added, 1)

            def window(n):
                nxt, k_unit = n + 1, n + 2
                ln_unit = n + 3 if n.s == 0 and (n + 3).exists() else None
                if not nxt.exists():
                    max_parts(n, 1)
                for k in range(STEPS):
                    tiles = n.tiles(k)
                    if tiles:
                        if k == 5 and ln_unit is not None:
                            dve.wait_ge(cstat_ready, ln_unit.count(1, 1))
                        reduce_tile(n + tiles[0][0], tiles[0][1])
                        if k == 0 and not n.first():
                            max_parts(n, 1)
                    if k == BACK_STEP and (n + -1).exists():
                        normalise_unit(n + -1)
                    if nxt.exists():
                        if k == Q2_STEP:
                            place_q(nxt, 1)
                        if k == Q1_STEP and k_unit.exists():
                            place_q(k_unit, 0)
                        for ahead, j in tiles[1:]:
                            reduce_tile(n + ahead, j)
                            if not ahead and j == TILES - 1:
                                max_parts(n, 1)
                        if (1, TILES // 2 - 1) in tiles:
                            max_parts(nxt, 0)
                    if 0 <= k - K_STEP - 1 < 3 and k_unit.exists():
                        k_second_part(k_unit, k - K_STEP - 1)
                    if ln_unit is not None:
                        if k in (1, 2, 3, 4):
                            ctx_stats(ln_unit, range(3 * (k - 1), 3 * k))
                        if k == 5:
                            ctx_aggregate(ln_unit)
                        if k in (7, 8, 9):
                            ctx_normalise(ln_unit, (k - 7,))

            every = range(NCH)
            u0, u1 = Unit(0, None, 0), Unit(0, None, 1)
            for buf in (vaug_sa, vaug[0], vaug[1]):
                last = nc.vector.memset(buf[:], 1.0)
            last.then_inc(v_ones, 1)
            token_ln(0)
            ctx_stats(u0, range(6))
            token_gain(0)
            ctx_stats(u0, range(6, NCH))
            dve.wait_ge(ld_mask, 16)
            dve.wait_ge(sa_qp_full, 1)
            nc.vector.tensor_scalar(q_sa[:], MI[:, 0:N], bias_q(0), None, ALU.add).then_inc(sa_q, 1)
            dve.wait_ge(cstat_ready, u0.count(1, 1))
            ctx_aggregate(u0)
            nc.vector.tensor_reduce(wabs[:], watt[:, 2], AX.X, ALU.add, apply_absolute_value=True
                                    ).then_inc(wabs_ready, 1)
            for i in range(SA_STEPS):
                if i < B:
                    dve.wait_ge(sa_sm_full, i + 1)
                    wait(dve, sa_sub, i)
                    scores = SM[0:PC, 0, 0:N].rearrange("q (p k) -> q p k", p=PAIRS)
                    nc.vector.tensor_reduce(nmx_sa[:], scores, AX.X, ALU.max, negate=True).then_inc(sa_max, 1)
                    dve.wait_ge(sa_max, i + 1)
                    wait(dve, sa_tp_full, i - 1)
                    nc.vector.tensor_tensor(p_sa[:, i % 2], scores,
                                            nmx_sa[:].unsqueeze(2).broadcast_to([PC, PAIRS, L]), ALU.add
                                            ).then_inc(sa_sub, 1)
                if 0 <= i - 3 < B:
                    normalise(SM[:, 1], sa_pot, sa_rden, sa_norm, i - 2, i - 2, (i - 3) % 2)
                for kind, unit, third in SA_PIECES.get(i - 2, ()):
                    if kind == "k":
                        k_second_part(u0, third)
                if i == 0:
                    dve.wait_ge(gam_full, 1)
                    nc.vector.tensor_copy(gam[:], MI[:, 0:4]).then_inc(gam_ready, 1)
                    ctx_normalise(u0, (0, 1))
                if i == 1:
                    ctx_normalise(u0, (2,))
                    ctx_stats(u1, every)
                if i == 2:
                    dve.wait_ge(cstat_ready, u1.count(1, 1))
                    ctx_aggregate(u1)
                if i == 4:
                    ctx_normalise(u1, (0,))
                if i == 5:
                    ctx_normalise(u1, (1, 2))
                if i == 6:
                    ctx_stats(u0 + 2, every)
                if i == 7:
                    dve.wait_ge(cstat_ready, (u0 + 2).count(1, 1))
                    ctx_aggregate(u0 + 2)
                if i in (9, 10, 11):
                    ctx_normalise(u0 + 2, (i - 9,))
            add_projection(0)
            token_ln(1)
            token_gain(1)
            split_q(0)

            dve.wait_ge(gam_ready, 1)
            nc.vector.tensor_scalar(thr[:, 0], gam[:], EPS, 0.5, ALU.add, ALU.mult)
            nc.vector.tensor_scalar(thr[:, 1], gam[:], EPS, -0.5, ALU.add, ALU.mult).then_inc(thr_ready, 1)
            dve.wait_ge(thr_ready, 1)
            for w in range(4):
                nc.vector.tensor_scalar(wt[:, 0, w], watt[:, 2, w], thr[:, 0, w:w + 1], None, ALU.is_gt)
                last = nc.vector.tensor_scalar(wt[:, 1, w], watt[:, 2, w], thr[:, 1, w:w + 1], None, ALU.is_lt)
            last.then_inc(tern1, 1)
            dve.wait_ge(tern1, 1)
            nc.vector.tensor_tensor(wt[:, 0], wt[:, 0], wt[:, 1], ALU.subtract).then_inc(tern2, 1)
            dve.wait_ge(tern2, 1)
            for w in range(4):
                last = nc.vector.scalar_tensor_tensor(out=wt[:, 1, w], in0=wt[:, 0, w], scalar=gam[:, w:w + 1],
                                                      in1=watt[:, 2, w], op0=ALU.mult, op1=ALU.subtract)
            last.then_inc(tern3, 1)
            dve.wait_ge(tern3, 1)
            nc.vector.tensor_tensor(watt[:, 2], watt[:, 2], wt[:, 1], ALU.add).then_inc(wq_ready, 1)

            def start_pass(s):
                first = Unit(s, None, 0)
                place_q(first, 0)
                for j in range(START_TILES):
                    reduce_tile(first, j, banks=4)
                    if j == 3:
                        place_q(first, 1)
                    if j == START_TILES - 2:
                        place_q(first + 1, 0)
                    if j in (1, 4, 7):
                        k_second_part(first + 1, j // 3)
                    if j == TILES // 2 - 1:
                        max_parts(first, 0)

            def finish_pass(s):
                normalise_unit(Unit(s, None, B - 1))
                add_projection(s + 1)

            start_pass(0)
            run_windows(dve, 0, window)
            finish_pass(0)

            v0 = Unit(1, None, 0)
            token_ln(2)
            token_gain(2)
            k_second_part(v0, 0)
            dve.wait_ge(ld_rows, 48)
            dve.wait_ge(rt_full, 1)
            rb = rows[:, RB0:RB0 + E].unsqueeze(1).broadcast_to([TP, TT, E])
            nc.vector.tensor_tensor(lg[:], SM[0:TP, 1, 0:TT * E].rearrange("p (t e) -> p t e", t=TT), rb, ALU.add
                                    ).then_inc(lg_ready, 1)
            dve.wait_ge(lg_ready, 1)
            mine = lg[:].unsqueeze(3).broadcast_to([TP, TT, E, E])
            other = lg[:].unsqueeze(2).broadcast_to([TP, TT, E, E])
            tri = rows[:, TRI0:TRI0 + E * E].unsqueeze(1).broadcast_to([TP, TT, E * E])
            nc.vector.tensor_tensor(cmp[:, 0], other, mine, ALU.is_gt)
            nc.vector.tensor_tensor(cmp[:, 1], other, mine, ALU.is_equal)
            nc.vector.tensor_reduce(top[:, 0], lg[:], AX.X, ALU.max).then_inc(cmp_ready, 1)
            dve.wait_ge(cmp_ready, 1)
            eq = cmp[:, 1].rearrange("p t e f -> p t (e f)")
            nc.vector.tensor_tensor(eq, eq, tri, ALU.mult).then_inc(cmp_ready, 1)
            dve.wait_ge(cmp_ready, 2)
            both = cmp[:, 0].rearrange("p t e f -> p t (e f)")
            nc.vector.tensor_tensor(both, both, eq, ALU.add).then_inc(cmp_ready, 1)
            dve.wait_ge(cmp_ready, 3)
            nc.vector.tensor_reduce(rank[:], cmp[:, 0], AX.X, ALU.add)
            nc.vector.tensor_tensor(lg[:], lg[:], top[:, 0].unsqueeze(2).broadcast_to([TP, TT, E]), ALU.subtract
                                    ).then_inc(gexp_in, 1)
            dve.wait_ge(gexp_in, 1)
            nc.vector.tensor_scalar(rank[:], rank[:], 1.5, None, ALU.is_lt).then_inc(rank_ready, 1)
            dve.wait_ge(gexp_done, 1)
            dve.wait_ge(rank_ready, 1)
            nc.vector.tensor_tensor(gates[:], gates[:], rank[:], ALU.mult).then_inc(gate_step, 1)
            dve.wait_ge(gate_step, 1)
            nc.vector.tensor_reduce(top[:, 1], gates[:], AX.X, ALU.add).then_inc(gate_step, 1)
            dve.wait_ge(gate_step, 2)
            nc.vector.reciprocal(top[:, 2], top[:, 1]).then_inc(gate_step, 1)
            dve.wait_ge(gate_step, 3)
            nc.vector.tensor_tensor(gates[:], gates[:], top[:, 2].unsqueeze(2).broadcast_to([TP, TT, E]), ALU.mult
                                    ).then_inc(gates_ready, 1)
            k_second_part(v0, 1)
            k_second_part(v0, 2)

            def add_experts(it):
                for j in range(2):
                    dve.wait_ge(fc2_step, it * (2 * CPE) + (j + 1) * CPE)
                    wait(dve, expert_added, it * 2 + j)
                    for t in range(TT):
                        last = nc.vector.scalar_tensor_tensor(
                            out=xt[:, t], in0=SM[0:TP, j, D * t:D * (t + 1)], scalar=gates[:, t, bass.ds(it * 2 + j, 1)],
                            in1=xt[:, t], op0=ALU.mult, op1=ALU.add)
                    last.then_inc(expert_added, 1)
            dve.wait_ge(gates_ready, 1)
            dve.wait_ge(gt_full, 1)
            nc.vector.tensor_copy(gT[:], MI[0:E, 0:N]).then_inc(gT_ready, 1)
            add_experts(0)
            dve.wait_ge(b2_full, 1)
            dve.wait_ge(expert_added, 2)
            nc.vector.tensor_tensor(xt[:], xt[:], MI[0:TP, :].rearrange("p (t d) -> p t d", t=TT), ALU.add
                                    ).then_inc(b2_added, 1)
            dve.wait_ge(b2_added, 1)
            with dve.Fori(1, E // 2) as it:
                add_experts(it)
            token_ln(3)
            token_gain(3)
            split_q(1)
            start_pass(1)
            run_windows(dve, 1, window)
            finish_pass(1)

        @block.tensor
        def _(pe):
            mm = nc.tensor.matmul

            def misc_free(prev):
                if prev is not None:
                    pe.wait_ge(*prev)

            def transpose_tokens(n):
                pe.wait_ge(xn_ready, n + 1)
                for t in range(TT):
                    last = nc.tensor.transpose(SM[:, 0, TP * t:TP * (t + 1)], xn[:, t], ident[0:TP, 0:TP])
                last.then_inc(lnt_full, 1)

            def project_q(n, ln):
                pe.wait_ge(hT_ready, ln + 1)
                mm(SM[:, 0, 0:N], watt[:, n + 1, 0], hT[:], start=True, stop=True).then_inc(qp_full, 1)

            def project_out(n, done):
                pe.wait_ge(*done)
                for t in range(TT):
                    tile = PO[0:TP, D * t:D * (t + 1)]
                    mm(tile, attnT[:, TP * t:TP * (t + 1)], watt[:, n, 3], start=True, stop=False)
                    last = mm(tile, ones_row[:], rows[0:1, D * n:D * (n + 1)], start=False, stop=True)
                last.then_inc(op_full, 1)

            def transpose_ctx(n, i, prev):
                misc_free(prev)
                pe.wait_ge(cn_ready, n.count(3, i + 1))
                for c in range(CPT):
                    last = nc.tensor.transpose(MI[:, KC * c:KC * (c + 1)], cx[n.par][:, CPT * i + c],
                                               ident[0:KC, 0:KC])
                last.then_inc(xt_full, 1)
                return xt_evac, n.count(3, i + 1)

            def project_k(n, i, prev, bank=MI):
                misc_free(prev)
                if n.s == 0:
                    pe.wait_ge(xt_evac, n.count(3, i + 1))
                else:
                    pe.wait_ge(ld_xT[n.par], n.pass_par_count(16, 16))
                mm(bank[:, 0:THIRD], watt[:, n.s + 1, 1], xT[n.par][:, THIRD * i:THIRD * (i + 1)],
                   start=True, stop=True).then_inc(kp_full, 1)
                return k_evac, n.count(6, 2 * i + 2)

            def project_v(n, i, prev):
                misc_free(prev)
                if i == 0 and n.s == 0:
                    pe.wait_ge(xt_evac, n.count(3, 3))
                for c in range(CPT):
                    at = KC * (CPT * i + c)
                    last = mm(MI[0:KC, D * c:D * (c + 1)], xT[n.par][:, at:at + KC], watt[:, n.s + 1, 2],
                              start=True, stop=True)
                last.then_inc(vp_full, 1)
                return v_evac, n.count(3, i + 1)

            def project_k_apart(n, prev):
                for i in range(3):
                    last = project_k(n, i, prev, K_BANKS[i])
                return last

            def transpose_max(n, half):
                if n.first() and n.s == 0 and half == 0:
                    pe.wait_ge(identb_ready, 1)
                pe.wait_ge(mparts_ready, n.count(2, half + 1))
                nc.tensor.transpose(MX[half], mparts[:].rearrange("q m p -> q (m p)"),
                                    identb[0:PC, 0:PC]).then_inc(mx_full, 1)

            def transpose_po(bank):
                for half in range(2):
                    for hh in range(2):
                        at = 256 * half + (128 - VW) * hh
                        last = mm(bank[0:L, at:at + 128], po[:, PC * half + L * hh:PC * half + L * (hh + 1)],
                                  ident[:], start=True, stop=True, skip_group_check=True)
                return last

            def output_back(n, prev):
                misc_free(prev)
                pe.wait_ge(po_evac, n.count(1, 1))
                transpose_po(MI).then_inc(pot_full, 1)
                return norm_done, n.count(1, 1)

            def output_forth(n):
                pe.wait_ge(norm_done, n.count(1, 1))
                mm(OT, on[:, n.par].rearrange("q h d -> q (h d)"), ident[0:L, 0:L], start=True, stop=True
                   ).then_inc(ont_full, 1)

            def scores(n, k):
                half = k // HSTEP
                if k % HSTEP == 0:
                    pe.wait_ge(shift_loaded[half][n.par], n.par_count(16, 16))
                wait(pe, exp_done, n.count(STEPS, k - 1))
                for cc in range(2):
                    at = KC * (2 * (k % HSTEP) + cc)
                    for p in range(4):
                        last = mm(ST[:, k % 2, cc, PC * p:PC * (p + 1)], kst[n.par][:, 4 * half + p, at:at + 128],
                                  qst[n.par][:, 4 * half + p], start=True, stop=True)
                last.then_inc(st_full, 1)
                own_mx, next_mx = n.mx_steps()
                if k == own_mx:
                    transpose_max(n, 1)
                if k == next_mx and (n + 1).exists():
                    transpose_max(n + 1, 0)
                if k == FORTH_STEP and (n + -1).exists():
                    output_forth(n + -1)

            def max_tile(n, j, banks=2):
                if j == 0:
                    pe.wait_ge(qst_ready, n.count(2, 1))
                    pe.wait_ge(kst_loaded[0][n.par], n.par_count(16 * TERMS, 16 * TERMS))
                if j == TILES // 2:
                    pe.wait_ge(qst_ready, n.count(2, 2))
                    pe.wait_ge(kst_loaded[1][n.par], n.par_count(16 * TERMS, 16 * TERMS))
                wait(pe, sm_red, n.count(TILES, j + 1 - banks))
                at = THIRD * (j % 3)
                mm(tile_bank(j, banks), qst[n.par][0:SROWS, j // 3], kst[n.par][0:SROWS, j // 3, at:at + THIRD],
                   start=True, stop=True).then_inc(sm_full, 1)

            def values(n, k):
                half = k // HSTEP
                pe.wait_ge(exp_done, n.count(STEPS, k + 1))
                if k == 0:
                    wait(pe, po_evac, n.count(1, 0))
                if k < HSTEP:
                    pe.wait_ge(v_evac, n.count(3, (2 * k + 1) // CPT + 1))
                for cc in range(2):
                    c = 2 * (k % HSTEP) + cc
                    for p in range(4):
                        at = 2 * VW * (4 * half + p)
                        last = mm(PO[32 * p:32 * p + 32, PC * half:PC * (half + 1)], vaug[n.par][:, c, at:at + 32],
                                  PT[0:KC, k % 2, cc, PC * p:PC * (p + 1)], start=(k == 0 and cc == 0),
                                  stop=(k % HSTEP == HSTEP - 1 and cc == 1), skip_group_check=True)
                last.then_inc(pv_done, 1)

            def window(n):
                nxt, k_unit, prv = n + 1, n + 2, n + -1
                ln_unit = n + 3 if n.s == 0 and (n + 3).exists() else None
                if n.s == 0 and k_unit.exists():
                    prev = (xt_evac, k_unit.count(3, 3))
                else:
                    prev = (v_evac, n.count(3, 3))
                for k in range(STEPS):
                    scores(n, k)
                    tiles = [(n + ahead, j) for ahead, j in n.tiles(k)]
                    if tiles:
                        max_tile(*tiles[0])
                    if k:
                        values(n, k - 1)
                    elif prv.exists():
                        values(prv, STEPS - 1)
                    for tile in tiles[1:-1]:
                        max_tile(*tile)
                    if 0 <= k - K_STEP < 3 and k_unit.exists():
                        prev = project_k(k_unit, k - K_STEP, prev)
                    if k == BACK_STEP and prv.exists():
                        prev = output_back(prv, prev)
                    if 0 <= k - V_STEP < 3 and nxt.exists():
                        prev = project_v(nxt, k - V_STEP, prev)
                    if 0 <= k - CTX_STEP < 3 and ln_unit is not None:
                        prev = transpose_ctx(ln_unit, k - CTX_STEP, prev)
                    if len(tiles) > 1:
                        max_tile(*tiles[-1])
                return prev

            u0, u1 = Unit(0, None, 0), Unit(0, None, 1)
            pe.wait_ge(ld_x, 32)
            transpose_tokens(0)
            pe.wait_ge(ld_w, 16)
            pe.wait_ge(hT_ready, 1)
            mm(MI[:, 0:N], watt[:, 0, 0], hT[:], start=True, stop=True).then_inc(sa_qp_full, 1)
            mm(PO[:, 0:N], watt[:, 0, 1], hT[:], start=True, stop=True).then_inc(sa_kp_full, 1)
            for i in range(2):
                for c in range(4):
                    b = 4 * i + c
                    last = mm(ST[0:L, 0, i, D * c:D * (c + 1)], hT[:, L * b:L * (b + 1)], watt[:, 0, 2],
                              start=True, stop=True)
                last.then_inc(sa_vp_full, 1)
            pe.wait_ge(sa_q, 1)
            pe.wait_ge(wabs_ready, 1)
            pe.wait_ge(padded, 1)
            mm(MI[:, 0:4], mean_w[:], wabs[:], start=True, stop=True).then_inc(gam_full, 1)
            prev = (gam_ready, 1)

            def piece(kind, unit, third, prev):
                n = Unit(0, None, unit)
                if kind == "t":
                    return transpose_ctx(n, third, prev)
                return project_k(n, third, prev)

            for i in range(SA_STEPS):
                pieces = SA_PIECES.get(i, ())
                if i < B:
                    pe.wait_ge(sa_qbd, i + 1)
                    if i == 0:
                        pe.wait_ge(sa_k, 1)
                    wait(pe, sa_sub, i)
                    for p in range(PAIRS):
                        last = mm(SM[0:PC, 0, L * p:L * (p + 1)],
                                  qbd[:, i % 2, 2 * p:2 * p + 2].rearrange("n h q -> n (h q)"),
                                  k_sa[:, L * i:L * (i + 1)], start=True, stop=True)
                    last.then_inc(sa_sm_full, 1)
                if pieces:
                    prev = piece(*pieces[0], prev)
                if 0 <= i - 1 < B:
                    b = i - 1
                    pe.wait_ge(sa_exp, b + 1)
                    if b == 0:
                        pe.wait_ge(sa_v_evac, 2)
                    wait(pe, sa_pt, b - 1)
                    for p in range(PAIRS):
                        last = nc.tensor.transpose(ST[0:L, b % 2, p // 4, PC * (p % 4):PC * (p % 4 + 1)],
                                                   p_sa[:, b % 2, p], ident[0:PC, 0:PC])
                    last.then_inc(sa_tp_full, 1)
                if 0 <= i - 4 < B:
                    b = i - 4
                    pe.wait_ge(sa_norm, b + 1)
                    if i - 1 >= B:
                        pe.wait_ge(sa_pt, min(i - 2, B))
                        pe.wait_ge(sa_att, b - 1)
                    nc.tensor.transpose(ST[:, (i - 1) % 2, 1, 4 * PC:4 * PC + L],
                                        on[:, b % 2].rearrange("q h d -> q (h d)"), ident[0:L, 0:L]
                                        ).then_inc(sa_ont, 1)
                if 0 <= i - 2 < B:
                    b = i - 2
                    pe.wait_ge(sa_pt, b + 1)
                    if b == 0:
                        pe.wait_ge(sa_k, 1)
                    wait(pe, sa_po, b)
                    for p in range(PAIRS):
                        half, q = p // 4, p % 4
                        last = mm(PO[32 * q:32 * q + 32, PC * half:PC * (half + 1)],
                                  vaug_sa[:, b, 2 * VW * p:2 * VW * p + 32],
                                  PT[0:L, b % 2, half, PC * q:PC * (q + 1)], start=(half == 0), stop=True,
                                  skip_group_check=True)
                    last.then_inc(sa_pv, 1)
                if len(pieces) > 1:
                    prev = piece(*pieces[1], prev)
                if 0 <= i - 3 < B:
                    b = i - 3
                    pe.wait_ge(sa_po, b + 1)
                    wait(pe, sa_norm, b)
                    transpose_po(SM[:, 1]).then_inc(sa_pot, 1)
            pe.wait_ge(ld_rows, 48)
            project_out(0, (sa_att, B))
            prev = project_k_apart(u1, prev)
            transpose_tokens(1)
            pe.wait_ge(padded, 1)
            pe.wait_ge(ld_ones, 32)
            project_q(0, 1)

            def start_pass(s, prev):
                first = Unit(s, None, 0)
                for j in range(START_TILES):
                    max_tile(first, j, banks=4)
                    if j in (1, 4, 7):
                        prev = project_v(first, j // 3, prev)
                    if s == 0 and j in (10, 13, 16):
                        prev = transpose_ctx(first + 2, (10, 13, 16).index(j), prev)
                    if j == TILES // 2 + 3:
                        transpose_max(first, 0)

            def finish_pass(s):
                last = Unit(s, None, B - 1)
                k_unit = Unit(1, None, 0) if s == 0 else None
                values(last, STEPS - 1)
                if k_unit:
                    pe.wait_ge(wq_ready, 1)
                    project_k(k_unit, 0, None, K_BANKS[0])
                prev = output_back(last, (v_evac, last.count(3, 3)))
                if k_unit:
                    project_k(k_unit, 1, None, K_BANKS[1])
                output_forth(last)
                if k_unit:
                    prev = project_k(k_unit, 2, prev, K_BANKS[2])
                return prev

            start_pass(0, prev)
            run_windows(pe, 0, window)
            prev = finish_pass(0)
            project_out(1, (ont_evac, B))

            v0 = Unit(1, None, 0)
            transpose_tokens(2)
            pe.wait_ge(hT_ready, 3)
            for t in range(TT):
                last = mm(SM[0:TP, 1, E * t:E * (t + 1)], hT[:, TP * t:TP * (t + 1)], rwT[:], start=True, stop=True)
            last.then_inc(rt_full, 1)

            def transpose_gates():
                pe.wait_ge(gates_ready, 1)
                for t in range(TT):
                    last = nc.tensor.transpose(MI[0:E, TP * t:TP * (t + 1)], gates[:, t], ident[0:TP, 0:TP])
                last.then_inc(gt_full, 1)

            def experts(it):
                def fc1(i):
                    j, c = i // CPE, i % CPE
                    if c == 0:
                        pe.wait_ge(ld_exp[j], it * 32 + 32)
                    if not isinstance(it, int) or i >= CPE:
                        pe.wait_ge(gelu_done, it * (2 * CPE) + (i + 1 - CPE))
                    mm(ST[:, c // 2, c % 2, 0:N], w1s[j][:, D * c:D * (c + 1)], hT[:], start=True, stop=True
                       ).then_inc(fc1_full, 1)

                def fc2(i):
                    j, c = i // CPE, i % CPE
                    pe.wait_ge(gelu_done, it * (2 * CPE) + (i + 1))
                    if i == 0 and isinstance(it, int):
                        pe.wait_ge(lg_ready, 1)
                    if c == 0 and not isinstance(it, int):
                        pe.wait_ge(expert_added, it * 2 + (j - 1))
                    for t in range(TT):
                        last = mm(SM[0:TP, j, D * t:D * (t + 1)], h1[:, c, TP * t:TP * (t + 1)], w2s[j][:, c],
                                  start=(c == 0 and t == 0), stop=(c == CPE - 1), skip_group_check=True)
                    last.then_inc(fc2_step, 1)
                for i in range(FC1_AHEAD):
                    fc1(i)
                for i in range(2 * CPE):
                    if i + FC1_AHEAD < 2 * CPE:
                        fc1(i + FC1_AHEAD)
                    fc2(i)
                    if isinstance(it, int) and i == CPE - 1:
                        transpose_gates()
            misc_free(prev)
            experts(0)
            pe.wait_ge(gT_ready, 1)
            for t in range(TT):
                last = mm(MI[0:TP, D * t:D * (t + 1)], gT[:, TP * t:TP * (t + 1)], b2[:], start=True, stop=True)
            last.then_inc(b2_full, 1)
            with pe.Fori(1, E // 2) as it:
                experts(it)
            prev = (b2_added, 1)
            prev = project_k_apart(v0 + 1, prev)
            transpose_tokens(3)
            project_q(1, 3)
            start_pass(1, prev)
            run_windows(pe, 1, window)
            prev = finish_pass(1)
            project_out(2, (ont_evac, 2 * B))


def _orders():
    n = np.arange(D)
    q_order = (n % PAIRS) * PR + n // PAIRS
    k_order = ((n // 64) * 4 + n % 4) * PR + n % 64 // 4
    half, member, pair, dim = n // 64, n // 32 % 2, n // 8 % 4, n % 8
    o_order = (8 * half + 2 * pair + member) * DH + dim
    return q_order, k_order, o_order


def kernel(**inputs):
    import concourse.bacc as _bacc
    from concourse.bass_utils import run_bass_kernel_spmd as _run

    a = {k: np.asarray(v) for k, v in inputs.items()}
    q_order, k_order, o_order = _orders()
    n = np.arange(D)

    def attention(wq, wk, wv, wo, k_order):
        return np.stack([wq.T[:, q_order], wk.T[:, k_order], wv.T, wo.T[o_order]])

    weights, columns = [], []
    for p, order in (("L0_xattn_sa_", q_order), ("L0_xattn_ca_", k_order)):
        w, b = a[p + "in_w"], a[p + "in_b"]
        weights.append(attention(w[:D], w[D:2 * D], w[2 * D:], a[p + "out_w"], order))
        columns += [b[:D][q_order], b[D:2 * D][order], b[2 * D:][o_order]]
    p = "L1_xattn_"
    weights.append(attention(a[p + "Wq"], a[p + "Wk"], a[p + "Wv"], a[p + "Wo"], k_order))
    columns += [a[p + "bq"][q_order], a[p + "bk"][k_order], a[p + "bv"][o_order]]
    for ln in ("L0_xattn_sa_ln_", "L0_xattn_ca_q_ln_", "L0_xattn_ca_kv_ln_", "L0_xattn_moe_ln_"):
        columns += [a[ln + "g"], a[ln + "b"]]
    columns += [a["L1_xattn_ln_gamma"], a["L1_xattn_ln_beta"]]
    columns += list(a["L0_xattn_e_fc1_b"].reshape(E * CPE, D))
    before = np.tril(np.ones((E, E), np.float32), -1)
    arrays = {
        "x": a["x"].reshape(N, D),
        "ctx": a["ctx_1024"],
        "ctxT": a["ctx_1024"].transpose(0, 2, 1),
        "watt": np.stack(weights),
        "vec": np.stack(columns, axis=1),
        "rows": np.concatenate([a["L0_xattn_sa_out_b"], a["L0_xattn_ca_out_b"], a["L1_xattn_bo"],
                                a["L0_xattn_router_b"], before.reshape(-1)]),
        "rwT": a["L0_xattn_router_w"].T,
        "w1T": a["L0_xattn_e_fc1_w"].transpose(0, 2, 1),
        "w2T": a["L0_xattn_e_fc2_w"].transpose(0, 2, 1).reshape(E, CPE, D, D).transpose(0, 2, 1, 3),
        "b2": a["L0_xattn_e_fc2_b"],
        "ident": np.eye(D, dtype=np.float32),
        "mask": np.concatenate([q_order[:, None] // DH == np.arange(H),
                                n[:, None] % PR // DH == np.arange(2)], axis=1).astype(np.float32),
    }
    nc = _bacc.Bacc("TRN2", target_bir_lowering=False, num_devices=1)
    feeds, args = {}, []
    for name, array in arrays.items():
        feeds[f"in_{name}"] = np.ascontiguousarray(array)
        args.append(nc.dram_tensor(f"in_{name}", array.shape, F32, kind="ExternalInput").ap())
    args.append(nc.dram_tensor("out_x", (N, D), F32, kind="ExternalOutput").ap())
    build_kernel(nc, *args)
    result = _run(nc, [feeds], core_ids=[0])
    return result.results[0]["out_x"].reshape(B, L, D)
```
